# Optimizing a Trainium2 kernel written in Bass

```python
import numpy as np
import jax
import jax.numpy as jnp

def _softmax(x, axis=-1):
    return jax.nn.softmax(x, axis=axis)

def _gelu(x):
    return jax.nn.gelu(x, approximate=True)

def _silu(x):
    return jax.nn.silu(x)

def _sigmoid(x):
    return jax.nn.sigmoid(x)

def _layernorm(x, axis=-1, eps=1e-05):
    m = jnp.mean(x, axis=axis, keepdims=True)
    v = jnp.var(x, axis=axis, keepdims=True)
    return (x - m) / jnp.sqrt(v + eps)

def _scatter_add(tgt, idx, src, axis=0):
    return tgt.at[idx].add(src)

def _segment_sum(src, seg, n):
    return jax.ops.segment_sum(src, seg, n)
kernel_name = 'mk_flamingo_gated_d4_seqx_r8_f3f56f'

def setup_inputs(seed: int=0):
    np.random.seed(seed)
    _w = jnp.asarray

    def _rec_inputs():
        import jax
        import jax.numpy as jnp
        _rk = jax.random.key(seed)
        x = -0.0002928 + 1 * jax.random.normal(jax.random.fold_in(_rk, 1), (32, 64, 128), jnp.float32)
        _lenS = 64 - jax.random.randint(jax.random.fold_in(_rk, 7), (32,), 0, max(1, 64 // 4) + 1, jnp.int32)
        _lenS2 = 64 - jax.random.randint(jax.random.fold_in(_rk, 8), (32,), 0, max(1, 64 // 4) + 1, jnp.int32)
        _ctx_1024P = jax.random.normal(jax.random.fold_in(_rk, 11), (32, 16, 128), jnp.float32)
        _ctx_1024c = jax.random.dirichlet(jax.random.fold_in(_rk, 511), 0.3 * jnp.ones((16,), jnp.float32), (32, 64))
        _ctx_1024t = jnp.einsum('bsk,bkd->bsd', _ctx_1024c, _ctx_1024P)
        _ctx_1024t = _ctx_1024t * jax.lax.rsqrt(jnp.mean(jnp.square(_ctx_1024t)) + 1e-12) * 0.953939
        ctx_1024 = -1.39393e-06 + 0.999914 * (_ctx_1024t + 0.3 * jax.random.normal(jax.random.fold_in(_rk, 611), (32, 64, 128), jnp.float32))
        _validS = jnp.arange(64)[None, :] < _lenS[:, None]
        _validS2 = jnp.arange(64)[None, :] < _lenS2[:, None]
        _causal = jnp.tril(jnp.ones((64, 64), dtype=bool))
        mask_BxSxS2_ik1 = jnp.where(jnp.broadcast_to(_validS2[:, None, :], (32, 64, 64)), 1, 0).astype(jnp.int32)
        mask_BxS2_bf1 = jnp.ones((32, 64), dtype=bool)
        _g = jax.random.normal(jax.random.fold_in(_rk, 9001), (2, 4), jnp.float32)
        _g = jnp.sign(_g) * jnp.maximum(jnp.abs(_g), 1.0) + (_g == 0) * 1.0
        g_xattn = _g[0]
        g_ffn = _g[1]
        return (x, ctx_1024, mask_BxSxS2_ik1, mask_BxS2_bf1, g_xattn, g_ffn)
    x, ctx_1024, mask_BxSxS2_ik1, mask_BxS2_bf1, g_xattn, g_ffn = _rec_inputs()

    def _L0_xattn_setup():
        import jax, jax.numpy as jnp
        import numpy as np
        import math
        DIM_Q = 128
        DIM_V = 128
        DIM_O = 128
        H = 16
        DH_Q = DIM_Q // H
        DH_V = DIM_O // H
        TEMP = math.sqrt(DIM_O)
        EPS = 1e-05

        def layernorm(x, g, b):
            mu = jnp.mean(x, axis=-1, keepdims=True)
            var = jnp.mean(jnp.square(x - mu), axis=-1, keepdims=True)
            return (x - mu) * jax.lax.rsqrt(var + EPS) * g + b
        key = jax.random.key(seed)
        ks = jax.random.split(key, 8)
        B, LQ, LK = (2, 256, 256)
        s = 0.02
        return {'Q': jax.random.normal(ks[0], (B, LQ, DIM_Q), jnp.float32), 'K': jax.random.normal(ks[1], (B, LK, DIM_Q), jnp.float32), 'V': jax.random.normal(ks[2], (B, LK, DIM_V), jnp.float32), 'Wq': jax.random.normal(ks[3], (DIM_Q, DIM_Q), jnp.float32) * s, 'Wk': jax.random.normal(ks[4], (DIM_Q, DIM_Q), jnp.float32) * s, 'Wv': jax.random.normal(ks[5], (DIM_O, DIM_V), jnp.float32) * s, 'Wo': jax.random.normal(ks[6], (DIM_O, DIM_O), jnp.float32) * s, 'g_pre': jnp.ones((DIM_Q,), jnp.float32), 'b_pre': jnp.zeros((DIM_Q,), jnp.float32), 'g_ln': jnp.ones((DIM_O,), jnp.float32), 'b_ln': jnp.zeros((DIM_O,), jnp.float32)}
    _L0_xattn_all = _L0_xattn_setup()
    _L0_xattn_in = {k: v for k, v in _L0_xattn_all.items() if k in ('Wq', 'Wk', 'Wv', 'Wo', 'g_pre', 'b_pre', 'g_ln', 'b_ln')}
    del _L0_xattn_all

    def _L0_ffn_setup():
        import jax, jax.numpy as jnp
        import numpy as np
        FEATURES = 128
        D_IN = 128

        def fp8_gemm_optimized(x, input_scale, kernel, kernel_scale):
            s_in = input_scale[0]
            s_k = kernel_scale[0]
            x_q = (x.astype(jnp.float32) / s_in).astype(jnp.float8_e4m3fn)
            k_q = (kernel.astype(jnp.float32) / s_k).astype(jnp.float8_e4m3fn)
            y = jnp.dot(x_q.astype(jnp.float32), k_q.astype(jnp.float32), preferred_element_type=jnp.float32)
            return y * (s_in * s_k)
        key = jax.random.key(seed)
        kx, kk, kb = jax.random.split(key, 3)
        x = jax.random.normal(kx, (4, 1024, D_IN), dtype=jnp.float32)
        limit = np.sqrt(6.0 / (D_IN + FEATURES)).astype(np.float32)
        kernel = jax.random.uniform(kk, (D_IN, FEATURES), dtype=jnp.float32, minval=-limit, maxval=limit).astype(jnp.bfloat16)
        input_scale = jnp.ones((1,), dtype=jnp.float32)
        kernel_scale = jnp.ones((1,), dtype=jnp.float32)
        bias = jnp.zeros((FEATURES,), dtype=jnp.bfloat16)
        return {'x': x, 'kernel': kernel, 'input_scale': input_scale, 'kernel_scale': kernel_scale, 'bias': bias}
    _L0_ffn_all = _L0_ffn_setup()
    _L0_ffn_in = {k: v for k, v in _L0_ffn_all.items() if k in ('kernel', 'input_scale', 'kernel_scale', 'bias')}
    del _L0_ffn_all

    def _L1_xattn_setup():
        import jax, jax.numpy as jnp
        import numpy as np
        D_MODEL = 128
        NUM_HEADS = 16
        D_K = D_MODEL // NUM_HEADS
        NEG = -1000000000.0
        key = jax.random.key(seed)
        ks = jax.random.split(key, 9)
        B, S, D = (2, 256, D_MODEL)
        scale = 1.0 / np.sqrt(D)
        return {'query': jax.random.normal(ks[0], (B, S, D), jnp.float32), 'key': jax.random.normal(ks[1], (B, S, D), jnp.float32), 'value': jax.random.normal(ks[2], (B, S, D), jnp.float32), 'mask': jax.random.randint(ks[3], (B, S, S), 0, 2, jnp.int32), 'W_q': jax.random.normal(ks[4], (D, D), jnp.float32) * scale, 'W_k': jax.random.normal(ks[5], (D, D), jnp.float32) * scale, 'W_v': jax.random.normal(ks[6], (D, D), jnp.float32) * scale, 'W_o': jax.random.normal(ks[7], (D, D), jnp.float32) * scale, 'b_o': jax.random.normal(ks[8], (D,), jnp.float32) * 0.01}
    _L1_xattn_all = _L1_xattn_setup()
    _L1_xattn_in = {k: v for k, v in _L1_xattn_all.items() if k in ('W_q', 'W_k', 'W_v', 'W_o', 'b_o')}
    del _L1_xattn_all

    def _L1_ffn_setup():
        import jax, jax.numpy as jnp
        import numpy as np
        HIDDEN = 128
        NUM_EXPERTS = 8
        TOP_K = 2
        FFN = 512
        BATCH, SEQ = (4, 256)
        key = jax.random.key(seed)
        k_x, k_r, k_w1, k_w2 = jax.random.split(key, 4)
        x = jax.random.normal(k_x, (BATCH, SEQ, HIDDEN), dtype=jnp.float32)
        router_w = jax.random.normal(k_r, (NUM_EXPERTS, HIDDEN), dtype=jnp.float32) * (1.0 / np.sqrt(HIDDEN))
        lim = float(np.sqrt(6.0 / (FFN + HIDDEN)))
        expert_w1 = jax.random.uniform(k_w1, (NUM_EXPERTS, FFN, HIDDEN), dtype=jnp.float32, minval=-lim, maxval=lim)
        expert_w2 = jax.random.uniform(k_w2, (NUM_EXPERTS, HIDDEN, FFN), dtype=jnp.float32, minval=-lim, maxval=lim)
        return {'x': x, 'router_w': router_w, 'expert_w1': expert_w1, 'expert_w2': expert_w2}
    _L1_ffn_all = _L1_ffn_setup()
    _L1_ffn_in = {k: v for k, v in _L1_ffn_all.items() if k in ('router_w', 'expert_w1', 'expert_w2')}
    del _L1_ffn_all

    def _L2_xattn_setup():
        import jax, jax.numpy as jnp
        import numpy as np
        D_MODEL = 128
        QK_DIM = 64
        EPS = 1e-06

        def _linear_params(key, fan_in, fan_out):
            k1, k2 = jax.random.split(key)
            bound = 1.0 / np.sqrt(fan_in)
            W = jax.random.uniform(k1, (fan_out, fan_in), jnp.float32, -bound, bound)
            b = jax.random.uniform(k2, (fan_out,), jnp.float32, -bound, bound)
            return (W, b)
        key = jax.random.key(seed)
        ks = jax.random.split(key, 9)
        B, Tq, Tk = (4, 512, 512)
        queries = jax.random.normal(ks[0], (B, Tq, D_MODEL), jnp.float32)
        keys = jax.random.normal(ks[1], (B, Tk, D_MODEL), jnp.float32)
        values = jax.random.normal(ks[2], (B, Tk, D_MODEL), jnp.float32)
        query_mask = jnp.ones((B, Tq), dtype=bool)
        key_mask = jnp.ones((B, Tk), dtype=bool)
        Wg, bg = _linear_params(ks[3], D_MODEL, D_MODEL)
        Wv, bv = _linear_params(ks[4], D_MODEL, D_MODEL)
        Wq, bq = _linear_params(ks[5], D_MODEL, QK_DIM)
        Wk, bk = _linear_params(ks[6], D_MODEL, QK_DIM)
        Wo, bo = _linear_params(ks[7], D_MODEL, D_MODEL)
        return {'queries': queries, 'keys': keys, 'values': values, 'query_mask': query_mask, 'key_mask': key_mask, 'Wg': Wg, 'bg': bg, 'Wv': Wv, 'bv': bv, 'Wq': Wq, 'bq': bq, 'Wk': Wk, 'bk': bk, 'Wo': Wo, 'bo': bo}
    _L2_xattn_all = _L2_xattn_setup()
    _L2_xattn_in = {k: v for k, v in _L2_xattn_all.items() if k in ('Wg', 'bg', 'Wv', 'bv', 'Wq', 'bq', 'Wk', 'bk', 'Wo', 'bo')}
    del _L2_xattn_all

    def _L2_ffn_setup():
        import jax, jax.numpy as jnp
        import numpy as np
        EMBED_DIM = 128
        HIDDEN_DIM = 512
        NUM_EXPERTS = 8
        TOP_K = 2
        key = jax.random.key(seed)
        ks = jax.random.split(key, 4)
        std1 = float(np.sqrt(2.0 / EMBED_DIM))
        std2 = float(np.sqrt(2.0 / HIDDEN_DIM))
        x = jax.random.normal(ks[0], (1, 256, EMBED_DIM), dtype=jnp.float32)
        w_router = jax.random.normal(ks[1], (EMBED_DIM, NUM_EXPERTS), dtype=jnp.float32) * 0.02
        w1 = jax.random.normal(ks[2], (NUM_EXPERTS, EMBED_DIM, HIDDEN_DIM), dtype=jnp.float32) * std1
        b1 = jnp.zeros((NUM_EXPERTS, HIDDEN_DIM), dtype=jnp.float32)
        w2 = jax.random.normal(ks[3], (NUM_EXPERTS, HIDDEN_DIM, EMBED_DIM), dtype=jnp.float32) * std2
        b2 = jnp.zeros((NUM_EXPERTS, EMBED_DIM), dtype=jnp.float32)
        return {'x': x, 'w_router': w_router, 'w1': w1, 'b1': b1, 'w2': w2, 'b2': b2}
    _L2_ffn_all = _L2_ffn_setup()
    _L2_ffn_in = {k: v for k, v in _L2_ffn_all.items() if k in ('w_router', 'w1', 'b1', 'w2', 'b2')}
    del _L2_ffn_all

    def _L3_xattn_setup():
        import jax, jax.numpy as jnp
        import numpy as np
        B, T, D, H = (2, 256, 128, 16)
        DH = D // H
        key = jax.random.key(seed)
        ks = jax.random.split(key, 11)
        s = 1.0 / np.sqrt(D)
        return {'q': jax.random.normal(ks[0], (B, T, D), jnp.float32), 'k': jax.random.normal(ks[1], (B, T, D), jnp.float32), 'v': jax.random.normal(ks[2], (B, T, D), jnp.float32), 'wq_w': jax.random.normal(ks[3], (D, D), jnp.float32) * s, 'wq_b': jnp.zeros((D,), jnp.float32), 'wk_w': jax.random.normal(ks[4], (D, D), jnp.float32) * s, 'wk_b': jnp.zeros((D,), jnp.float32), 'wv_w': jax.random.normal(ks[5], (D, D), jnp.float32) * s, 'wv_b': jnp.zeros((D,), jnp.float32), 'wo_w': jax.random.normal(ks[6], (D, D), jnp.float32) * s, 'wo_b': jnp.zeros((D,), jnp.float32)}
    _L3_xattn_all = _L3_xattn_setup()
    _L3_xattn_in = {k: v for k, v in _L3_xattn_all.items() if k in ('wq_w', 'wq_b', 'wk_w', 'wk_b', 'wv_w', 'wv_b', 'wo_w', 'wo_b')}
    del _L3_xattn_all

    def _L3_ffn_setup():
        import jax, jax.numpy as jnp
        import numpy as np
        B, S, H, F, E, K = (2, 256, 128, 512, 8, 2)

        def _init_w(key, shape, fan_in):
            return jax.random.normal(key, shape, jnp.float32) * fan_in ** (-0.5)

        def _ffn(x, wi, bi, wo, bo):
            return jax.nn.selu(x @ wi + bi) @ wo + bo
        key = jax.random.key(seed)
        ks = jax.random.split(key, 6)
        return {'x': jax.random.normal(ks[0], (B, S, H), jnp.float32), 'gate_wi': _init_w(ks[1], (H, F), H), 'gate_bi': jnp.zeros((F,), jnp.float32), 'gate_wo': _init_w(ks[2], (F, H), F), 'gate_bo': jnp.zeros((H,), jnp.float32), 'exp_wi': _init_w(ks[3], (E, H, F), H), 'exp_bi': jnp.zeros((E, F), jnp.float32), 'exp_wo': _init_w(ks[4], (E, F, H), F), 'exp_bo': jnp.zeros((E, H), jnp.float32)}
    _L3_ffn_all = _L3_ffn_setup()
    _L3_ffn_in = {k: v for k, v in _L3_ffn_all.items() if k in ('gate_wi', 'gate_bi', 'gate_wo', 'gate_bo', 'exp_wi', 'exp_bi', 'exp_wo', 'exp_bo')}
    del _L3_ffn_all
    return {'x': x, 'ctx_1024': ctx_1024, 'mask_BxSxS2_ik1': mask_BxSxS2_ik1, 'mask_BxS2_bf1': mask_BxS2_bf1, 'g_xattn': g_xattn, 'g_ffn': g_ffn, 'L0_xattn_Wq': _L0_xattn_in['Wq'], 'L0_xattn_Wk': _L0_xattn_in['Wk'], 'L0_xattn_Wv': _L0_xattn_in['Wv'], 'L0_xattn_Wo': _L0_xattn_in['Wo'], 'L0_xattn_g_pre': _L0_xattn_in['g_pre'], 'L0_xattn_b_pre': _L0_xattn_in['b_pre'], 'L0_xattn_g_ln': _L0_xattn_in['g_ln'], 'L0_xattn_b_ln': _L0_xattn_in['b_ln'], 'L0_ffn_kernel': _L0_ffn_in['kernel'], 'L0_ffn_input_scale': _L0_ffn_in['input_scale'], 'L0_ffn_kernel_scale': _L0_ffn_in['kernel_scale'], 'L0_ffn_bias': _L0_ffn_in['bias'], 'L1_xattn_W_q': _L1_xattn_in['W_q'], 'L1_xattn_W_k': _L1_xattn_in['W_k'], 'L1_xattn_W_v': _L1_xattn_in['W_v'], 'L1_xattn_W_o': _L1_xattn_in['W_o'], 'L1_xattn_b_o': _L1_xattn_in['b_o'], 'L1_ffn_router_w': _L1_ffn_in['router_w'], 'L1_ffn_expert_w1': _L1_ffn_in['expert_w1'], 'L1_ffn_expert_w2': _L1_ffn_in['expert_w2'], 'L2_xattn_Wg': _L2_xattn_in['Wg'], 'L2_xattn_bg': _L2_xattn_in['bg'], 'L2_xattn_Wv': _L2_xattn_in['Wv'], 'L2_xattn_bv': _L2_xattn_in['bv'], 'L2_xattn_Wq': _L2_xattn_in['Wq'], 'L2_xattn_bq': _L2_xattn_in['bq'], 'L2_xattn_Wk': _L2_xattn_in['Wk'], 'L2_xattn_bk': _L2_xattn_in['bk'], 'L2_xattn_Wo': _L2_xattn_in['Wo'], 'L2_xattn_bo': _L2_xattn_in['bo'], 'L2_ffn_w_router': _L2_ffn_in['w_router'], 'L2_ffn_w1': _L2_ffn_in['w1'], 'L2_ffn_b1': _L2_ffn_in['b1'], 'L2_ffn_w2': _L2_ffn_in['w2'], 'L2_ffn_b2': _L2_ffn_in['b2'], 'L3_xattn_wq_w': _L3_xattn_in['wq_w'], 'L3_xattn_wq_b': _L3_xattn_in['wq_b'], 'L3_xattn_wk_w': _L3_xattn_in['wk_w'], 'L3_xattn_wk_b': _L3_xattn_in['wk_b'], 'L3_xattn_wv_w': _L3_xattn_in['wv_w'], 'L3_xattn_wv_b': _L3_xattn_in['wv_b'], 'L3_xattn_wo_w': _L3_xattn_in['wo_w'], 'L3_xattn_wo_b': _L3_xattn_in['wo_b'], 'L3_ffn_gate_wi': _L3_ffn_in['gate_wi'], 'L3_ffn_gate_bi': _L3_ffn_in['gate_bi'], 'L3_ffn_gate_wo': _L3_ffn_in['gate_wo'], 'L3_ffn_gate_bo': _L3_ffn_in['gate_bo'], 'L3_ffn_exp_wi': _L3_ffn_in['exp_wi'], 'L3_ffn_exp_bi': _L3_ffn_in['exp_bi'], 'L3_ffn_exp_wo': _L3_ffn_in['exp_wo'], 'L3_ffn_exp_bo': _L3_ffn_in['exp_bo']}

def reference(x, ctx_1024, mask_BxSxS2_ik1, mask_BxS2_bf1, g_xattn, g_ffn, L0_xattn_Wq, L0_xattn_Wk, L0_xattn_Wv, L0_xattn_Wo, L0_xattn_g_pre, L0_xattn_b_pre, L0_xattn_g_ln, L0_xattn_b_ln, L0_ffn_kernel, L0_ffn_input_scale, L0_ffn_kernel_scale, L0_ffn_bias, L1_xattn_W_q, L1_xattn_W_k, L1_xattn_W_v, L1_xattn_W_o, L1_xattn_b_o, L1_ffn_router_w, L1_ffn_expert_w1, L1_ffn_expert_w2, L2_xattn_Wg, L2_xattn_bg, L2_xattn_Wv, L2_xattn_bv, L2_xattn_Wq, L2_xattn_bq, L2_xattn_Wk, L2_xattn_bk, L2_xattn_Wo, L2_xattn_bo, L2_ffn_w_router, L2_ffn_w1, L2_ffn_b1, L2_ffn_w2, L2_ffn_b2, L3_xattn_wq_w, L3_xattn_wq_b, L3_xattn_wk_w, L3_xattn_wk_b, L3_xattn_wv_w, L3_xattn_wv_b, L3_xattn_wo_w, L3_xattn_wo_b, L3_ffn_gate_wi, L3_ffn_gate_bi, L3_ffn_gate_wo, L3_ffn_gate_bo, L3_ffn_exp_wi, L3_ffn_exp_bi, L3_ffn_exp_wo, L3_ffn_exp_bo):
    import jax
    import jax.numpy as jnp

    def _L0_xattn_ref(Q, K, V, Wq, Wk, Wv, Wo, g_pre, b_pre, g_ln, b_ln):
        import jax, jax.numpy as jnp
        import numpy as np
        import math
        DIM_Q = 128
        DIM_V = 128
        DIM_O = 128
        H = 16
        DH_Q = DIM_Q // H
        DH_V = DIM_O // H
        TEMP = math.sqrt(DIM_O)
        EPS = 1e-05

        def layernorm(x, g, b):
            mu = jnp.mean(x, axis=-1, keepdims=True)
            var = jnp.mean(jnp.square(x - mu), axis=-1, keepdims=True)
            return (x - mu) * jax.lax.rsqrt(var + EPS) * g + b
        B, LQ, _ = Q.shape
        LK = K.shape[1]
        Qn = layernorm(Q, g_pre, b_pre)
        Kn = layernorm(K, g_pre, b_pre)
        q = (Qn @ Wq.T).reshape(B, LQ, H, DH_Q)
        k = (Kn @ Wk.T).reshape(B, LK, H, DH_Q)
        v = (V @ Wv.T).reshape(B, LK, H, DH_V)
        L = jnp.einsum('bqhd,bkhd->bhqk', q, k) / TEMP
        L = jnp.clip(L, -10000.0, 10000.0)
        A = jax.nn.softmax(L, axis=-1)
        O = jnp.einsum('bhqk,bkhd->bqhd', A, v).reshape(B, LQ, DIM_O)
        O = layernorm(O, g_ln, b_ln)
        O = O + jax.nn.gelu(O @ Wo.T, approximate=False)
        return O

    def _L0_ffn_ref(x, kernel, input_scale, kernel_scale, bias):
        import jax, jax.numpy as jnp
        import numpy as np
        FEATURES = 128
        D_IN = 128

        def fp8_gemm_optimized(x, input_scale, kernel, kernel_scale):
            s_in = input_scale[0]
            s_k = kernel_scale[0]
            x_q = (x.astype(jnp.float32) / s_in).astype(jnp.float8_e4m3fn)
            k_q = (kernel.astype(jnp.float32) / s_k).astype(jnp.float8_e4m3fn)
            y = jnp.dot(x_q.astype(jnp.float32), k_q.astype(jnp.float32), preferred_element_type=jnp.float32)
            return y * (s_in * s_k)
        dtype = jnp.bfloat16
        x = x.astype(dtype)
        orig_shape = x.shape
        x2 = x.reshape(-1, x.shape[-1])
        y = fp8_gemm_optimized(x2, input_scale, kernel, kernel_scale)
        y = y.astype(dtype) + bias
        return y.reshape(orig_shape[:-1] + (FEATURES,))

    def _L1_xattn_ref(query, key, value, mask, W_q, W_k, W_v, W_o, b_o):
        import jax, jax.numpy as jnp
        import numpy as np
        D_MODEL = 128
        NUM_HEADS = 16
        D_K = D_MODEL // NUM_HEADS
        NEG = -1000000000.0
        B, S, D = query.shape
        H, dk = (NUM_HEADS, D_K)

        def split_heads(x, W):
            return jnp.einsum('bsd,ed->bse', x, W).reshape(B, S, H, dk).transpose(0, 2, 1, 3)
        Q = split_heads(query, W_q)
        K = split_heads(key, W_k)
        V = split_heads(value, W_v)
        scores = jnp.einsum('bhqd,bhkd->bhqk', Q, K) / jnp.sqrt(jnp.float32(dk))
        scores = jnp.where(mask[:, None, :, :] == 0, NEG, scores)
        attn = jax.nn.softmax(scores, axis=-1)
        out = jnp.einsum('bhqk,bhkd->bhqd', attn, V)
        out = out.transpose(0, 2, 1, 3).reshape(B, S, D)
        return jnp.einsum('bsd,ed->bse', out, W_o) + b_o

    def _L1_ffn_ref(x, router_w, expert_w1, expert_w2):
        import jax, jax.numpy as jnp
        import numpy as np
        HIDDEN = 128
        NUM_EXPERTS = 8
        TOP_K = 2
        FFN = 512
        BATCH, SEQ = (4, 256)
        B, S, D = x.shape
        xf = x.reshape(-1, D)
        scores = xf @ router_w.T
        top_v, top_i = jax.lax.top_k(scores, TOP_K)
        routing_w = jax.nn.softmax(top_v, axis=-1)
        out = jnp.zeros_like(xf)
        for e in range(NUM_EXPERTS):
            w_e = jnp.sum(jnp.where(top_i == e, routing_w, 0.0), axis=-1)
            h = jax.nn.gelu(xf @ expert_w1[e].T, approximate=False)
            out = out + h @ expert_w2[e].T * w_e[:, None]
        return out.reshape(B, S, D)

    def _L2_xattn_ref(queries, keys, values, query_mask, key_mask, Wg, bg, Wv, bv, Wq, bq, Wk, bk, Wo, bo):
        import jax, jax.numpy as jnp
        import numpy as np
        D_MODEL = 128
        QK_DIM = 64
        EPS = 1e-06

        def _linear_params(key, fan_in, fan_out):
            k1, k2 = jax.random.split(key)
            bound = 1.0 / np.sqrt(fan_in)
            W = jax.random.uniform(k1, (fan_out, fan_in), jnp.float32, -bound, bound)
            b = jax.random.uniform(k2, (fan_out,), jnp.float32, -bound, bound)
            return (W, b)
        u = jax.nn.silu(jnp.einsum('btd,ed->bte', queries, Wg) + bg)
        v = jnp.einsum('btd,ed->bte', values, Wv) + bv
        q = jax.nn.relu(jnp.einsum('btd,sd->bts', queries, Wq) + bq) ** 2
        k = jax.nn.relu(jnp.einsum('btd,sd->bts', keys, Wk) + bk) ** 2
        km = key_mask[..., None].astype(k.dtype)
        k = k * km
        v = v * km
        kv = jnp.einsum('bks,bkd->bsd', k, v)
        k_sum = jnp.sum(k, axis=1)
        qkv = jnp.einsum('bqs,bsd->bqd', q, kv)
        z = jnp.einsum('bqs,bs->bq', q, k_sum) + EPS
        a = qkv / z[..., None]
        out = jnp.einsum('btd,ed->bte', u * a, Wo) + bo
        out = out * query_mask[..., None].astype(out.dtype)
        return out

    def _L2_ffn_ref(x, w_router, w1, b1, w2, b2):
        import jax, jax.numpy as jnp
        import numpy as np
        EMBED_DIM = 128
        HIDDEN_DIM = 512
        NUM_EXPERTS = 8
        TOP_K = 2
        orig_shape = x.shape
        xf = x.reshape(-1, EMBED_DIM)
        logits = xf @ w_router
        probs = jax.nn.softmax(logits, axis=-1)
        topk_w, topk_idx = jax.lax.top_k(probs, TOP_K)
        mask = jax.nn.one_hot(topk_idx, NUM_EXPERTS, dtype=xf.dtype)
        weights = jnp.sum(topk_w[..., None] * mask, axis=1)
        h = jnp.einsum('te,ieh->tih', xf, w1) + b1
        h = jax.nn.gelu(h)
        out = jnp.einsum('tih,ihe->tie', h, w2) + b2
        out = jnp.sum(out * weights[..., None], axis=1)
        return out.reshape(orig_shape)

    def _L3_xattn_ref(q, k, v, wq_w, wq_b, wk_w, wk_b, wv_w, wv_b, wo_w, wo_b):
        import jax, jax.numpy as jnp
        import numpy as np
        B, T, D, H = (2, 256, 128, 16)
        DH = D // H
        b, t, d = q.shape
        wq = (q @ wq_w.T + wq_b).reshape(b, t, H, DH)
        wk = (k @ wk_w.T + wk_b).reshape(b, t, H, DH)
        wv = (v @ wv_w.T + wv_b).reshape(b, t, H, DH)
        scores = jnp.einsum('bthd,bshd->bhts', wq, wk) / jnp.sqrt(jnp.float32(DH))
        probs = jax.nn.softmax(scores, axis=-1)
        attn = jnp.einsum('bhts,bshd->bthd', probs, wv)
        attn = attn.reshape(b, t, d)
        return attn @ wo_w.T + wo_b

    def _L3_ffn_ref(x, gate_wi, gate_bi, gate_wo, gate_bo, exp_wi, exp_bi, exp_wo, exp_bo):
        import jax, jax.numpy as jnp
        import numpy as np
        B, S, H, F, E, K = (2, 256, 128, 512, 8, 2)

        def _init_w(key, shape, fan_in):
            return jax.random.normal(key, shape, jnp.float32) * fan_in ** (-0.5)

        def _ffn(x, wi, bi, wo, bo):
            return jax.nn.selu(x @ wi + bi) @ wo + bo
        Bb, Ss, Hh = x.shape
        xf = x.reshape(-1, Hh)
        gate_logits = _ffn(xf, gate_wi, gate_bi, gate_wo, gate_bo)
        topv, topi = jax.lax.top_k(gate_logits, K)
        topv = topv / jnp.sum(topv, axis=-1, keepdims=True)
        onehot = (topi[..., None] == jnp.arange(E)).astype(x.dtype)
        w = jnp.einsum('nk,nke->ne', topv, onehot)
        h = jax.nn.selu(jnp.einsum('nh,ehf->enf', xf, exp_wi) + exp_bi[:, None, :])
        out_e = jnp.einsum('enf,efh->enh', h, exp_wo) + exp_bo[:, None, :]
        out = jnp.einsum('enh,ne->nh', out_e, w)
        return out.reshape(Bb, Ss, Hh)
    x = x + jnp.tanh(g_xattn[0]) * _L0_xattn_ref(_layernorm(x, axis=-1), ctx_1024, ctx_1024, L0_xattn_Wq, L0_xattn_Wk, L0_xattn_Wv, L0_xattn_Wo, L0_xattn_g_pre, L0_xattn_b_pre, L0_xattn_g_ln, L0_xattn_b_ln)
    x = x + jnp.tanh(g_ffn[0]) * _L0_ffn_ref(_layernorm(x, axis=-1), L0_ffn_kernel, L0_ffn_input_scale, L0_ffn_kernel_scale, L0_ffn_bias)
    x = x + jnp.tanh(g_xattn[1]) * _L1_xattn_ref(_layernorm(x, axis=-1), ctx_1024, ctx_1024, mask_BxSxS2_ik1, L1_xattn_W_q, L1_xattn_W_k, L1_xattn_W_v, L1_xattn_W_o, L1_xattn_b_o)
    x = x + jnp.tanh(g_ffn[1]) * _L1_ffn_ref(_layernorm(x, axis=-1), L1_ffn_router_w, L1_ffn_expert_w1, L1_ffn_expert_w2)
    x = x + jnp.tanh(g_xattn[2]) * _L2_xattn_ref(_layernorm(x, axis=-1), ctx_1024, ctx_1024, mask_BxS2_bf1, mask_BxS2_bf1, L2_xattn_Wg, L2_xattn_bg, L2_xattn_Wv, L2_xattn_bv, L2_xattn_Wq, L2_xattn_bq, L2_xattn_Wk, L2_xattn_bk, L2_xattn_Wo, L2_xattn_bo)
    x = x + jnp.tanh(g_ffn[2]) * _L2_ffn_ref(_layernorm(x, axis=-1), L2_ffn_w_router, L2_ffn_w1, L2_ffn_b1, L2_ffn_w2, L2_ffn_b2)
    x = x + jnp.tanh(g_xattn[3]) * _L3_xattn_ref(_layernorm(x, axis=-1), ctx_1024, ctx_1024, L3_xattn_wq_w, L3_xattn_wq_b, L3_xattn_wk_w, L3_xattn_wk_b, L3_xattn_wv_w, L3_xattn_wv_b, L3_xattn_wo_w, L3_xattn_wo_b)
    x = x + jnp.tanh(g_ffn[3]) * _L3_ffn_ref(_layernorm(x, axis=-1), L3_ffn_gate_wi, L3_ffn_gate_bi, L3_ffn_gate_wo, L3_ffn_gate_bo, L3_ffn_exp_wi, L3_ffn_exp_bi, L3_ffn_exp_wo, L3_ffn_exp_bo)
    return x

_drawn_inputs = setup_inputs


def setup_inputs(seed=0):
    import zlib

    import numpy as np

    out = dict(_drawn_inputs(seed))
    spreads = {'L0_xattn_g_pre': (1.0, 0.6),
     'L0_xattn_b_pre': (0.0, 0.8),
     'L0_xattn_g_ln': (1.0, 0.2),
     'L0_xattn_b_ln': (0.0, 0.1),
     'L0_ffn_bias': (0.0, 0.1),
     'L2_ffn_b1': (0.0, 0.513),
     'L2_ffn_b2': (0.0, 0.437),
     'L3_xattn_wq_b': (0.0, 0.354),
     'L3_xattn_wk_b': (0.0, 2.0),
     'L3_xattn_wv_b': (0.0, 0.1),
     'L3_xattn_wo_b': (0.0, 0.1),
     'L3_ffn_gate_bi': (0.0, 0.1),
     'L3_ffn_gate_bo': (0.0, 0.1),
     'L3_ffn_exp_bi': (0.0, 0.8),
     'L3_ffn_exp_bo': (0.0, 0.8)}
    factors = {'g_ffn': 24.104,
     'L0_xattn_Wq': 2.689,
     'L0_xattn_Wk': 2.881,
     'L1_xattn_b_o': 3.065,
     'L2_xattn_bg': 6.167,
     'L2_xattn_bv': 4.739,
     'L2_xattn_Wq': 13.332,
     'L2_xattn_bq': 64.0,
     'L2_xattn_Wk': 14.477,
     'L2_xattn_bk': 64.0}
    for name, (base, spread) in spreads.items():
        noise = np.random.default_rng([zlib.crc32(name.encode()), seed]).standard_normal(out[name].shape)
        drawn = base * np.exp(spread * noise) if base else spread * noise
        out[name] = jnp.asarray(drawn.astype(out[name].dtype))
    for name, factor in factors.items():
        out[name] = (out[name] * factor).astype(out[name].dtype)
    return out
```

```python
import itertools
import math

import concourse.bass as bass
from concourse import mybir
from collections import namedtuple
from contextlib import ExitStack, contextmanager

F32, BF16, F16, I32, U32, U8, FP8 = (mybir.dt.float32, mybir.dt.bfloat16, mybir.dt.float16,
                                 mybir.dt.int32, mybir.dt.uint32, mybir.dt.uint8, mybir.dt.float8e4)
ACT, ALU = mybir.ActivationFunctionType, mybir.AluOpType
AX_X = mybir.AxisListType.X

B, S, D, H, DH = 32, 64, 128, 16, 8
P = 128
N = B * S
T = N // P
E, F = 8, 512
FC = F // P
HALF = H // 2
VW = 2 * (DH + 1)
CH = H // 2
PAIRS = 2 * N
NB = PAIRS // P + E
NBX = NB + 8
LN_EPS = 1e-5
NEG = -1000000000.0
SELU_SCALE = 1.0507009873554804934193349852946
SELU_ALPHA = 1.6732632423543772848170429916717
KV_EPS = 1e-6
SEM_NUMBERS = itertools.cycle((range(110, 150), range(160, 200)))
GATHER_NUMBERS = range(210, 228)


def upto(engine, sem, tile, per=1):
    if isinstance(tile, int) and tile < 0:
        return
    engine.wait_ge(sem, (tile + 1) * per)


def settle(engine, *waits):
    waits = [(sem, value) for sem, value in waits if not isinstance(value, int) or value > 0]
    if any(not isinstance(value, int) for _, value in waits):
        waits = [(sem, value if isinstance(value, int) else engine.snap(value)) for sem, value in waits]
        for _, value in waits:
            if not isinstance(value, int):
                engine.compute_val(value)
        engine.wait_ge(waits[0][0], 1)
    for sem, value in waits:
        engine.wait_ge(sem, value)


def arrived(engine, sems_, u, q):
    engine.wait_ge(sems_[q], (u - q) * 8 + 16)


def inside(u):
    return not isinstance(u, int) or 0 <= u < T


class Memory:
    pass


@contextmanager
def sems(nc, prefix, *names):
    numbers = next(SEM_NUMBERS)
    free = iter(numbers)
    with ExitStack() as c:
        one = lambda n: c.enter_context(nc.semaphore(prefix + n, num=next(free)))
        Semaphores = namedtuple("Semaphores", [n.rstrip("*") for n in names])
        yield Semaphores(*([one(f"{n[:-1]}{i}") for i in range(2)] if n.endswith("*") else one(n) for n in names))
        nc.sync.sem_clear(numbers)


def row(tensor, t):
    return tensor[:, tile_of(t), :].rearrange("p a d -> p (a d)")


def tile_of(t):
    return bass.ds(t, 1) if not isinstance(t, int) else slice(t, t + 1)


def pipeline(eng, step, first, last, steady):
    lo, hi = steady
    for t in range(first, lo):
        step(t, t % 2)
    with eng.Fori(lo, hi, 2) as i:
        step(i, lo % 2)
        step(i + 1, (lo + 1) % 2)
    for t in range(hi, last + 1):
        step(t, t % 2)


def batch_stats(nc, m, name, bn6, rstd, nmr, double=False):
    with sems(nc, name, "chain", "var_ready", "pow_done") as s, nc.Block() as block:
        v, ve, pw = s.chain, s.var_ready, s.pow_done
        sm, df, var = m.st_a, m.st_b, m.st_c

        @block.vector
        def _(dve):
            nc.vector.tensor_tensor(sm[:], bn6[:, :, 1], bn6[:, :, 4], ALU.add).then_inc(v, 1)
            nc.vector.tensor_tensor(df[:], bn6[:, :, 1], bn6[:, :, 4], ALU.subtract).then_inc(v, 1)
            nc.vector.tensor_tensor(var[:], bn6[:, :, 2], bn6[:, :, 5], ALU.add).then_inc(v, 1)
            dve.wait_ge(v, 3)
            nc.vector.scalar_tensor_tensor(m.st_d[:], df[:], 0.25, df[:], ALU.mult, ALU.mult).then_inc(v, 1)
            dve.wait_ge(v, 4)
            nc.vector.scalar_tensor_tensor(var[:], var[:], 1.0 / D, m.st_d[:], ALU.mult, ALU.add).then_inc(v, 1)
            dve.wait_ge(v, 5)
            nc.vector.tensor_scalar(m.st_e[:], var[:], LN_EPS, None, ALU.add).then_inc(ve, 1)
            dve.wait_ge(pw, 1)
            if double:
                nc.vector.tensor_tensor(df[:], rstd[:], rstd[:], ALU.mult).then_inc(v, 1)
                dve.wait_ge(v, 6)
                nc.vector.tensor_tensor(df[:], df[:], var[:], ALU.mult).then_inc(v, 1)
                dve.wait_ge(v, 7)
                nc.vector.tensor_scalar(m.st_e[:], df[:], LN_EPS, None, ALU.add).then_inc(ve, 1)
                dve.wait_ge(pw, 2)
                nc.vector.tensor_tensor(rstd[:], rstd[:], m.st_d[:], ALU.mult).then_inc(v, 1)
                dve.wait_ge(v, 8)
            nc.vector.scalar_tensor_tensor(nmr[:], sm[:], -0.5, rstd[:], ALU.mult, ALU.mult)

        @block.gpsimd
        def _(pool):
            pool.wait_ge(ve, 1)
            nc.gpsimd.tensor_tensor(rstd[:], m.st_e[:], m.minus_half[:], ALU.pow).then_inc(pw, 1)
            if double:
                pool.wait_ge(ve, 2)
                nc.gpsimd.tensor_tensor(m.st_d[:], m.st_e[:], m.minus_half[:], ALU.pow).then_inc(pw, 1)


def attention(nc, m, layer, wq, wk, wv, wo, bq=0.0, bk=0.0, bv=None, tg=None, out_bias=None):
    L0, L1 = layer == 0, layer == 1
    lag = 2 if L0 else 1
    scale = 1.0 / D ** 0.5 if L0 else 1.0 / DH ** 0.5
    clip = 10000.0 / scale
    PT, A, QKV = (m.PT0, m.PT1), m.bankA, m.bankB
    names = ["ctx_in*", "mask_in*", "xn_ready", "xT_done", "xnT_ready", "qk_done", "v_done", "k_out", "v_out",
             "kexp_ready", "scores_done", "pred", "masked", "max_done", "clipped", "sub_done", "exp_done",
             "pt_done", "pt_out", "pv_done", "rec_done", "raw_ready", "stats_done", "var_ready", "pow_done", "hat_done",
             "o_ready", "oT_done", "oT_ready", "out_done", "x_done", "bias_done"]
    first, last = -4, T - 1 + lag
    steady = (3, 11)
    with ExitStack() as c:
        s = c.enter_context(sems(nc, f"a{layer}_", *names))
        block = c.enter_context(nc.Block())

        @block.sync
        def _(sp):
            def step(t, p):
                u, q = t + 3, 1 - p
                if inside(u):
                    upto(sp, s.v_done, u - 2)
                    sp.dma_start(m.ctx_t[q][:], m.ctxT_dram[:, bass.ds(u * P, P)]).then_inc(s.ctx_in[q], 16)
                    if L1:
                        upto(sp, s.pred, u - 2)
                        sp.dma_start(m.mask_t[q][:], m.mask_dram[bass.ds(u * P, P), :]).then_inc(s.mask_in[q], 16)
            pipeline(sp, step, first, last, steady)

        @block.vector
        def _(dve):
            def soften(u, q):
                if L1:
                    arrived(dve, s.mask_in, u, q)
                    nc.vector.tensor_scalar(m.pred[q][:], m.mask_t[q][:], 0, None, ALU.is_equal).then_inc(s.pred, 1)
                for r in range(2):
                    sc = m.S[q][:, r * F:(r + 1) * F].rearrange("p (h k) -> p h k", k=S)
                    pr = m.probs[q][:, r * F:(r + 1) * F].rearrange("p (h k) -> p h k", k=S)
                    mx = m.rowmax[q][:, r * HALF:(r + 1) * HALF]
                    if not L1:
                        dve.wait_ge(s.scores_done, u * 2 + r + 1)
                    else:
                        settle(dve, (s.scores_done, u * 2 + r + 1), (s.pred, u + 1))
                        nc.vector.copy_predicated(sc, m.pred[q][:].unsqueeze(1).to_broadcast([P, HALF, S]),
                                                  m.negs[:].unsqueeze(1).to_broadcast([P, HALF, S])).then_inc(s.masked, 1)
                        dve.wait_ge(s.masked, u * 2 + r + 1)
                    nc.vector.tensor_reduce(mx, sc, AX_X, ALU.max).then_inc(s.max_done, 1)
                    dve.wait_ge(s.max_done, u * 2 + r + 1)
                    if r == 0:
                        upto(dve, s.pt_done, u - 2, 2)
                    rows = mx.unsqueeze(2).to_broadcast([P, HALF, S])
                    if L0:
                        nc.vector.tensor_scalar(mx, mx, -clip, clip, ALU.max, ALU.min).then_inc(s.clipped, 1)
                        dve.wait_ge(s.clipped, u * 2 + r + 1)
                        nc.vector.scalar_tensor_tensor(pr, sc, -clip, rows, ALU.max, ALU.subtract).then_inc(s.sub_done, 1)
                    else:
                        nc.vector.tensor_tensor(pr, sc, rows, ALU.subtract).then_inc(s.sub_done, 1)

            def step(t, p):
                if L0 and inside(t):
                    for r in range(2):
                        dve.wait_ge(s.pt_done, t * 2 + r + 1)
                        if r == 0:
                            upto(dve, s.pv_done, t - 1)
                        nc.vector.tensor_scalar(m.PTs[:, r * F:(r + 1) * F], PT[r][:], 1.0, None,
                                                ALU.min).then_inc(s.pt_out, 1)
                if L0 and inside(t - 1):
                    u, q = t - 1, 1 - p
                    upto(dve, s.pow_done, u)
                    upto(dve, s.stats_done, u, 2)
                    nc.vector.tensor_scalar(m.raw[q][:], m.raw[q][:], m.omv[q][:, 0:1], m.orstd[q][:],
                                            ALU.subtract, ALU.mult).then_inc(s.hat_done, 1)
                    dve.wait_ge(s.hat_done, 2 * u + 1)
                    nc.vector.tensor_tensor(m.raw[q][:], m.raw[q][:], m.g_ln, ALU.mult).then_inc(s.hat_done, 1)
                    dve.wait_ge(s.hat_done, 2 * u + 2)
                    upto(dve, s.oT_done, u - 2)
                    nc.vector.tensor_tensor(m.os[q][:], m.raw[q][:], m.b_ln, ALU.add).then_inc(s.o_ready, 1)
                    upto(dve, s.o_ready, u)
                    nc.vector.tensor_copy(row(m.ola, u), m.os[q][:])
                if inside(t + 1):
                    soften(t + 1, 1 - p)
                if inside(t):
                    o = m.PT0[:, 0:H * (DH + 1)].rearrange("p (h e) -> p h e", e=DH + 1)
                    upto(dve, s.pv_done, t)
                    nc.vector.reciprocal(m.rden[:], o[:, :, DH]).then_inc(s.rec_done, 1)
                    upto(dve, s.rec_done, t)
                    if not L0:
                        upto(dve, s.oT_done, t - 2)
                    dst = (m.raw if L0 else m.os)[p][:]
                    nc.vector.tensor_tensor(dst.rearrange("p (h d) -> p h d", d=DH), o[:, :, 0:DH],
                                            m.rden[:].unsqueeze(2).to_broadcast([P, H, DH]),
                                            ALU.mult).then_inc(s.raw_ready if L0 else s.o_ready, 1)
                    if L0:
                        upto(dve, s.raw_ready, t)
                        nc.vector.bn_stats(m.obn[:], m.raw[p][:]).then_inc(s.stats_done, 1)
                        settle(dve, (s.stats_done, 2 * t + 1))
                        nc.vector.bn_aggr(m.omv[p][:], m.obn[:]).then_inc(s.stats_done, 1)
                        dve.wait_ge(s.stats_done, 2 * t + 2)
                        nc.vector.tensor_scalar(m.ovar[p][:], m.omv[p][:, 1:2], LN_EPS, None, ALU.add).then_inc(s.var_ready, 1)
                u = t - lag
                if inside(u):
                    upto(dve, s.out_done, u)
                    if L0:
                        nc.vector.tensor_copy(row(m.za, u), m.PT1[:, 0:D]).then_inc(s.x_done, 1)
                    else:
                        xt = row(m.x, u)
                        nc.vector.scalar_tensor_tensor(xt, m.PT1[:, 0:D], tg, xt, ALU.mult, ALU.add).then_inc(s.x_done, 1)
                        upto(dve, s.x_done, u)
                        nc.vector.tensor_tensor(xt, xt, out_bias, ALU.add).then_inc(s.bias_done, 1)
                        upto(dve, s.bias_done, u)
                        nc.vector.bn_stats(row(m.bn6, u), xt)
                u, q = t + 4, p
                if inside(u):
                    upto(dve, s.xT_done, u - 2)
                    ln = nc.vector.tensor_scalar(m.xn[q][:], row(m.x, u), m.rstd[:, tile_of(u)], m.nmr[:, tile_of(u)],
                                                 ALU.mult, ALU.add)
                    if L0:
                        ln = nc.vector.tensor_scalar(m.cn[q][:], row(m.ctx, u), m.crstd[:, tile_of(u)],
                                                     m.cnmr[:, tile_of(u)], ALU.mult, ALU.add)
                    ln.then_inc(s.xn_ready, 1)
            pipeline(dve, step, first, last, steady)

        @block.gpsimd
        def _(pool):
            def step(t, p):
                u, q = t + 2, p
                if inside(u):
                    upto(pool, s.k_out, u)
                    upto(pool, s.scores_done, u - 2, 2)
                    nc.gpsimd.tensor_tensor(m.kexp[q][:], m.kT[q][:].unsqueeze(1).to_broadcast([P, HALF, P]),
                                            m.head_mask.unsqueeze(2).to_broadcast([P, HALF, P]),
                                            ALU.mult).then_inc(s.kexp_ready, 1)
                if L0 and inside(t):
                    upto(pool, s.var_ready, t)
                    nc.gpsimd.tensor_tensor(m.orstd[p][:], m.ovar[p][:], m.minus_half[:, 0:1], ALU.pow).then_inc(s.pow_done, 1)
            pipeline(pool, step, first, last, steady)

        @block.scalar
        def _(act):
            def step(t, p):
                u, q = t + 2, p
                v, r = t + 1, 1 - p
                if inside(u):
                    upto(act, s.qk_done, u)
                if inside(v):
                    upto(act, s.v_done, v)
                if inside(u):
                    upto(act, s.scores_done, u - 2, 2)
                    upto(act, s.kexp_ready, u - 2)
                    nc.scalar.activation(m.qT[q][:], QKV[:, 0:P], ACT.Identity, bias=bq)
                    nc.scalar.activation(m.kT[q][:], QKV[:, P:2 * P], ACT.Identity, bias=bk).then_inc(s.k_out, 1)
                if inside(v):
                    upto(act, s.pv_done, v - 2)
                    for hh in range(2):
                        src = QKV[64 * hh:64 * hh + 64, 2 * P:4 * P].rearrange("p (b c e d) -> p b c e d", b=2, c=CH, e=2)
                        dst = m.vexp[r][64 * hh:64 * hh + 64, :, :].rearrange("p b (c e d) -> p b c e d", c=CH, e=2)
                        out = nc.scalar.copy(dst[:, :, :, hh, 0:DH], src[:, :, :, hh, :])
                    out.then_inc(s.v_out, 1)
                if not L0 and inside(t):
                    for r2 in range(2):
                        act.wait_ge(s.pt_done, t * 2 + r2 + 1)
                        if r2 == 0:
                            upto(act, s.pv_done, t - 1)
                        nc.scalar.copy(m.PTs[:, r2 * F:(r2 + 1) * F], PT[r2][:]).then_inc(s.pt_out, 1)
                u, w = t + 3, t - lag
                if inside(w):
                    upto(act, s.oT_done, w)
                if inside(u):
                    upto(act, s.xT_done, u)
                if inside(w):
                    upto(act, s.out_done, w - 1)
                    nc.scalar.activation(m.oT[:], A[:, 0:P], ACT.Identity, bias=0.0 if bv is None else bv).then_inc(s.oT_ready, 1)
                if inside(u):
                    q = 1 - p
                    upto(act, s.qk_done, u - 2)
                    if L0:
                        nc.scalar.activation(m.xnT[q][:], A[:, P:2 * P], ACT.Identity, scale=m.g_pre, bias=m.b_pre)
                        nc.scalar.activation(m.cnT[q][:], A[:, 2 * P:3 * P], ACT.Identity, scale=m.g_pre,
                                             bias=m.b_pre).then_inc(s.xnT_ready, 1)
                    else:
                        nc.scalar.copy(m.xnT[q][:], A[:, P:2 * P]).then_inc(s.xnT_ready, 1)
                u, q = t + 1, 1 - p
                if inside(u):
                    for r in range(2):
                        act.wait_ge(s.sub_done, u * 2 + r + 1)
                        pr = m.probs[q][:, r * F:(r + 1) * F]
                        nc.scalar.activation(pr, pr, ACT.Exp, scale=scale).then_inc(s.exp_done, 1)
            pipeline(act, step, first, last, steady)

        @block.tensor
        def _(pe):
            def step(t, p):
                u, q = t + 2, p
                v, r = t + 1, 1 - p
                if inside(u):
                    upto(pe, s.xnT_ready, u)
                    arrived(pe, s.ctx_in, u, q)
                    upto(pe, s.k_out, u - 1)
                if inside(v):
                    upto(pe, s.v_out, v - 1)
                if inside(u):
                    nc.tensor.matmul(QKV[:, 0:P], wq, m.xnT[q][:], start=True, stop=True)
                    nc.tensor.matmul(QKV[:, P:2 * P], wk, m.cnT[q][:] if L0 else m.ctx_t[q][:], start=True,
                                     stop=True).then_inc(s.qk_done, 1)
                if inside(v):
                    for b in range(2):
                        for hh in range(2):
                            out = nc.tensor.matmul(QKV[64 * hh:64 * hh + 64, (2 + b) * P:(3 + b) * P],
                                                   m.ctx_t[r][:, b * S:(b + 1) * S], wv, start=True, stop=True)
                    out.then_inc(s.v_done, 1)
                if inside(t):
                    for r2 in range(2):
                        act_done = t * 2 + r2 + 1
                        pe.wait_ge(s.exp_done, act_done)
                        if r2 == 0:
                            upto(pe, s.raw_ready if L0 else s.o_ready, t - 1)
                        else:
                            upto(pe, s.x_done, t - 1 - lag)
                        for c4 in range(4):
                            cc = 4 * r2 + c4
                            out = nc.tensor.transpose(PT[r2][:, c4 * P:(c4 + 1) * P], m.probs[p][:, cc * P:(cc + 1) * P], m.ident)
                        out.then_inc(s.pt_done, 1)
                u, q = t + 1, 1 - p
                if inside(u):
                    settle(pe, (s.kexp_ready, u + 1), (s.sub_done, 2 * (u - 1)))
                    for r2 in range(2):
                        for b in range(2):
                            out = nc.tensor.matmul(m.S[q][64 * b:64 * b + 64, r2 * F:(r2 + 1) * F],
                                                   m.qT[q][64 * r2:64 * r2 + 64, S * b:S * b + S],
                                                   m.kexp[q][64 * r2:64 * r2 + 64, :, S * b:S * b + S], start=True, stop=True)
                        out.then_inc(s.scores_done, 1)
                w, u = t - lag, t + 3
                if inside(w):
                    upto(pe, s.o_ready, w)
                    upto(pe, s.oT_ready, w - 1)
                if inside(u):
                    upto(pe, s.xn_ready, u)
                    upto(pe, s.xnT_ready, u - 1)
                if inside(w):
                    nc.tensor.transpose(A[:, 0:P], m.os[(p + lag) % 2][:], m.ident).then_inc(s.oT_done, 1)
                if inside(u):
                    out = nc.tensor.transpose(A[:, P:2 * P], m.xn[1 - p][:], m.ident)
                    if L0:
                        out = nc.tensor.transpose(A[:, 2 * P:3 * P], m.cn[1 - p][:], m.ident)
                    out.then_inc(s.xT_done, 1)
                if inside(t):
                    upto(pe, s.pt_out, t, 2)
                    upto(pe, s.v_out, t)
                    for cc in range(CH):
                        for b in range(2):
                            out = nc.tensor.matmul(m.PT0[64 * b:64 * b + 64, cc * VW:(cc + 1) * VW],
                                                   m.PTs[:, cc * P + S * b:cc * P + S * b + S],
                                                   m.vexp[p][:, b, cc * VW:(cc + 1) * VW], start=True, stop=True)
                    out.then_inc(s.pv_done, 1)
                if inside(w):
                    upto(pe, s.oT_ready, w)
                    if not inside(t):
                        upto(pe, s.pt_out, T - 1, 2)
                    upto(pe, s.x_done, w - 1)
                    nc.tensor.matmul(m.PT1[:, 0:D], m.oT[:], wo, start=True, stop=True).then_inc(s.out_done, 1)
            pipeline(pe, step, first, last, steady)


def xattn0_tail(nc, m, tg):
    G = 4
    with sems(nc, "t0_", "gelu_done", "sum_done", "x_done") as s, nc.Block() as block:
        @block.scalar
        def _(act):
            for g in range(G):
                z = m.za[:, g * (T // G):(g + 1) * (T // G), :]
                nc.scalar.activation(z, z, ACT.Gelu).then_inc(s.gelu_done, 1)

        @block.vector
        def _(dve):
            for g in range(G):
                sl = slice(g * (T // G), (g + 1) * (T // G))
                dve.wait_ge(s.gelu_done, g + 1)
                nc.vector.tensor_tensor(m.za[:, sl, :], m.za[:, sl, :], m.ola[:, sl, :], ALU.add).then_inc(s.sum_done, 1)
                dve.wait_ge(s.sum_done, g + 1)
                nc.vector.scalar_tensor_tensor(m.x[:, sl, :], m.za[:, sl, :], tg, m.x[:, sl, :], ALU.mult, ALU.add).then_inc(s.x_done, 1)
                dve.wait_ge(s.x_done, g + 1)
                for t in range(sl.start, sl.stop):
                    nc.vector.bn_stats(m.bn6[:, t, :], m.x[:, t, :])


def quantize(nc, wait, done, src, scale, m, q):
    v, big = m.qv[:], m.qbig[:]
    done(nc.vector.tensor_scalar(v, src, scale, None, ALU.mult))
    wait()
    nc.vector.tensor_scalar(big, v, 448.0, -448.0, ALU.min, ALU.max)
    nc.vector.tensor_scalar(m.q8a[:], v, 16.0, -16.0, ALU.min, ALU.max, saturate=False)
    done(nc.vector.tensor_tensor(m.qsq[:], v, v, ALU.mult))
    wait()
    nc.vector.tensor_scalar(m.q8b[:], big, 0.5, None, ALU.mult, saturate=False)
    nc.vector.tensor_scalar(q, m.q8a[:], 0.5, None, ALU.mult)
    done(nc.vector.tensor_scalar(m.qover[:], m.qsq[:], 256.0, None, ALU.is_gt))
    wait()
    done(nc.vector.tensor_copy(big, m.q8b[:]))
    wait()
    done(nc.vector.copy_predicated(q, m.qover[:], big))
    wait()


def ffn0(nc, m, tg):
    steady = (2, 12)
    with sems(nc, "f0_", "chain", "xq_ready", "xT_done", "xT_ready", "y_done", "flag_done", "q_done", "x_chain", "y_read") as s, nc.Block() as block:
        @block.vector
        def _(dve):
            def step(t, p):
                u = t + 2
                if inside(u):
                    n = [0]

                    def done(ins):
                        n[0] += 1
                        ins.then_inc(s.chain, 1)

                    def wait():
                        settle(dve, (s.chain, u * 7 + n[0]))
                    done(nc.vector.tensor_scalar(m.xb[:], row(m.x, u), m.rstd[:, tile_of(u)], m.nmr[:, tile_of(u)], ALU.mult, ALU.add))
                    wait()
                    upto(dve, s.xT_done, u - 2)
                    quantize(nc, wait, done, m.xb[:], m.scales[:, 2:3], m, m.xn[p][:])
                    nan = m.nanf[:, tile_of(u)]
                    done(nc.vector.tensor_reduce(nan, m.qv[:], AX_X, ALU.max, apply_absolute_value=True))
                    wait()
                    nc.vector.tensor_scalar(nan, nan, 464.0, 3e38, ALU.is_gt, ALU.mult).then_inc(s.xq_ready, 1)
                    upto(dve, s.xq_ready, u)
                    nc.vector.tensor_scalar(nan, nan, 1e5, None, ALU.mult).then_inc(s.flag_done, 1)
                    upto(dve, s.flag_done, u)
                    nc.vector.tensor_tensor(nan, nan, nan, ALU.subtract).then_inc(s.q_done, 1)
                    assert n[0] == 7, n
                if inside(t):
                    upto(dve, s.y_done, t)
                    upto(dve, s.q_done, t)
                    nc.vector.tensor_scalar(m.yb[:], m.bankB[:, 0:D], m.scales[:, 3:4], m.nanf[:, tile_of(t)], ALU.mult, ALU.add).then_inc(s.y_read, 1)
                    upto(dve, s.y_read, t)
                    nc.vector.tensor_tensor(m.yb2[:], m.yb[:], m.bias0[:], ALU.add).then_inc(s.x_chain, 1)
                    dve.wait_ge(s.x_chain, 2 * t + 1)
                    nc.vector.scalar_tensor_tensor(row(m.x, t), m.yb2[:], tg, row(m.x, t), ALU.mult, ALU.add).then_inc(s.x_chain, 1)
                    dve.wait_ge(s.x_chain, 2 * t + 2)
                    nc.vector.bn_stats(row(m.bn6, t), row(m.x, t))
            pipeline(dve, step, -2, T - 1, steady)

        @block.scalar
        def _(act):
            def step(t, p):
                if inside(t + 1):
                    upto(act, s.xT_done, t + 1)
                    upto(act, s.y_done, t - 1)
                    nc.scalar.copy(m.xqT[1 - p][:], m.bankA[:, 0:P]).then_inc(s.xT_ready, 1)
            pipeline(act, step, -2, T - 1, steady)

        @block.tensor
        def _(pe):
            def step(t, p):
                if inside(t + 1):
                    upto(pe, s.q_done, t + 1)
                    upto(pe, s.xT_ready, t)
                    nc.tensor.transpose(m.bankA[:, 0:P], m.xn[1 - p][:], m.ident).then_inc(s.xT_done, 1)
                if inside(t):
                    upto(pe, s.xT_ready, t)
                    upto(pe, s.y_read, t - 1)
                    nc.tensor.matmul(m.bankB[:, 0:D], m.xqT[p][:], m.kq[:], start=True, stop=True).then_inc(s.y_done, 1)
            pipeline(pe, step, -2, T - 1, steady)


def linear_attention(nc, m, wg, wv, wo, wq, wk, bg, bv, bk, bq, bo):
    names = ["ctx_in*", "xn_ready", "xT_done", "xnT_ready", "k_done", "u_done", "q_done", "bias_done", "kv_ready", "q_ready", "ub_ready", "silu_done",
             "kv_done", "kvs_ready", "r_done", "z_done", "ua_ready", "uaT_done", "uaT_ready", "out_done", "x_chain"]
    steady = (2, 12)
    W = D + 1
    U, Q, KV, R, C, O = m.S[0][:, 0:F], m.S[0][:, F:2 * F], m.S[1][:, 0:F], m.S[1][:, F:2 * F], m.PT0, m.PT1
    with sems(nc, "l2_", *names) as s, nc.Block() as block:
        first, last = -3, T - 1

        @block.sync
        def _(sp):
            def step(t, p):
                u, q = t + 2, p
                if inside(u):
                    upto(sp, s.u_done, u - 2)
                    sp.dma_start(m.ctx_t[q][:], m.ctxT_dram[:, bass.ds(u * P, P)]).then_inc(s.ctx_in[q], 16)
            pipeline(sp, step, first, last, steady)

        @block.vector
        def _(dve):
            def step(t, p):
                u, q = t + 1, 1 - p
                if inside(u):
                    km = m.kmask[:, tile_of(u)]
                    upto(dve, s.u_done, u)
                    nc.vector.tensor_tensor(m.kb[:], U[:, D:D + D // 2], bk, ALU.add).then_inc(s.bias_done, 1)
                    nc.vector.tensor_tensor(m.vb[:], U[:, 2 * D:3 * D], bv, ALU.add).then_inc(s.bias_done, 1)
                    upto(dve, s.silu_done, u - 1)
                    nc.vector.tensor_tensor(m.ub[:], U[:, 0:D], bg, ALU.add).then_inc(s.ub_ready, 1)
                    dve.wait_ge(s.bias_done, 2 * u + 1)
                    upto(dve, s.kv_done, u - 2)
                    nc.vector.scalar_tensor_tensor(m.kk[q][:], m.kb[:], 0.0, m.kb[:], ALU.max, ALU.mult)
                    dve.wait_ge(s.bias_done, 2 * u + 2)
                    nc.vector.tensor_copy(m.va[q][:, D:W], km)
                    nc.vector.tensor_scalar(m.va[q][:, 0:D], m.vb[:], km, None, ALU.mult).then_inc(s.kv_ready, 1)
                if inside(t):
                    upto(dve, s.r_done, t)
                    nc.vector.tensor_scalar(m.zr[:], R[:, D:W], KV_EPS, None, ALU.add).then_inc(s.z_done, 1)
                    dve.wait_ge(s.z_done, 2 * t + 1)
                    nc.vector.reciprocal(m.zr[:], m.zr[:]).then_inc(s.z_done, 1)
                    dve.wait_ge(s.z_done, 2 * t + 2)
                    upto(dve, s.silu_done, t)
                    upto(dve, s.uaT_done, t - 2)
                    nc.vector.scalar_tensor_tensor(m.ua[p][:], R[:, 0:D], m.zr[:], m.us[p][:], ALU.mult, ALU.mult).then_inc(s.ua_ready, 1)
                if inside(u):
                    upto(dve, s.q_done, u)
                    nc.vector.tensor_scalar(m.qr[:], Q[:, 0:S], bq, 0.0, ALU.add, ALU.max).then_inc(s.q_ready, 1)
                    dve.wait_ge(s.q_ready, 2 * u + 1)
                    upto(dve, s.r_done, u - 2)
                    nc.vector.tensor_tensor(m.qq[q][:], m.qr[:], m.qr[:], ALU.mult).then_inc(s.q_ready, 1)
                    upto(dve, s.kv_done, u)
                    nc.vector.tensor_copy(m.kvs[q][:], KV[:, 0:W]).then_inc(s.kvs_ready, 1)
                if inside(t):
                    xt, wt = row(m.x, t), m.qgate[:, tile_of(t)]
                    upto(dve, s.out_done, t)
                    nc.vector.scalar_tensor_tensor(xt, O[:, 0:D], wt, xt, ALU.mult, ALU.add).then_inc(s.x_chain, 1)
                    dve.wait_ge(s.x_chain, 2 * t + 1)
                    nc.vector.scalar_tensor_tensor(xt, bo, wt, xt, ALU.mult, ALU.add).then_inc(s.x_chain, 1)
                    dve.wait_ge(s.x_chain, 2 * t + 2)
                    nc.vector.bn_stats(row(m.bn6, t), xt)
                u, q = t + 3, 1 - p
                if inside(u):
                    upto(dve, s.xT_done, u - 2)
                    nc.vector.tensor_scalar(m.xn[q][:], row(m.x, u), m.rstd[:, tile_of(u)], m.nmr[:, tile_of(u)],
                                            ALU.mult, ALU.add).then_inc(s.xn_ready, 1)
            pipeline(dve, step, first, last, steady)

        @block.scalar
        def _(act):
            def step(t, p):
                u, q = t + 1, 1 - p
                if inside(u):
                    upto(act, s.ub_ready, u)
                    upto(act, s.ua_ready, u - 2)
                    nc.scalar.activation(m.us[q][:], m.ub[:], ACT.Silu).then_inc(s.silu_done, 1)
                if inside(t + 2):
                    upto(act, s.xT_done, t + 2)
                    upto(act, s.q_done, t)
                    nc.scalar.copy(m.xnT[p][:], m.bankA[:, 0:P]).then_inc(s.xnT_ready, 1)
                if inside(t):
                    upto(act, s.uaT_done, t)
                    upto(act, s.out_done, t - 1)
                    nc.scalar.copy(m.oT[:], C[:, 0:P]).then_inc(s.uaT_ready, 1)
            pipeline(act, step, first, last, steady)

        @block.tensor
        def _(pe):
            def step(t, p):
                u, q = t + 1, 1 - p
                if inside(u):
                    arrived(pe, s.ctx_in, u, q)
                    upto(pe, s.xnT_ready, u)
                    upto(pe, s.ub_ready, u - 1)
                    upto(pe, s.kv_ready, u - 1)
                    nc.tensor.matmul(U[:, 0:D], m.xnT[q][:], wg, start=True, stop=True)
                    nc.tensor.matmul(U[:, 2 * D:3 * D], m.ctx_t[q][:], wv, start=True, stop=True)
                    nc.tensor.matmul(U[:, D:D + D // 2], m.ctx_t[q][:], wk, start=True, stop=True).then_inc(s.u_done, 1)
                    upto(pe, s.q_ready, u - 1, 2)
                    for b in range(2):
                        out = nc.tensor.matmul(Q[64 * b:64 * b + 64, 0:S], wq, m.xnT[q][:, S * b:S * b + S], start=True, stop=True)
                    out.then_inc(s.q_done, 1)
                if inside(t):
                    settle(pe, (s.q_ready, 2 * t + 2), (s.kvs_ready, t + 1), (s.ua_ready, t))
                    for b in range(2):
                        out = nc.tensor.matmul(R[64 * b:64 * b + 64, 0:W], m.qq[p][64 * b:64 * b + 64, :],
                                               m.kvs[p][64 * b:64 * b + 64, :], start=True, stop=True)
                    out.then_inc(s.r_done, 1)
                if inside(t + 2):
                    upto(pe, s.xn_ready, t + 2)
                    upto(pe, s.xnT_ready, t + 1)
                    nc.tensor.transpose(m.bankA[:, 0:P], m.xn[p][:], m.ident).then_inc(s.xT_done, 1)
                if inside(u):
                    settle(pe, (s.kv_ready, u + 1), (s.kvs_ready, u))
                    for b in range(2):
                        out = nc.tensor.matmul(KV[64 * b:64 * b + 64, 0:W], m.kk[q][64 * b:64 * b + 64, :],
                                               m.va[q][64 * b:64 * b + 64, :], start=True, stop=True)
                    out.then_inc(s.kv_done, 1)
                if inside(t):
                    upto(pe, s.ua_ready, t)
                    upto(pe, s.uaT_ready, t - 1)
                    nc.tensor.transpose(C[:, 0:P], m.ua[p][:], m.ident).then_inc(s.uaT_done, 1)
                    upto(pe, s.uaT_ready, t)
                    if not isinstance(t, int) or t >= 1:
                        pe.wait_ge(s.x_chain, 2 * t - 1)
                    nc.tensor.matmul(O[:, 0:D], m.oT[:], wo, start=True, stop=True).then_inc(s.out_done, 1)
            pipeline(pe, step, first, last, steady)


def router(nc, m, layer, wr):
    names = ["xn_ready", "xT_done", "xnT_ready", "lg_done", "lg_read", "soft", "exp_done", "pr_ready", "top_done", "idx_done", "out*"]
    steady = (2, 12)
    with sems(nc, f"r{layer}_", *names) as s, nc.Block() as block:
        first, last = -3, T - 1

        @block.sync
        def _(sp):
            def step(t, p):
                u, q = t + 2, p
                if inside(u):
                    upto(sp, s.xn_ready, u)
                    sp.dma_start(m.XN[bass.ds(u * P, P), :], m.xn[q][:]).then_inc(s.out[q], 16)
            pipeline(sp, step, first, last, steady)
            for q in range(2):
                sp.wait_ge(s.out[q], T // 2 * 16)

        @block.vector
        def _(dve):
            def step(t, p):
                if inside(t):
                    upto(dve, s.lg_done, t)
                    nc.vector.tensor_copy(m.lg[:], m.bankB[:, 0:E]).then_inc(s.lg_read, 1)
                    pr, ready = m.lg, (s.lg_read, t + 1)
                    if layer == 2:
                        upto(dve, s.lg_read, t)
                        nc.vector.tensor_reduce(m.lmax[:], m.lg[:], AX_X, ALU.max, negate=True).then_inc(s.soft, 1)
                        upto(dve, s.exp_done, t)
                        nc.vector.reciprocal(m.lsum[:], m.lsum[:]).then_inc(s.pr_ready, 1)
                        dve.wait_ge(s.pr_ready, 2 * t + 1)
                        nc.vector.tensor_scalar(m.lp[:], m.le[:], m.lsum[:], None, ALU.mult).then_inc(s.pr_ready, 1)
                        pr, ready = m.lp, (s.pr_ready, 2 * t + 2)
                    two_best(nc, m, dve, s, pr[:], t, ready)
                u, q = t + 3, 1 - p
                if inside(u):
                    upto(dve, s.xT_done, u - 2)
                    if isinstance(u, int):
                        if u >= 2:
                            dve.wait_ge(s.out[q], (u // 2) * 16)
                    else:
                        dve.wait_ge(s.out[q], (u - q) * 8)
                    nc.vector.tensor_scalar(m.xn[q][:], row(m.x, u), m.rstd[:, tile_of(u)], m.nmr[:, tile_of(u)],
                                            ALU.mult, ALU.add).then_inc(s.xn_ready, 1)
            pipeline(dve, step, first, last, steady)

        @block.scalar
        def _(act):
            def step(t, p):
                u, q = t + 1, 1 - p
                if inside(u):
                    upto(act, s.xT_done, u)
                    upto(act, s.lg_done, u - 2)
                    nc.scalar.copy(m.xnT[q][:], m.bankA[:, 0:P]).then_inc(s.xnT_ready, 1)
                if layer == 2 and inside(t):
                    upto(act, s.soft, t)
                    nc.scalar.activation(m.le[:], m.lg[:], ACT.Exp, bias=m.lmax[:], accum_out=m.lsum[:]).then_inc(s.exp_done, 1)
            pipeline(act, step, first, last, steady)

        @block.tensor
        def _(pe):
            def step(t, p):
                u, q = t + 1, 1 - p
                if inside(u):
                    upto(pe, s.xn_ready, u)
                    upto(pe, s.xnT_ready, u - 1)
                    nc.tensor.transpose(m.bankA[:, 0:P], m.xn[q][:], m.ident).then_inc(s.xT_done, 1)
                if inside(t):
                    upto(pe, s.xnT_ready, t)
                    upto(pe, s.lg_read, t - 1)
                    nc.tensor.matmul(m.bankB[:, 0:E], m.xnT[p][:], wr, start=True, stop=True).then_inc(s.lg_done, 1)
            pipeline(pe, step, first, last, steady)


def two_best(nc, m, dve, s, scores, t, ready):
    settle(dve, ready, (s.idx_done, t))
    nc.vector.max(m.top[:], scores).then_inc(s.top_done, 1)
    settle(dve, (s.top_done, t + 1))
    nc.vector.max_index(m.idx[:], m.top[:], scores).then_inc(s.idx_done, 1)
    nc.vector.tensor_copy(m.tv[:, :, tile_of(t)].rearrange("p a b -> p (a b)"), m.top[:, 0:2])
    upto(dve, s.idx_done, t)
    nc.vector.tensor_copy(m.ti[:, :, tile_of(t)].rearrange("p a b -> p (a b)"), m.idx[:, 0:2])


def dispatch(nc, m, layer, tg):
    J = 2 * T
    with sems(nc, f"d{layer}_", "chain", "marks_ready", "sums_done", "gap_ready", "exp_done", "hot_ready", "list_step", "list_done") as s, nc.Block() as block:
        @block.vector
        def _(dve):
            n = [0]

            def then(ins):
                n[0] += 1
                ins.then_inc(s.chain, 1)
                dve.wait_ge(s.chain, n[0])

            e_t = lambda ap: ap.unsqueeze(1).to_broadcast([P, E, T])
            t_e = lambda ap: ap.unsqueeze(2).to_broadcast([P, E, T])
            v0, v1, w0, w1 = m.tv[:, 0, :], m.tv[:, 1, :], m.wt[:, 0, :], m.wt[:, 1, :]
            if layer == 1:
                nc.vector.tensor_tensor(m.st_a[:], v1, v0, ALU.subtract).then_inc(s.gap_ready, 1)
            for k in range(2):
                then(nc.vector.tensor_tensor(m.hot[k][:], e_t(m.ti[:, k, :]), t_e(m.con["expert"]), ALU.is_equal))
            nc.vector.tensor_tensor(m.marks[:], m.hot[0][:], m.hot[1][:], ALU.add).then_inc(s.marks_ready, 1)
            if layer == 1:
                dve.wait_ge(s.exp_done, 1)
                then(nc.vector.tensor_scalar(m.st_c[:], m.st_b[:], 1.0, None, ALU.add))
                then(nc.vector.reciprocal(m.st_c[:], m.st_c[:]))
                then(nc.vector.tensor_scalar(w0, m.st_c[:], tg, None, ALU.mult))
                nc.vector.tensor_tensor(w1, w0, m.st_b[:], ALU.mult)
            elif layer == 2:
                nc.vector.tensor_scalar(m.wt[:], m.tv[:], tg, None, ALU.mult)
            else:
                then(nc.vector.tensor_tensor(m.st_c[:], v0, v1, ALU.add))
                then(nc.vector.reciprocal(m.st_c[:], m.st_c[:]))
                then(nc.vector.tensor_scalar(m.st_c[:], m.st_c[:], tg, None, ALU.mult))
                nc.vector.tensor_tensor(w0, v0, m.st_c[:], ALU.mult)
                nc.vector.tensor_tensor(w1, v1, m.st_c[:], ALU.mult)
            dve.wait_ge(s.sums_done, 2)
            flat = lambda tensor: tensor[:].rearrange("p e t -> p (e t)")
            then(nc.vector.tensor_copy(flat(m.tot), m.bankB[:, 0:P]))
            then(nc.vector.tensor_tensor_scan(flat(m.incl), m.con["keep"], flat(m.tot), 0.0, ALU.mult, ALU.add))
            then(nc.vector.tensor_tensor(m.pos[:], m.incl[:], m.tot[:], ALU.subtract))
            then(nc.vector.tensor_tensor(flat(m.pos), flat(m.pos), m.bankA[:, 0:P], ALU.add))
            count = m.incl[:, :, T - 1]
            then(nc.vector.tensor_tensor(m.tot[:], t_e(count), e_t(m.con["tile128"]), ALU.is_gt))
            then(nc.vector.tensor_reduce(m.nb[:], m.tot[:], AX_X, ALU.add))
            then(nc.vector.tensor_tensor_scan(m.cum[:], m.ones[:, 0:E], m.nb[:], 0.0, ALU.mult, ALU.add))
            then(nc.vector.tensor_tensor(m.base[:], m.cum[:], m.nb[:], ALU.subtract))
            then(nc.vector.tensor_scalar(m.base[:], m.base[:], float(P), None, ALU.mult))
            then(nc.vector.tensor_tensor(m.pos[:], m.pos[:], t_e(m.base[:]), ALU.add))
            for k in range(2):
                then(nc.vector.tensor_tensor(m.tot[:], m.hot[k][:], m.pos[:], ALU.mult))
                then(nc.vector.tensor_reduce(m.dest[:, k, :], m.tot[:].rearrange("p e t -> p t e"), AX_X, ALU.add))
                then(nc.vector.tensor_reduce(m.valid[:, k, :], m.hot[k][:].rearrange("p e t -> p t e"), AX_X, ALU.add))
            then(nc.vector.tensor_tensor(m.wt[:], m.wt[:], m.valid[:], ALU.mult))
            then(nc.vector.tensor_tensor(m.valid[:], m.valid[:], m.con["token"].unsqueeze(1).to_broadcast([P, 2, T]), ALU.mult))
            then(nc.vector.tensor_copy(m.desti[:], m.dest[:]))
            then(nc.vector.tensor_scalar(m.blki[:], m.desti[:], 7, None, ALU.logical_shift_right))
            then(nc.vector.tensor_copy(m.blk[:], m.blki[:]))
            then(nc.vector.scalar_tensor_tensor(m.slot[:], m.blk[:], -float(P), m.dest[:], ALU.mult, ALU.add))
            then(nc.vector.tensor_scalar(m.nbf[:], m.cum[:, E - 1:E], 3.0, 1.0, ALU.max, ALU.add))
            then(nc.vector.tensor_copy(m.nbi[:], m.nbf[:]))
            then(nc.vector.tensor_scalar(m.nbi[:], m.nbi[:], 1, 1, ALU.logical_shift_right, ALU.logical_shift_left))
            big = m.ebc[:]
            then(nc.vector.tensor_tensor(big, m.con["block"].unsqueeze(1).to_broadcast([P, E, NBX]),
                                         m.cum[:].unsqueeze(2).to_broadcast([P, E, NBX]), ALU.is_ge))
            then(nc.vector.tensor_reduce(m.ebf[:], big.rearrange("p e b -> p b e"), AX_X, ALU.add))
            then(nc.vector.tensor_scalar(m.eb[:], m.ebf[:], float(E - 1), None, ALU.min))

            fl = lambda tensor: tensor[:].rearrange("p k t -> p (k t)")

            def step(j, q):
                upto(dve, s.list_step, j - 2)
                col = lambda tensor: fl(tensor)[:, tile_of(j)]
                nc.vector.tensor_scalar(m.hot_slot[q][:], m.con["slot"], col(m.slot), None, ALU.is_equal)
                nc.vector.tensor_scalar(m.hot_blk[q][:], m.con["block"], col(m.blk), col(m.valid), ALU.is_equal,
                                        ALU.mult).then_inc(s.hot_ready, 1)
            pipeline(dve, step, 0, J - 1, (2, J - 2))
            dve.wait_ge(s.list_done, 1)
            nc.vector.tensor_copy(m.tok[:], m.PT0[:, 0:NBX])

        @block.scalar
        def _(act):
            if layer == 1:
                act.wait_ge(s.gap_ready, 1)
                nc.scalar.activation(m.st_b[:], m.st_a[:], ACT.Exp).then_inc(s.exp_done, 1)

        @block.tensor
        def _(pe):
            pe.wait_ge(s.marks_ready, 1)
            marks = m.marks[:].rearrange("p e t -> p (e t)")
            nc.tensor.matmul(m.bankA[:, 0:P], m.con["upper"], marks, start=True, stop=True).then_inc(s.sums_done, 1)
            nc.tensor.matmul(m.bankB[:, 0:P], m.ones[:], marks, start=True, stop=True).then_inc(s.sums_done, 1)

            def step(j, q):
                upto(pe, s.hot_ready, j)
                first, last = isinstance(j, int) and j == 0, isinstance(j, int) and j == J - 1
                out = nc.tensor.matmul(m.PT0[:, 0:NBX], m.hot_slot[q][:], m.hot_blk[q][:], start=first, stop=last,
                                       skip_group_check=True)
                out.then_inc(s.list_done if last else s.list_step, 1)
            pipeline(pe, step, 0, J - 1, (2, J - 2))


def mlp(nc, m, layer, W, gate=False, b1=None, b2=None):
    selu = layer == 3
    biased = b1 is not None
    func = {1: ACT.Gelu, 2: ACT.Gelu_apprx_tanh, 3: ACT.Exp}[layer]
    names = ["idx_ready", "xn_ready", "xT_done", "xgT_ready", "h_done", "z_ready", "z2_ready", "h_ready", "selu_ready",
             "hT_done", "hT_ready", "y_done", "y_ready", "top_done", "idx_done", "out*", "rows_out*"]
    H_, HT, Y = [m.S[i][:, 0:F] for i in range(2)], [m.S[i][:, F:2 * F] for i in range(2)], (m.PT0, m.PT1)
    live = inside if gate else (lambda u: not isinstance(u, int) or u >= 0)
    xg_in = m.gather_sems[layer, "xg_in"]
    with sems(nc, f"{'g' if gate else 'm'}{layer}_", *names) as s, nc.Block() as block:
        def run(eng, step):
            if gate:
                return pipeline(eng, step, -4, T - 1, (2, 10))
            blocks = eng.value_load(m.nbi[0:1, 0:1], min_val=4, max_val=NB)
            for b in range(-4, 2):
                step(b, b % 2)
            with eng.Fori(2, blocks, 2) as i:
                step(i, 0)
                step(i + 1, 1)
            return blocks

        def expert(eng, b):
            return eng.value_load(m.eb[0:1, tile_of(b)], min_val=0, max_val=E - 1)

        @block.sync
        def _(sp):
            def step(b, p):
                if gate:
                    u, q = b + 4, p
                    if inside(u):
                        upto(sp, s.xn_ready, u)
                        sp.dma_start(m.XN[bass.ds(u * P, P), :], m.xn[q][:]).then_inc(s.rows_out[q], 16)
                elif live(b):
                    upto(sp, s.y_ready, b)
                    sp.dma_start(m.YS[bass.ds(b * P, P), :], m.ys[p][:]).then_inc(s.out[p], 16)
            blocks = run(sp, step)
            if gate:
                for q in range(2):
                    sp.wait_ge(s.rows_out[q], T // 2 * 16)
            else:
                settle(sp, (s.out[0], blocks * 8), (s.out[1], blocks * 8))

        if not gate:
            @block.gpsimd
            def _(pool):
                def step(b, p):
                    u, q = b + 4, p
                    settle(pool, (s.idx_ready, u + 1), (s.xT_done, u - 1))
                    nc.gpsimd.indirect_dma_start(m.xg[q][:], None, m.XN, bass.IndirectOffsetOnAxis(ap=m.idx_t[q][:], axis=0))\
                        .then_inc(xg_in[q], 16)
                run(pool, step)

        @block.vector
        def _(dve):
            def step(b, p):
                u, q = b + 4, p
                if not gate:
                    if isinstance(u, int):
                        if u >= 2:
                            arrived(dve, xg_in, u - 2, q)
                    else:
                        arrived(dve, xg_in, u - 2, q)
                    nc.vector.tensor_copy(m.idx_t[q][:], m.tok[:, tile_of(u)]).then_inc(s.idx_ready, 1)
                elif inside(u):
                    upto(dve, s.xT_done, u - 2)
                    if isinstance(u, int):
                        if u >= 2:
                            dve.wait_ge(s.rows_out[q], (u // 2) * 16)
                    else:
                        dve.wait_ge(s.rows_out[q], (u - q) * 8)
                    nc.vector.tensor_scalar(m.xn[q][:], row(m.x, u), m.rstd[:, tile_of(u)], m.nmr[:, tile_of(u)],
                                            ALU.mult, ALU.add).then_inc(s.xn_ready, 1)
                u, q = b + 2, p
                if live(u) and biased:
                    bias = b1[:, 0:F] if gate else b1[:, bass.ds(expert(dve, u) * F, F)]
                    upto(dve, s.h_done, u)
                    upto(dve, s.hT_done if selu else s.h_ready, u - 2)
                    if selu:
                        nc.vector.scalar_tensor_tensor(m.z[q][:], H_[q], SELU_SCALE, bias, ALU.mult, ALU.add).then_inc(s.z_ready, 1)
                        upto(dve, s.h_ready, u)
                        nc.vector.tensor_scalar(m.h[q][:], m.h[q][:], SELU_SCALE * SELU_ALPHA, -SELU_SCALE * SELU_ALPHA,
                                                ALU.min, ALU.add).then_inc(s.z2_ready, 1)
                        upto(dve, s.z2_ready, u)
                        nc.vector.scalar_tensor_tensor(m.h[q][:], m.z[q][:], 0.0, m.h[q][:], ALU.max, ALU.add).then_inc(s.selu_ready, 1)
                    else:
                        nc.vector.tensor_tensor(m.z[q][:], H_[q], bias, ALU.add).then_inc(s.z_ready, 1)
                if live(b):
                    upto(dve, s.y_done, b)
                    if gate:
                        nc.vector.tensor_tensor(m.lg128[:], Y[p][:, 0:D], b2, ALU.add).then_inc(s.y_ready, 1)
                        two_best(nc, m, dve, s, m.lg128[:], b, (s.y_ready, b + 1))
                    else:
                        if isinstance(b, int):
                            if b >= 2:
                                dve.wait_ge(s.out[p], (b // 2) * 16)
                        else:
                            dve.wait_ge(s.out[p], (b - p) * 8)
                        if b2 is None:
                            nc.vector.tensor_copy(m.ys[p][:], Y[p][:, 0:D]).then_inc(s.y_ready, 1)
                        else:
                            nc.vector.tensor_tensor(m.ys[p][:], Y[p][:, 0:D], b2[:, bass.ds(expert(dve, b) * D, D)],
                                                    ALU.add).then_inc(s.y_ready, 1)
            run(dve, step)

        @block.scalar
        def _(act):
            def step(b, p):
                if live(b):
                    upto(act, s.hT_done, b)
                    upto(act, s.y_done, b - 1)
                    nc.scalar.copy(m.hT[:], HT[p]).then_inc(s.hT_ready, 1)
                u, q = b + 2, p
                if live(u):
                    upto(act, s.z_ready if biased else s.h_done, u)
                    upto(act, s.hT_done, u - 2)
                    if selu:
                        nc.scalar.activation(m.h[q][:], m.z[q][:], func, scale=1.0 / SELU_SCALE, bias=m.ln_alpha[:, 0:1]).then_inc(s.h_ready, 1)
                    else:
                        nc.scalar.activation(m.h[q][:], m.z[q][:] if biased else H_[q], func).then_inc(s.h_ready, 1)
                u, q = b + 3, 1 - p
                if live(u):
                    upto(act, s.xT_done, u)
                    upto(act, s.h_done, u - 2)
                    nc.scalar.copy(m.xgT[q][:], m.bankA[:, 0:P]).then_inc(s.xgT_ready, 1)
            run(act, step)

        @block.tensor
        def _(pe):
            def step(b, p):
                if live(b):
                    upto(pe, s.selu_ready if selu else s.h_ready, b)
                    upto(pe, s.hT_ready, b - 2)
                    for k in range(FC):
                        out = nc.tensor.transpose(HT[p][:, k * P:(k + 1) * P], m.h[p][:, k * P:(k + 1) * P], m.ident)
                    out.then_inc(s.hT_done, 1)
                u, q = b + 2, p
                if live(u):
                    w1 = W[0] if gate else W[:, 0, bass.ds(expert(pe, u) * F, F)]
                    upto(pe, s.xgT_ready, u)
                    upto(pe, s.z_ready if biased else s.h_ready, u - 2)
                    nc.tensor.matmul(H_[q], m.xgT[q][:], w1, start=True, stop=True).then_inc(s.h_done, 1)
                u, q = b + 3, 1 - p
                if live(u):
                    if gate:
                        upto(pe, s.xn_ready, u)
                    else:
                        arrived(pe, xg_in, u, q)
                    upto(pe, s.xgT_ready, u - 1)
                    nc.tensor.transpose(m.bankA[:, 0:P], (m.xn if gate else m.xg)[q][:], m.ident).then_inc(s.xT_done, 1)
                if live(b):
                    e = None if gate else expert(pe, b)
                    upto(pe, s.hT_ready, b)
                    upto(pe, s.y_ready, b - 2)
                    for k in range(FC):
                        w2 = W[1][:, k * D:(k + 1) * D] if gate else W[:, 1, bass.ds(e * F + k * D, D)]
                        out = nc.tensor.matmul(Y[p][:, 0:D], m.hT[:, k * P:(k + 1) * P], w2, start=(k == 0), stop=(k == FC - 1))
                    out.then_inc(s.y_done, 1)
            run(pe, step)


def combine(nc, m, layer):
    steady = (2, 12)
    y0_in, y1_in = m.gather_sems[layer, "y0_in"], m.gather_sems[layer, "y1_in"]
    with sems(nc, f"k{layer}_", "idx_ready", "x_chain") as s, nc.Block() as block:
        @block.vector
        def _(dve):
            def step(t, p):
                u = t + 2
                if inside(u):
                    if not isinstance(u, int) or u >= 2:
                        arrived(dve, y0_in, u - 2, p)
                        arrived(dve, y1_in, u - 2, p)
                    nc.vector.tensor_copy(m.cidx[p][:], m.desti[:, :, tile_of(u)].rearrange("p a b -> p (a b)")).then_inc(s.idx_ready, 1)
                if inside(t):
                    xt = row(m.x, t)
                    for k, arr in enumerate((y0_in, y1_in)):
                        arrived(dve, arr, t, p)
                        if k:
                            dve.wait_ge(s.x_chain, 2 * t + 1)
                        nc.vector.scalar_tensor_tensor(xt, m.yg[k][p][:], m.wt[:, k, tile_of(t)], xt, ALU.mult, ALU.add).then_inc(s.x_chain, 1)
                    dve.wait_ge(s.x_chain, 2 * t + 2)
                    nc.vector.bn_stats(row(m.bn6, t), xt)
            pipeline(dve, step, -2, T - 1, steady)

        @block.gpsimd
        def _(pool):
            def step(t, p):
                u = t + 2
                if inside(u):
                    settle(pool, (s.idx_ready, u + 1), (s.x_chain, 2 * (u - 1)))
                    for k, arr in enumerate((y0_in, y1_in)):
                        nc.gpsimd.indirect_dma_start(m.yg[k][p][:], None, m.YS, bass.IndirectOffsetOnAxis(ap=m.cidx[p][:, k:k + 1], axis=0))\
                            .then_inc(arr[p], 16)
            pipeline(pool, step, -2, T - 1, steady)


W_NAMES = ["q0", "k0", "v0", "o0", "q1", "k1", "v1", "o1", "g2", "v2", "o2", "qk2", "q3", "k3", "v3", "o3"]
COL_NAMES = ["g_pre", "b_pre", "bq2", "bq3", "bk3", "bv3"]
ROW_SIZES = {"g_ln": D, "b_ln": D, "bo1": D, "bg2": D, "bv2": D, "bk2": D // 2, "bo2": D, "bo3": D,
             "gate_bi": F, "gate_bo": D}
ROW_AT = {}
_at = 0
for _n, _k in ROW_SIZES.items():
    ROW_AT[_n] = (_at, _at + _k)
    _at += _k
ROWS = _at
C_SIZES = {"ident": P, "head_mask": HALF, "upper": P, "expert": E, "tile128": T, "block": NBX, "slot": P,
           "token": T, "keep": P}
C_AT = {}
_at = 0
for _n, _k in C_SIZES.items():
    C_AT[_n] = (_at, _at + _k)
    _at += _k
CONSTS = _at


def program(nc, a, out, stop=99):
    with ExitStack() as c:
        def sb(name, shape, dt=F32):
            return c.enter_context(nc.sbuf_tensor(name, shape, dt))

        m = Memory()
        numbers = iter(GATHER_NUMBERS)
        gather_sems = {(layer, n): [c.enter_context(nc.semaphore(f"{n}{layer}_{i}", num=next(numbers))) for i in range(2)]
                       for layer in (1, 2, 3) for n in ("xg_in", "y0_in", "y1_in")}
        m.gather_sems = gather_sems
        m.x, m.ctx = sb("x", [P, T, D]), sb("ctx", [P, T, D])
        m.wts = sb("wts", [P, len(W_NAMES), P])
        m.cols = sb("cols", [P, len(COL_NAMES)])
        m.rows = sb("rows", [P, ROWS])
        m.consts = sb("consts", [P, CONSTS])
        m.gates = sb("gates", [P, 8])
        m.tg = sb("tg", [P, 8])
        m.bn6, m.cbn6 = sb("bn6", [P, T, 6]), sb("cbn6", [P, T, 6])
        m.rstd, m.nmr, m.crstd, m.cnmr, m.st_a, m.st_b, m.st_c, m.st_d, m.st_e, m.minus_half = (
            sb(n, [P, T]) for n in ("rstd", "nmr", "crstd", "cnmr", "st_a", "st_b", "st_c", "st_d", "st_e", "minus_half"))
        two = lambda n, shape, dt=F32: [sb(f"{n}{i}", shape, dt) for i in range(2)]
        m.ctx_t, m.xn, m.cn, m.xnT, m.cnT = (two(n, [P, P]) for n in ("ctx_t", "xn", "cn", "xnT", "cnT"))
        m.qT, m.kT, m.os, m.raw = (two(n, [P, P]) for n in ("qT", "kT", "os", "raw"))
        m.kexp = two("kexp", [P, HALF, P])
        m.vexp = two("vexp", [P, 2, CH * VW])
        m.probs = two("probs", [P, 2 * F])
        m.PTs, m.oT = sb("PTs", [P, 2 * F]), sb("oT", [P, P])
        m.rowmax = two("rowmax", [P, H])
        m.rden = sb("rden", [P, H])
        m.obn, m.omv, m.ovar, m.orstd = sb("obn", [P, 6]), two("omv", [P, 2]), two("ovar", [P, 1]), two("orstd", [P, 1])
        m.mask_t, m.pred = two("mask_t", [P, S], I32), two("pred", [P, S], I32)
        m.negs = sb("negs", [P, S])
        m.xb, m.yb, m.yb2 = sb("xb", [P, D], BF16), sb("yb", [P, D], BF16), sb("yb2", [P, D], BF16)
        m.qbig, m.qsq = sb("qbig", [P, D]), sb("qsq", [P, D])
        m.qv, m.q8a, m.q8b, m.qover = sb("qv", [P, D]), sb("q8a", [P, D], FP8), sb("q8b", [P, D], FP8), sb("qover", [P, D], I32)
        m.nanf, m.xqT = sb("nanf", [P, T]), two("xqT", [P, P], BF16)
        m.kraw, m.kq, m.bias0 = sb("kraw", [P, D], BF16), sb("kq", [P, D], BF16), sb("bias0", [P, D], BF16)
        m.scales, m.rks = sb("scales", [P, 4]), sb("rks", [P, 1])
        m.kmask8, m.kmask, m.qgate = sb("kmask8", [P, T], U8), sb("kmask", [P, T]), sb("qgate", [P, T])
        m.kb, m.vb, m.ub, m.zr, m.qr = sb("kb", [P, D // 2]), sb("vb", [P, D]), sb("ub", [P, D]), sb("zr", [P, 1]), sb("qr", [P, S])
        m.kk, m.va, m.us, m.ua, m.qq, m.kvs = (two(n, [P, k]) for n, k in (("kk", D // 2), ("va", D + 1), ("us", D), ("ua", D), ("qq", S), ("kvs", D + 1)))
        m.lg, m.lp, m.le, m.lmax, m.lsum = sb("lg", [P, E]), sb("lp", [P, E]), sb("le", [P, E]), sb("lmax", [P, 1]), sb("lsum", [P, 1])
        m.lg128 = sb("lg128", [P, D])
        m.top, m.idx = sb("top", [P, E]), sb("idx", [P, E], U32)
        m.tv, m.ti, m.wt = sb("tv", [P, 2, T]), sb("ti", [P, 2, T]), sb("wt", [P, 2, T])
        m.hot = two("hot", [P, E, T])
        m.marks, m.tot, m.incl, m.pos = (sb(n, [P, E, T]) for n in ("marks", "tot", "incl", "pos"))
        m.nb, m.cum, m.base = sb("nb", [P, E]), sb("cum", [P, E]), sb("base", [P, E])
        m.dest, m.valid, m.blk, m.slot = (sb(n, [P, 2, T]) for n in ("dest", "valid", "blk", "slot_of"))
        m.desti, m.blki = sb("desti", [P, 2, T], I32), sb("blki", [P, 2, T], I32)
        m.nbf, m.nbi = sb("nbf", [P, 1]), sb("nbi", [P, 1], I32)
        m.ebc, m.ebf, m.eb, m.tok = sb("ebc", [P, E, NBX]), sb("ebf", [P, NBX]), sb("eb", [P, NBX], I32), sb("tok", [P, NBX], I32)
        m.hot_slot, m.hot_blk = two("hot_slot", [P, P], F16), two("hot_blk", [P, NBX], F16)
        m.ones, m.ln_alpha = sb("ones", [P, P]), sb("ln_alpha", [P, 1])
        m.xg, m.xgT, m.ys, m.idx_t = two("xg", [P, D]), two("xgT", [P, P]), two("ys", [P, D]), two("idx_t", [P, 1], I32)
        m.z, m.h = [pr[:, 0:F] for pr in m.probs], [pr[:, F:2 * F] for pr in m.probs]
        m.hT = m.PTs[:, 0:F]
        m.yg = [two("yg0", [P, D]), two("yg1", [P, D])]
        m.cidx = two("cidx", [P, 2], I32)
        m.router_w = sb("router_w", [P, 2, E])
        m.gate_w = sb("gate_w", [P, 2, F])
        m.b1, m.b2 = sb("b1", [P, E * F]), sb("b2", [P, E * D])
        m.XN = nc.dram_tensor("XN", [N, D], F32, kind="Internal").ap()
        m.YS = nc.dram_tensor("YS", [(NB + 2) * P, D], F32, kind="Internal").ap()
        m.WA, m.WB = sb("WA", [P, 2, E * F]), sb("WB", [P, 2, E * F])
        m.za = m.WB[:, 0, 0:T * D].rearrange("p (t d) -> p t d", d=D)
        m.ola = m.WB[:, 1, 0:T * D].rearrange("p (t d) -> p t d", d=D)
        m.S = [c.enter_context(nc.psum_tensor(f"S{i}", [P, 2 * F], F32)) for i in range(2)]
        m.PT0, m.PT1, m.bankA, m.bankB = (c.enter_context(nc.psum_tensor(n, [P, F], F32)) for n in ("PT0", "PT1", "bankA", "bankB"))
        m.ctxT_dram, m.mask_dram = a["ctxT"], a["mask"]
        w = {n: m.wts[:, i, :] for i, n in enumerate(W_NAMES)}
        col = {n: m.cols[:, i:i + 1] for i, n in enumerate(COL_NAMES)}
        rowv = {n: m.rows[:, i:j] for n, (i, j) in ROW_AT.items()}
        con = {n: m.consts[:, i:j] for n, (i, j) in C_AT.items()}
        m.con = con
        m.ident, m.head_mask = con["ident"], con["head_mask"]
        m.g_pre, m.b_pre, m.g_ln, m.b_ln = col["g_pre"], col["b_pre"], rowv["g_ln"], rowv["b_ln"]
        tg = lambda i: m.tg[:, i:i + 1]

        with sems(nc, "s_", "x_in", "ctx_in", "w_in", "small_in", "zeroed", "zero_ready", "ys_out", "ready", "chain") as s, nc.Block() as block:
            @block.sync
            def _(sp):
                sp.dma_start(m.x[:], a["x"].rearrange("(t p) d -> p t d", p=P)).then_inc(s.x_in, 16)
                sp.dma_start(m.ctx[:], a["ctx"].rearrange("(t p) d -> p t d", p=P)).then_inc(s.ctx_in, 16)
                sp.dma_start(m.wts[:].rearrange("p a b -> p (a b)"), a["wts"]).then_inc(s.w_in, 16)
                sp.dma_start(m.WA[:].rearrange("p a b -> p (a b)"), a["moe1"]).then_inc(s.w_in, 16)
                sp.dma_start(m.gate_w[:].rearrange("p a b -> p (a b)"), a["gate_w"]).then_inc(s.w_in, 16)
                sp.dma_start(m.router_w[:].rearrange("p a b -> p (a b)"), a["router_w"]).then_inc(s.w_in, 16)
                sp.wait_ge(s.zero_ready, 1)
                sp.dma_start(m.YS.rearrange("(b p) d -> p b d", p=P),
                             m.xg[0][:].unsqueeze(1).to_broadcast([P, NB + 2, D])).then_inc(s.ys_out, 16)
                sp.wait_ge(s.w_in, 64)
                sp.wait_ge(s.ys_out, 16)

            @block.scalar
            def _(act):
                act.dma_start(m.gates[:], a["gates"].partition_broadcast(P)).then_inc(s.small_in, 16)
                act.dma_start(m.cols[:], a["cols"]).then_inc(s.small_in, 16)
                act.dma_start(m.rows[:], a["rows"].partition_broadcast(P)).then_inc(s.small_in, 16)
                act.dma_start(m.consts[:], a["consts"]).then_inc(s.small_in, 16)
                act.dma_start(m.kraw[:], a["kernel0"]).then_inc(s.small_in, 16)
                act.dma_start(m.bias0[:], a["bias0"].partition_broadcast(P)).then_inc(s.small_in, 16)
                act.dma_start(m.scales[:, 0:2], a["scales"].partition_broadcast(P)).then_inc(s.small_in, 16)
                act.dma_start(m.kmask8[:], a["kmask"]).then_inc(s.small_in, 16)
                act.wait_ge(s.small_in, 128)
                nc.scalar.activation(m.tg[:], m.gates[:], ACT.Tanh).then_inc(s.ready, 1)

            @block.gpsimd
            def _(pool):
                nc.gpsimd.memset(m.xg[0][:], 0.0).then_inc(s.zero_ready, 1)
                nc.gpsimd.memset(m.minus_half[:], -0.5)
                nc.gpsimd.memset(m.ones[:], 1.0)
                nc.gpsimd.memset(m.ln_alpha[:], math.log(SELU_SCALE * SELU_ALPHA))
                nc.gpsimd.memset(m.negs[:], NEG * DH ** 0.5)
                for i in range(2):
                    nc.gpsimd.memset(m.vexp[i][:], 0.0).then_inc(s.zeroed, 1)
                pool.wait_ge(s.zeroed, 2)
                for i in range(2):
                    v = m.vexp[i][:].rearrange("p b (c e d) -> p b c e d", c=CH, e=2)
                    for hh in range(2):
                        nc.gpsimd.memset(v[64 * hh:64 * hh + 64, :, :, hh, DH:DH + 1], 1.0)

            @block.vector
            def _(dve):
                dve.wait_ge(s.x_in, 16)
                for t in range(T):
                    nc.vector.bn_stats(m.bn6[:, t, :], m.x[:, t, :])
                dve.wait_ge(s.ctx_in, 16)
                for t in range(T):
                    nc.vector.bn_stats(m.cbn6[:, t, :], m.ctx[:, t, :])
                dve.wait_ge(s.ready, 1)
                for i, n in ((1, "bo1"), (3, "bo3")):
                    nc.vector.tensor_scalar(rowv[n], rowv[n], tg(i), None, ALU.mult)
                nc.vector.tensor_scalar(rowv["gate_bi"], rowv["gate_bi"], SELU_SCALE, None, ALU.mult)
                count = [0]

                def done(ins):
                    count[0] += 1
                    ins.then_inc(s.chain, 1)

                def wait():
                    dve.wait_ge(s.chain, count[0])
                done(nc.vector.tensor_copy(m.kmask[:], m.kmask8[:]))
                wait()
                nc.vector.tensor_scalar(m.qgate[:], m.kmask[:], tg(2), None, ALU.mult)
                done(nc.vector.reciprocal(m.scales[:, 2:3], m.scales[:, 0:1]))
                done(nc.vector.reciprocal(m.rks[:], m.scales[:, 1:2]))
                done(nc.vector.scalar_tensor_tensor(m.scales[:, 3:4], m.scales[:, 0:1], 4.0, m.scales[:, 1:2], ALU.mult, ALU.mult))
                wait()
                quantize(nc, wait, done, m.kraw[:], m.rks[:], m, m.xn[0][:])
                done(nc.vector.tensor_scalar(m.xn[1][:], m.qsq[:], 464.0 ** 2, None, ALU.is_gt))
                wait()
                done(nc.vector.tensor_scalar(m.xn[1][:], m.xn[1][:], 3e38, 1e5, ALU.mult, ALU.mult))
                wait()
                done(nc.vector.tensor_tensor(m.xn[1][:], m.xn[1][:], m.xn[1][:], ALU.subtract))
                wait()
                nc.vector.tensor_tensor(m.kq[:], m.xn[0][:], m.xn[1][:], ALU.add)

        batch_stats(nc, m, "c0_", m.cbn6, m.crstd, m.cnmr)
        batch_stats(nc, m, "x0_", m.bn6, m.rstd, m.nmr, double=True)
        attention(nc, m, 0, w["q0"], w["k0"], w["v0"], w["o0"])
        xattn0_tail(nc, m, tg(0))

        def finish():
            with sems(nc, "e_", "out") as s, nc.Block() as block:
                @block.sync
                def _(sp):
                    sp.dma_start(out.rearrange("(t p) d -> p t d", p=P), m.x[:]).then_inc(s.out, 16)
                    sp.wait_ge(s.out, 16)

        def load(name, pairs, scale_b1=False):
            with sems(nc, name, "w_in", "ready") as s, nc.Block() as block:
                sem = s.w_in

                @block.sync
                def _(sp):
                    for dst, src in pairs:
                        sp.dma_start(dst, src).then_inc(sem, 16)
                    sp.wait_ge(sem, 16 * len(pairs))

                @block.vector
                def _(dve):
                    if scale_b1:
                        dve.wait_ge(sem, 16 * len(pairs))
                        nc.vector.tensor_scalar(m.b1[:], m.b1[:], SELU_SCALE, None, ALU.mult)
        if stop == 0:
            return finish()
        batch_stats(nc, m, "x1_", m.bn6, m.rstd, m.nmr)
        ffn0(nc, m, tg(4))
        if stop == 1:
            return finish()
        batch_stats(nc, m, "x2_", m.bn6, m.rstd, m.nmr)
        attention(nc, m, 1, w["q1"], w["k1"], w["v1"], w["o1"], tg=tg(1), out_bias=rowv["bo1"])
        if stop == 2:
            return finish()
        batch_stats(nc, m, "x3_", m.bn6, m.rstd, m.nmr)
        router(nc, m, 1, m.router_w[:, 0, :])
        dispatch(nc, m, 1, tg(5))
        mlp(nc, m, 1, m.WA)
        combine(nc, m, 1)
        if stop == 3:
            return finish()
        load("w2_", [(m.WB[:].rearrange("p a b -> p (a b)"), a["moe2"]), (m.b1[:], a["b1_2"].partition_broadcast(P)),
                     (m.b2[:], a["b2_2"].partition_broadcast(P))])
        batch_stats(nc, m, "x4_", m.bn6, m.rstd, m.nmr)
        linear_attention(nc, m, w["g2"], w["v2"], w["o2"], w["qk2"][:, 0:64], w["qk2"][:, 64:128],
                         rowv["bg2"], rowv["bv2"], rowv["bk2"], col["bq2"], rowv["bo2"])
        if stop == 4:
            return finish()
        batch_stats(nc, m, "x5_", m.bn6, m.rstd, m.nmr)
        router(nc, m, 2, m.router_w[:, 1, :])
        dispatch(nc, m, 2, tg(6))
        mlp(nc, m, 2, m.WB, b1=m.b1, b2=m.b2)
        combine(nc, m, 2)
        if stop == 5:
            return finish()
        load("w3_", [(m.WA[:].rearrange("p a b -> p (a b)"), a["moe3"]), (m.b1[:], a["b1_3"].partition_broadcast(P)),
                     (m.b2[:], a["b2_3"].partition_broadcast(P))], scale_b1=True)
        batch_stats(nc, m, "x6_", m.bn6, m.rstd, m.nmr)
        attention(nc, m, 3, w["q3"], w["k3"], w["v3"], w["o3"], bq=col["bq3"], bk=col["bk3"], bv=col["bv3"],
                  tg=tg(3), out_bias=rowv["bo3"])
        if stop == 6:
            return finish()
        batch_stats(nc, m, "x7_", m.bn6, m.rstd, m.nmr)
        mlp(nc, m, 3, [m.gate_w[:, 0, :], m.gate_w[:, 1, :]], gate=True, b1=rowv["gate_bi"], b2=rowv["gate_bo"])
        dispatch(nc, m, 3, tg(7))
        mlp(nc, m, 3, m.WA, b1=m.b1, b2=m.b2)
        combine(nc, m, 3)
        finish()


def layouts(i):
    import numpy as np
    i = {k: np.asarray(v) for k, v in i.items()}
    f = np.float32
    x, ctx = i["x"].reshape(N, D), i["ctx_1024"].reshape(N, D)
    wq2k2 = np.concatenate([i["L2_xattn_Wq"].T, i["L2_xattn_Wk"].T], axis=1)
    w = {"q0": i["L0_xattn_Wq"].T, "k0": i["L0_xattn_Wk"].T, "v0": i["L0_xattn_Wv"].T, "o0": i["L0_xattn_Wo"].T,
         "q1": i["L1_xattn_W_q"].T, "k1": i["L1_xattn_W_k"].T, "v1": i["L1_xattn_W_v"].T, "o1": i["L1_xattn_W_o"].T,
         "g2": i["L2_xattn_Wg"].T, "v2": i["L2_xattn_Wv"].T, "o2": i["L2_xattn_Wo"].T, "qk2": wq2k2,
         "q3": i["L3_xattn_wq_w"].T, "k3": i["L3_xattn_wk_w"].T, "v3": i["L3_xattn_wv_w"].T, "o3": i["L3_xattn_wo_w"].T}
    cols = {"g_pre": i["L0_xattn_g_pre"], "b_pre": i["L0_xattn_b_pre"], "bq2": np.tile(i["L2_xattn_bq"], 2),
            "bq3": i["L3_xattn_wq_b"], "bk3": i["L3_xattn_wk_b"], "bv3": i["L3_xattn_wv_b"]}
    rows = {"g_ln": i["L0_xattn_g_ln"], "b_ln": i["L0_xattn_b_ln"], "bo1": i["L1_xattn_b_o"], "bg2": i["L2_xattn_bg"],
            "bv2": i["L2_xattn_bv"], "bk2": i["L2_xattn_bk"], "bo2": i["L2_xattn_bo"], "bo3": i["L3_xattn_wo_b"],
            "gate_bi": i["L3_ffn_gate_bi"], "gate_bo": i["L3_ffn_gate_bo"]}
    one = lambda n: np.arange(n, dtype=f)[None, :].repeat(P, 0)
    consts = {"ident": np.eye(P, dtype=f), "head_mask": ((np.arange(P)[:, None] % 64) // DH == np.arange(HALF)).astype(f),
              "upper": np.triu(np.ones((P, P), f), 1), "expert": one(E), "tile128": one(T) * P, "block": one(NBX),
              "slot": one(P), "token": one(T) * P + np.arange(P, dtype=f)[:, None],
              "keep": (np.arange(P) % T != 0).astype(f)[None, :].repeat(P, 0)}

    def moe(w1, w2):
        return np.concatenate([w1.transpose(1, 0, 2).reshape(P, E * F),
                               w2.reshape(E, FC, P, D).transpose(2, 0, 1, 3).reshape(P, E * F)], axis=1)

    return {"x": x, "ctx": ctx, "ctxT": ctx.T, "wts": np.stack([w[n] for n in W_NAMES], 1).reshape(P, -1),
            "cols": np.stack([cols[n] for n in COL_NAMES], 1), "rows": np.concatenate([rows[n] for n in ROW_SIZES]),
            "consts": np.concatenate([consts[n] for n in C_SIZES], axis=1),
            "gates": np.concatenate([i["g_xattn"], i["g_ffn"]]),
            "mask": i["mask_BxSxS2_ik1"].reshape(N, S),
            "kernel0": i["L0_ffn_kernel"], "bias0": i["L0_ffn_bias"],
            "scales": np.concatenate([i["L0_ffn_input_scale"], i["L0_ffn_kernel_scale"]]),
            "kmask": i["mask_BxS2_bf1"].view(np.uint8).reshape(T, P).T,
            "router_w": np.concatenate([i["L1_ffn_router_w"].T, i["L2_ffn_w_router"]], axis=1),
            "gate_w": np.concatenate([i["L3_ffn_gate_wi"], i["L3_ffn_gate_wo"].reshape(FC, P, D).transpose(1, 0, 2).reshape(P, F)], axis=1),
            "moe2": moe(i["L2_ffn_w1"], i["L2_ffn_w2"]), "moe3": moe(i["L3_ffn_exp_wi"], i["L3_ffn_exp_wo"]),
            "b1_2": i["L2_ffn_b1"].reshape(-1), "b2_2": i["L2_ffn_b2"].reshape(-1),
            "b1_3": i["L3_ffn_exp_bi"].reshape(-1), "b2_3": i["L3_ffn_exp_bo"].reshape(-1),
            "moe1": moe(i["L1_ffn_expert_w1"].transpose(0, 2, 1), i["L1_ffn_expert_w2"].transpose(0, 2, 1)),
            }


def kernel(**inputs):
    import numpy as np
    import concourse.bacc as bacc
    from concourse.bass_utils import run_bass_kernel_spmd

    nc = bacc.Bacc("TRN2", target_bir_lowering=False, num_devices=1)
    arrays, aps = {}, {}
    for name, array in layouts(inputs).items():
        array = np.ascontiguousarray(array)
        arrays[f"in_{name}"] = array
        aps[name] = nc.dram_tensor(f"in_{name}", array.shape, mybir.dt.from_np(array.dtype), kind="ExternalInput").ap()
    out = nc.dram_tensor("out_x", (N, D), F32, kind="ExternalOutput").ap()
    program(nc, aps, out)
    result = run_bass_kernel_spmd(nc, [arrays], core_ids=[0])
    return result.results[0]["out_x"].reshape(B, S, D)
```

```python
import itertools
import math

import concourse.bass as bass
from concourse import mybir
from collections import namedtuple
from contextlib import ExitStack, contextmanager

F32, BF16, F16, I32, U32, U8, FP8 = (mybir.dt.float32, mybir.dt.bfloat16, mybir.dt.float16,
                                 mybir.dt.int32, mybir.dt.uint32, mybir.dt.uint8, mybir.dt.float8e4)
ACT, ALU = mybir.ActivationFunctionType, mybir.AluOpType
AX_X = mybir.AxisListType.X

B, S, D, H, DH = 32, 64, 128, 16, 8
P = 128
N = B * S
T = N // P
E, F = 8, 512
FC = F // P
HALF = H // 2
VW = 2 * (DH + 1)
CH = H // 2
PAIRS = 2 * N
NB = PAIRS // P + E
NBX = NB + 8
LN_EPS = 1e-5
NEG = -1000000000.0
SELU_SCALE = 1.0507009873554804934193349852946
SELU_ALPHA = 1.6732632423543772848170429916717
KV_EPS = 1e-6
SEM_NUMBERS = itertools.cycle((range(110, 150), range(160, 200)))
GATHER_NUMBERS = range(210, 228)
PREFETCH_NUMBERS = range(230, 240)


def upto(engine, sem, tile, per=1):
    if isinstance(tile, int) and tile < 0:
        return
    engine.wait_ge(sem, (tile + 1) * per)


def settle(engine, *waits):
    waits = [(sem, value) for sem, value in waits if not isinstance(value, int) or value > 0]
    if any(not isinstance(value, int) for _, value in waits):
        waits = [(sem, value if isinstance(value, int) else engine.snap(value)) for sem, value in waits]
        for _, value in waits:
            if not isinstance(value, int):
                engine.compute_val(value)
        engine.wait_ge(waits[0][0], 1)
    for sem, value in waits:
        engine.wait_ge(sem, value)


def arrived(engine, sems_, u, q):
    engine.wait_ge(sems_[q], (u - q) * 8 + 16)


def inside(u):
    return not isinstance(u, int) or 0 <= u < T


class Memory:
    pass


@contextmanager
def sems(nc, prefix, *names):
    numbers = next(SEM_NUMBERS)
    free = iter(numbers)
    with ExitStack() as c:
        one = lambda n: c.enter_context(nc.semaphore(prefix + n, num=next(free)))
        Semaphores = namedtuple("Semaphores", [n.rstrip("*") for n in names])
        yield Semaphores(*([one(f"{n[:-1]}{i}") for i in range(2)] if n.endswith("*") else one(n) for n in names))
        nc.sync.sem_clear(numbers)


def row(tensor, t):
    return tensor[:, tile_of(t), :].rearrange("p a d -> p (a d)")


def tile_of(t):
    return bass.ds(t, 1) if not isinstance(t, int) else slice(t, t + 1)


def pipeline(eng, step, first, last, steady):
    lo, hi = steady
    for t in range(first, lo):
        step(t, t % 2)
    with eng.Fori(lo, hi, 2) as i:
        step(i, lo % 2)
        step(i + 1, (lo + 1) % 2)
    for t in range(hi, last + 1):
        step(t, t % 2)


def batch_stats(nc, m, name, bn6, rstd, nmr, double=False):
    with sems(nc, name, "chain", "var_ready", "pow_done") as s, nc.Block() as block:
        v, ve, pw = s.chain, s.var_ready, s.pow_done
        sm, df, var = m.st_a, m.st_b, m.st_c

        @block.vector
        def _(dve):
            nc.vector.tensor_tensor(sm[:], bn6[:, :, 1], bn6[:, :, 4], ALU.add).then_inc(v, 1)
            nc.vector.tensor_tensor(df[:], bn6[:, :, 1], bn6[:, :, 4], ALU.subtract).then_inc(v, 1)
            nc.vector.tensor_tensor(var[:], bn6[:, :, 2], bn6[:, :, 5], ALU.add).then_inc(v, 1)
            dve.wait_ge(v, 3)
            nc.vector.scalar_tensor_tensor(m.st_d[:], df[:], 0.25, df[:], ALU.mult, ALU.mult).then_inc(v, 1)
            dve.wait_ge(v, 4)
            nc.vector.scalar_tensor_tensor(var[:], var[:], 1.0 / D, m.st_d[:], ALU.mult, ALU.add).then_inc(v, 1)
            dve.wait_ge(v, 5)
            nc.vector.tensor_scalar(m.st_e[:], var[:], LN_EPS, None, ALU.add).then_inc(ve, 1)
            dve.wait_ge(pw, 1)
            if double:
                nc.vector.tensor_tensor(df[:], rstd[:], rstd[:], ALU.mult).then_inc(v, 1)
                dve.wait_ge(v, 6)
                nc.vector.tensor_tensor(df[:], df[:], var[:], ALU.mult).then_inc(v, 1)
                dve.wait_ge(v, 7)
                nc.vector.tensor_scalar(m.st_e[:], df[:], LN_EPS, None, ALU.add).then_inc(ve, 1)
                dve.wait_ge(pw, 2)
                nc.vector.tensor_tensor(rstd[:], rstd[:], m.st_d[:], ALU.mult).then_inc(v, 1)
                dve.wait_ge(v, 8)
            nc.vector.scalar_tensor_tensor(nmr[:], sm[:], -0.5, rstd[:], ALU.mult, ALU.mult)

        @block.gpsimd
        def _(pool):
            pool.wait_ge(ve, 1)
            nc.gpsimd.tensor_tensor(rstd[:], m.st_e[:], m.minus_half[:], ALU.pow).then_inc(pw, 1)
            if double:
                pool.wait_ge(ve, 2)
                nc.gpsimd.tensor_tensor(m.st_d[:], m.st_e[:], m.minus_half[:], ALU.pow).then_inc(pw, 1)


def attention(nc, m, layer, wq, wk, wv, wo, bq=0.0, bk=0.0, bv=None, tg=None, out_bias=None, fetch=None):
    L0, L1 = layer == 0, layer == 1
    lag = 2 if L0 else 1
    scale = 1.0 / D ** 0.5 if L0 else 1.0 / DH ** 0.5
    clip = 10000.0 / scale
    PT, A, QKV = (m.PT0, m.PT1), m.bankA, m.bankB
    names = ["ctx_in*", "mask_in*", "xn_ready", "xT_done", "xnT_ready", "qk_done", "v_done", "k_out", "v_out",
             "kexp_ready", "scores_done", "pred", "masked", "max_done", "clipped", "sub_done", "exp_done",
             "pt_done", "pt_out", "pv_done", "rec_done", "raw_ready", "stats_done", "var_ready", "pow_done", "hat_done",
             "o_ready", "oT_done", "oT_ready", "out_done", "x_done", "bias_done"]
    first, last = -4, T - 1 + lag
    steady = (3, 11)
    with ExitStack() as c:
        s = c.enter_context(sems(nc, f"a{layer}_", *names))
        block = c.enter_context(nc.Block())

        @block.sync
        def _(sp):
            def step(t, p):
                u, q = t + 3, 1 - p
                if inside(u):
                    upto(sp, s.v_done, u - 2)
                    sp.dma_start(m.ctx_t[q][:], m.ctxT_dram[:, bass.ds(u * P, P)]).then_inc(s.ctx_in[q], 16)
                    if L1:
                        upto(sp, s.pred, u - 2)
                        sp.dma_start(m.mask_t[q][:], m.mask_dram[bass.ds(u * P, P), :]).then_inc(s.mask_in[q], 16)
            pipeline(sp, step, first, last, steady)
            if fetch is not None:
                fetch(sp)

        @block.vector
        def _(dve):
            def soften(u, q):
                if L1:
                    arrived(dve, s.mask_in, u, q)
                    nc.vector.tensor_scalar(m.pred[q][:], m.mask_t[q][:], 0, None, ALU.is_equal).then_inc(s.pred, 1)
                for r in range(2):
                    sc = m.S[q][:, r * F:(r + 1) * F].rearrange("p (h k) -> p h k", k=S)
                    pr = m.probs[q][:, r * F:(r + 1) * F].rearrange("p (h k) -> p h k", k=S)
                    mx = m.rowmax[q][:, r * HALF:(r + 1) * HALF]
                    if not L1:
                        dve.wait_ge(s.scores_done, u * 2 + r + 1)
                    else:
                        settle(dve, (s.scores_done, u * 2 + r + 1), (s.pred, u + 1))
                        nc.vector.copy_predicated(sc, m.pred[q][:].unsqueeze(1).to_broadcast([P, HALF, S]),
                                                  m.negs[:].unsqueeze(1).to_broadcast([P, HALF, S])).then_inc(s.masked, 1)
                        dve.wait_ge(s.masked, u * 2 + r + 1)
                    nc.vector.tensor_reduce(mx, sc, AX_X, ALU.max).then_inc(s.max_done, 1)
                    dve.wait_ge(s.max_done, u * 2 + r + 1)
                    if r == 0:
                        upto(dve, s.pt_done, u - 2, 2)
                    rows = mx.unsqueeze(2).to_broadcast([P, HALF, S])
                    if L0:
                        nc.vector.tensor_scalar(mx, mx, -clip, clip, ALU.max, ALU.min).then_inc(s.clipped, 1)
                        dve.wait_ge(s.clipped, u * 2 + r + 1)
                        nc.vector.scalar_tensor_tensor(pr, sc, -clip, rows, ALU.max, ALU.subtract).then_inc(s.sub_done, 1)
                    else:
                        nc.vector.tensor_tensor(pr, sc, rows, ALU.subtract).then_inc(s.sub_done, 1)

            def step(t, p):
                if L0 and inside(t):
                    for r in range(2):
                        dve.wait_ge(s.pt_done, t * 2 + r + 1)
                        if r == 0:
                            upto(dve, s.pv_done, t - 1)
                        nc.vector.tensor_scalar(m.PTs[:, r * F:(r + 1) * F], PT[r][:], 1.0, None,
                                                ALU.min).then_inc(s.pt_out, 1)
                if L0 and inside(t - 1):
                    u, q = t - 1, 1 - p
                    upto(dve, s.pow_done, u)
                    upto(dve, s.stats_done, u, 2)
                    nc.vector.tensor_scalar(m.raw[q][:], m.raw[q][:], m.omv[q][:, 0:1], m.orstd[q][:],
                                            ALU.subtract, ALU.mult).then_inc(s.hat_done, 1)
                    dve.wait_ge(s.hat_done, 2 * u + 1)
                    nc.vector.tensor_tensor(m.raw[q][:], m.raw[q][:], m.g_ln, ALU.mult).then_inc(s.hat_done, 1)
                    dve.wait_ge(s.hat_done, 2 * u + 2)
                    upto(dve, s.oT_done, u - 2)
                    nc.vector.tensor_tensor(m.os[q][:], m.raw[q][:], m.b_ln, ALU.add).then_inc(s.o_ready, 1)
                    upto(dve, s.o_ready, u)
                    nc.vector.tensor_copy(row(m.ola, u), m.os[q][:])
                if inside(t + 1):
                    soften(t + 1, 1 - p)
                if inside(t):
                    o = m.PT0[:, 0:H * (DH + 1)].rearrange("p (h e) -> p h e", e=DH + 1)
                    upto(dve, s.pv_done, t)
                    nc.vector.reciprocal(m.rden[:], o[:, :, DH]).then_inc(s.rec_done, 1)
                    upto(dve, s.rec_done, t)
                    if not L0:
                        upto(dve, s.oT_done, t - 2)
                    dst = (m.raw if L0 else m.os)[p][:]
                    nc.vector.tensor_tensor(dst.rearrange("p (h d) -> p h d", d=DH), o[:, :, 0:DH],
                                            m.rden[:].unsqueeze(2).to_broadcast([P, H, DH]),
                                            ALU.mult).then_inc(s.raw_ready if L0 else s.o_ready, 1)
                    if L0:
                        upto(dve, s.raw_ready, t)
                        nc.vector.bn_stats(m.obn[:], m.raw[p][:]).then_inc(s.stats_done, 1)
                        settle(dve, (s.stats_done, 2 * t + 1))
                        nc.vector.bn_aggr(m.omv[p][:], m.obn[:]).then_inc(s.stats_done, 1)
                        dve.wait_ge(s.stats_done, 2 * t + 2)
                        nc.vector.tensor_scalar(m.ovar[p][:], m.omv[p][:, 1:2], LN_EPS, None, ALU.add).then_inc(s.var_ready, 1)
                u = t - lag
                if inside(u):
                    upto(dve, s.out_done, u)
                    if L0:
                        nc.vector.tensor_copy(row(m.za, u), m.PT1[:, 0:D]).then_inc(s.x_done, 1)
                    else:
                        xt = row(m.x, u)
                        nc.vector.scalar_tensor_tensor(xt, m.PT1[:, 0:D], tg, xt, ALU.mult, ALU.add).then_inc(s.x_done, 1)
                        upto(dve, s.x_done, u)
                        nc.vector.tensor_tensor(xt, xt, out_bias, ALU.add).then_inc(s.bias_done, 1)
                        upto(dve, s.bias_done, u)
                        nc.vector.bn_stats(row(m.bn6, u), xt)
                u, q = t + 4, p
                if inside(u):
                    upto(dve, s.xT_done, u - 2)
                    ln = nc.vector.tensor_scalar(m.xn[q][:], row(m.x, u), m.rstd[:, tile_of(u)], m.nmr[:, tile_of(u)],
                                                 ALU.mult, ALU.add)
                    if L0:
                        ln = nc.vector.tensor_scalar(m.cn[q][:], row(m.ctx, u), m.crstd[:, tile_of(u)],
                                                     m.cnmr[:, tile_of(u)], ALU.mult, ALU.add)
                    ln.then_inc(s.xn_ready, 1)
            pipeline(dve, step, first, last, steady)

        @block.gpsimd
        def _(pool):
            def step(t, p):
                u, q = t + 2, p
                if inside(u):
                    upto(pool, s.k_out, u)
                    upto(pool, s.scores_done, u - 2, 2)
                    nc.gpsimd.tensor_tensor(m.kexp[q][:], m.kT[q][:].unsqueeze(1).to_broadcast([P, HALF, P]),
                                            m.head_mask.unsqueeze(2).to_broadcast([P, HALF, P]),
                                            ALU.mult).then_inc(s.kexp_ready, 1)
                if L0 and inside(t):
                    upto(pool, s.var_ready, t)
                    nc.gpsimd.tensor_tensor(m.orstd[p][:], m.ovar[p][:], m.minus_half[:, 0:1], ALU.pow).then_inc(s.pow_done, 1)
            pipeline(pool, step, first, last, steady)

        @block.scalar
        def _(act):
            def step(t, p):
                u, q = t + 2, p
                v, r = t + 1, 1 - p
                if inside(u):
                    upto(act, s.qk_done, u)
                if inside(v):
                    upto(act, s.v_done, v)
                if inside(u):
                    upto(act, s.scores_done, u - 2, 2)
                    upto(act, s.kexp_ready, u - 2)
                    nc.scalar.activation(m.qT[q][:], QKV[:, 0:P], ACT.Identity, bias=bq)
                    nc.scalar.activation(m.kT[q][:], QKV[:, P:2 * P], ACT.Identity, bias=bk).then_inc(s.k_out, 1)
                if inside(v):
                    upto(act, s.pv_done, v - 2)
                    for hh in range(2):
                        src = QKV[64 * hh:64 * hh + 64, 2 * P:4 * P].rearrange("p (b c e d) -> p b c e d", b=2, c=CH, e=2)
                        dst = m.vexp[r][64 * hh:64 * hh + 64, :, :].rearrange("p b (c e d) -> p b c e d", c=CH, e=2)
                        out = nc.scalar.copy(dst[:, :, :, hh, 0:DH], src[:, :, :, hh, :])
                    out.then_inc(s.v_out, 1)
                if not L0 and inside(t):
                    for r2 in range(2):
                        act.wait_ge(s.pt_done, t * 2 + r2 + 1)
                        if r2 == 0:
                            upto(act, s.pv_done, t - 1)
                        nc.scalar.copy(m.PTs[:, r2 * F:(r2 + 1) * F], PT[r2][:]).then_inc(s.pt_out, 1)
                u, w = t + 3, t - lag
                if inside(w):
                    upto(act, s.oT_done, w)
                if inside(u):
                    upto(act, s.xT_done, u)
                if inside(w):
                    upto(act, s.out_done, w - 1)
                    nc.scalar.activation(m.oT[:], A[:, 0:P], ACT.Identity, bias=0.0 if bv is None else bv).then_inc(s.oT_ready, 1)
                if inside(u):
                    q = 1 - p
                    upto(act, s.qk_done, u - 2)
                    if L0:
                        nc.scalar.activation(m.xnT[q][:], A[:, P:2 * P], ACT.Identity, scale=m.g_pre, bias=m.b_pre)
                        nc.scalar.activation(m.cnT[q][:], A[:, 2 * P:3 * P], ACT.Identity, scale=m.g_pre,
                                             bias=m.b_pre).then_inc(s.xnT_ready, 1)
                    else:
                        nc.scalar.copy(m.xnT[q][:], A[:, P:2 * P]).then_inc(s.xnT_ready, 1)
                u, q = t + 1, 1 - p
                if inside(u):
                    for r in range(2):
                        act.wait_ge(s.sub_done, u * 2 + r + 1)
                        pr = m.probs[q][:, r * F:(r + 1) * F]
                        nc.scalar.activation(pr, pr, ACT.Exp, scale=scale).then_inc(s.exp_done, 1)
            pipeline(act, step, first, last, steady)

        @block.tensor
        def _(pe):
            def step(t, p):
                u, q = t + 2, p
                v, r = t + 1, 1 - p
                if inside(u):
                    upto(pe, s.xnT_ready, u)
                    arrived(pe, s.ctx_in, u, q)
                    upto(pe, s.k_out, u - 1)
                if inside(v):
                    upto(pe, s.v_out, v - 1)
                if inside(u):
                    nc.tensor.matmul(QKV[:, 0:P], wq, m.xnT[q][:], start=True, stop=True)
                    nc.tensor.matmul(QKV[:, P:2 * P], wk, m.cnT[q][:] if L0 else m.ctx_t[q][:], start=True,
                                     stop=True).then_inc(s.qk_done, 1)
                if inside(v):
                    for b in range(2):
                        for hh in range(2):
                            out = nc.tensor.matmul(QKV[64 * hh:64 * hh + 64, (2 + b) * P:(3 + b) * P],
                                                   m.ctx_t[r][:, b * S:(b + 1) * S], wv, start=True, stop=True)
                    out.then_inc(s.v_done, 1)
                if inside(t):
                    for r2 in range(2):
                        act_done = t * 2 + r2 + 1
                        pe.wait_ge(s.exp_done, act_done)
                        if r2 == 0:
                            upto(pe, s.raw_ready if L0 else s.o_ready, t - 1)
                        else:
                            upto(pe, s.x_done, t - 1 - lag)
                        for c4 in range(4):
                            cc = 4 * r2 + c4
                            out = nc.tensor.transpose(PT[r2][:, c4 * P:(c4 + 1) * P], m.probs[p][:, cc * P:(cc + 1) * P], m.ident)
                        out.then_inc(s.pt_done, 1)
                u, q = t + 1, 1 - p
                if inside(u):
                    settle(pe, (s.kexp_ready, u + 1), (s.sub_done, 2 * (u - 1)))
                    for r2 in range(2):
                        for b in range(2):
                            out = nc.tensor.matmul(m.S[q][64 * b:64 * b + 64, r2 * F:(r2 + 1) * F],
                                                   m.qT[q][64 * r2:64 * r2 + 64, S * b:S * b + S],
                                                   m.kexp[q][64 * r2:64 * r2 + 64, :, S * b:S * b + S], start=True, stop=True)
                        out.then_inc(s.scores_done, 1)
                w, u = t - lag, t + 3
                if inside(w):
                    upto(pe, s.o_ready, w)
                    upto(pe, s.oT_ready, w - 1)
                if inside(u):
                    upto(pe, s.xn_ready, u)
                    upto(pe, s.xnT_ready, u - 1)
                if inside(w):
                    nc.tensor.transpose(A[:, 0:P], m.os[(p + lag) % 2][:], m.ident).then_inc(s.oT_done, 1)
                if inside(u):
                    out = nc.tensor.transpose(A[:, P:2 * P], m.xn[1 - p][:], m.ident)
                    if L0:
                        out = nc.tensor.transpose(A[:, 2 * P:3 * P], m.cn[1 - p][:], m.ident)
                    out.then_inc(s.xT_done, 1)
                if inside(t):
                    upto(pe, s.pt_out, t, 2)
                    upto(pe, s.v_out, t)
                    for cc in range(CH):
                        for b in range(2):
                            out = nc.tensor.matmul(m.PT0[64 * b:64 * b + 64, cc * VW:(cc + 1) * VW],
                                                   m.PTs[:, cc * P + S * b:cc * P + S * b + S],
                                                   m.vexp[p][:, b, cc * VW:(cc + 1) * VW], start=True, stop=True)
                    out.then_inc(s.pv_done, 1)
                if inside(w):
                    upto(pe, s.oT_ready, w)
                    if not inside(t):
                        upto(pe, s.pt_out, T - 1, 2)
                    upto(pe, s.x_done, w - 1)
                    nc.tensor.matmul(m.PT1[:, 0:D], m.oT[:], wo, start=True, stop=True).then_inc(s.out_done, 1)
            pipeline(pe, step, first, last, steady)


def xattn0_tail(nc, m, tg):
    G = 4
    with sems(nc, "t0_", "gelu_done", "sum_done", "x_done") as s, nc.Block() as block:
        @block.scalar
        def _(act):
            for g in range(G):
                z = m.za[:, g * (T // G):(g + 1) * (T // G), :]
                nc.scalar.activation(z, z, ACT.Gelu).then_inc(s.gelu_done, 1)

        @block.vector
        def _(dve):
            for g in range(G):
                sl = slice(g * (T // G), (g + 1) * (T // G))
                dve.wait_ge(s.gelu_done, g + 1)
                nc.vector.tensor_tensor(m.za[:, sl, :], m.za[:, sl, :], m.ola[:, sl, :], ALU.add).then_inc(s.sum_done, 1)
                dve.wait_ge(s.sum_done, g + 1)
                nc.vector.scalar_tensor_tensor(m.x[:, sl, :], m.za[:, sl, :], tg, m.x[:, sl, :], ALU.mult, ALU.add).then_inc(s.x_done, 1)
                dve.wait_ge(s.x_done, g + 1)
                for t in range(sl.start, sl.stop):
                    nc.vector.bn_stats(m.bn6[:, t, :], m.x[:, t, :])


def quantize(nc, dve, sem, start, m, v, half, square, big, q):
    n = v.shape[-1]
    small8, big8, over = m.small8[:, 0:n], m.big8[:, 0:n], m.over[:, 0:n]
    nc.vector.tensor_scalar(small8, v, 16.0, -16.0, ALU.min, ALU.max, saturate=False)
    nc.vector.tensor_scalar(over, square, 256.0, None, ALU.is_gt)
    nc.vector.tensor_scalar(big8, half, 224.0, -224.0, ALU.min, ALU.max, saturate=False).then_inc(sem, 1)
    dve.wait_ge(sem, start + 1)
    nc.vector.tensor_scalar(q, small8, 0.5, None, ALU.mult).then_inc(sem, 1)
    nc.vector.tensor_copy(big, big8).then_inc(sem, 1)
    dve.wait_ge(sem, start + 3)
    nc.vector.copy_predicated(q, over, big).then_inc(sem, 1)


def ffn0(nc, m, tg, fetch):
    G = F // D
    flat = lambda tensor: tensor.rearrange("p t d -> p (t d)")
    with sems(nc, "f0_", "ln_done", "scaled", "squares", "quant", "q_read", "nan_chain", "q_ready", "qT_done", "qT_ready", "y_done", "y_chain", "x_done") as s, nc.Block() as block:
        block.sync(fetch)
        v, half = [pr[:, 0:F] for pr in m.probs], [pr[:, F:2 * F] for pr in m.probs]
        square, quant = [flat(k[:, 0:G, :]) for k in m.kexp], [flat(k[:, G:2 * G, :]) for k in m.kexp]
        big, Y = m.PTs[:, 0:F], (m.PT0, m.PT1)

        @block.scalar
        def _(act):
            for g in range(T // G):
                q = g % 2
                upto(act, s.scaled, g - 1)
                for t in range(G):
                    u = g * G + t
                    out = nc.scalar.activation(m.xb[:, t * D:(t + 1) * D], m.x[:, u, :], ACT.Identity,
                                               scale=m.rstd[:, u:u + 1], bias=m.nmr[:, u:u + 1])
                out.then_inc(s.ln_done, 1)
                upto(act, s.ln_done, g)
                upto(act, s.q_read, g - 2)
                nc.scalar.activation(v[q], m.xb[:], ACT.Copy, scale=m.scales[:, 2:3]).then_inc(s.scaled, 1)
                upto(act, s.scaled, g)
                nc.scalar.activation(half[q], v[q], ACT.Copy, scale=0.5)
                nc.scalar.activation(square[q], v[q], ACT.Square).then_inc(s.squares, 1)
                if g:
                    upto(act, s.qT_done, g - 1)
                    upto(act, s.y_done, g - 2)
                    nc.scalar.copy(m.xqT[:], m.bankA[:]).then_inc(s.qT_ready, 1)
            upto(act, s.qT_done, T // G - 1)
            upto(act, s.y_done, T // G - 2)
            nc.scalar.copy(m.xqT[:], m.bankA[:]).then_inc(s.qT_ready, 1)

        @block.vector
        def _(dve):
            def add(g):
                yb = flat(m.yb[:])
                upto(dve, s.y_done, g)
                nc.vector.tensor_scalar(yb, Y[g % 2][:], m.scales[:, 3:4], None, ALU.mult).then_inc(s.y_chain, 1)
                dve.wait_ge(s.y_chain, 2 * g + 1)
                nc.vector.tensor_tensor(m.yb2[:], m.yb[:], m.bias0[:].unsqueeze(1).to_broadcast([P, G, D]),
                                        ALU.add).then_inc(s.y_chain, 1)
                dve.wait_ge(s.y_chain, 2 * g + 2)
                for t in range(G):
                    u = g * G + t
                    out = nc.vector.scalar_tensor_tensor(m.x[:, u, :], m.yb2[:, t, :], m.tgn[:, u:u + 1], m.x[:, u, :],
                                                         ALU.mult, ALU.add)
                out.then_inc(s.x_done, 1)
                upto(dve, s.x_done, g)
                for t in range(G):
                    nc.vector.bn_stats(m.bn6[:, g * G + t, :], m.x[:, g * G + t, :])

            for g in range(T // G):
                q = g % 2
                upto(dve, s.squares, g)
                upto(dve, s.qT_done, g - 2)
                quantize(nc, dve, s.quant, 4 * g, m, v[q], half[q], square[q], big, quant[q])
                tgn = m.tgn[:, g * G:(g + 1) * G]
                nc.vector.tensor_reduce(tgn, v[q].rearrange("p (t d) -> p t d", d=D), AX_X, ALU.max,
                                        apply_absolute_value=True).then_inc(s.nan_chain, 1)
                dve.wait_ge(s.nan_chain, 4 * g + 1)
                nc.vector.tensor_scalar(tgn, tgn, 464.0, 3e38, ALU.is_gt, ALU.mult).then_inc(s.nan_chain, 1)
                dve.wait_ge(s.nan_chain, 4 * g + 2)
                nc.vector.tensor_scalar(tgn, tgn, 1e5, 0.0, ALU.mult, ALU.mult).then_inc(s.nan_chain, 1)
                dve.wait_ge(s.nan_chain, 4 * g + 3)
                nc.vector.tensor_scalar(tgn, tgn, tg, None, ALU.add).then_inc(s.nan_chain, 1)
                dve.wait_ge(s.quant, 4 * g + 4)
                dve.wait_ge(s.nan_chain, 4 * g + 4)
                nc.vector.tensor_copy(m.settled[:], tgn[:, 0:1]).then_inc(s.q_read, 1)
                if g:
                    add(g - 1)
            add(T // G - 1)

        @block.tensor
        def _(pe):
            for g in range(T // G):
                upto(pe, s.q_read, g)
                upto(pe, s.qT_ready, g - 1)
                for t in range(G):
                    out = nc.tensor.transpose(m.bankA[:, t * P:(t + 1) * P], quant[g % 2][:, t * P:(t + 1) * P], m.ident)
                out.then_inc(s.qT_done, 1)
                upto(pe, s.qT_ready, g)
                upto(pe, s.x_done, g - 2)
                for t in range(G):
                    out = nc.tensor.matmul(Y[g % 2][:, t * D:(t + 1) * D], m.xqT[:, t * P:(t + 1) * P], m.kq[:],
                                           start=True, stop=True)
                out.then_inc(s.y_done, 1)


def linear_attention(nc, m, wg, wv, wo, wq, wk, bg, bv, bk, bq, bo, fetch):
    names = ["ctx_in*", "xn_ready", "xT_done", "xnT_ready", "k_done", "u_done", "q_done", "bias_done", "kv_ready", "q_ready", "ub_ready", "silu_done",
             "kv_done", "kvs_ready", "r_done", "z_done", "ua_ready", "uaT_done", "uaT_ready", "out_done", "x_chain"]
    steady = (2, 12)
    W = D + 1
    U, Q, KV, R, C, O = m.S[0][:, 0:F], m.S[0][:, F:2 * F], m.S[1][:, 0:F], m.S[1][:, F:2 * F], m.PT0, m.PT1
    with sems(nc, "l2_", *names) as s, nc.Block() as block:
        first, last = -3, T - 1

        @block.sync
        def _(sp):
            def step(t, p):
                u, q = t + 2, p
                if inside(u):
                    upto(sp, s.u_done, u - 2)
                    sp.dma_start(m.ctx_t[q][:], m.ctxT_dram[:, bass.ds(u * P, P)]).then_inc(s.ctx_in[q], 16)
            pipeline(sp, step, first, last, steady)
            fetch(sp)

        @block.vector
        def _(dve):
            def step(t, p):
                u, q = t + 1, 1 - p
                if inside(u):
                    km = m.kmask[:, tile_of(u)]
                    upto(dve, s.u_done, u)
                    nc.vector.tensor_tensor(m.kb[:], U[:, D:D + D // 2], bk, ALU.add).then_inc(s.bias_done, 1)
                    nc.vector.tensor_tensor(m.vb[:], U[:, 2 * D:3 * D], bv, ALU.add).then_inc(s.bias_done, 1)
                    upto(dve, s.silu_done, u - 1)
                    nc.vector.tensor_tensor(m.ub[:], U[:, 0:D], bg, ALU.add).then_inc(s.ub_ready, 1)
                    dve.wait_ge(s.bias_done, 2 * u + 1)
                    upto(dve, s.kv_done, u - 2)
                    nc.vector.scalar_tensor_tensor(m.kk[q][:], m.kb[:], 0.0, m.kb[:], ALU.max, ALU.mult)
                    dve.wait_ge(s.bias_done, 2 * u + 2)
                    nc.vector.tensor_copy(m.va[q][:, D:W], km)
                    nc.vector.tensor_scalar(m.va[q][:, 0:D], m.vb[:], km, None, ALU.mult).then_inc(s.kv_ready, 1)
                if inside(t):
                    upto(dve, s.r_done, t)
                    nc.vector.tensor_scalar(m.zr[:], R[:, D:W], KV_EPS, None, ALU.add).then_inc(s.z_done, 1)
                    dve.wait_ge(s.z_done, 2 * t + 1)
                    nc.vector.reciprocal(m.zr[:], m.zr[:]).then_inc(s.z_done, 1)
                    dve.wait_ge(s.z_done, 2 * t + 2)
                    upto(dve, s.silu_done, t)
                    upto(dve, s.uaT_done, t - 2)
                    nc.vector.scalar_tensor_tensor(m.ua[p][:], R[:, 0:D], m.zr[:], m.us[p][:], ALU.mult, ALU.mult).then_inc(s.ua_ready, 1)
                if inside(u):
                    upto(dve, s.q_done, u)
                    nc.vector.tensor_scalar(m.qr[:], Q[:, 0:S], bq, 0.0, ALU.add, ALU.max).then_inc(s.q_ready, 1)
                    dve.wait_ge(s.q_ready, 2 * u + 1)
                    upto(dve, s.r_done, u - 2)
                    nc.vector.tensor_tensor(m.qq[q][:], m.qr[:], m.qr[:], ALU.mult).then_inc(s.q_ready, 1)
                    upto(dve, s.kv_done, u)
                    nc.vector.tensor_copy(m.kvs[q][:], KV[:, 0:W]).then_inc(s.kvs_ready, 1)
                if inside(t):
                    xt, wt = row(m.x, t), m.qgate[:, tile_of(t)]
                    upto(dve, s.out_done, t)
                    nc.vector.scalar_tensor_tensor(xt, O[:, 0:D], wt, xt, ALU.mult, ALU.add).then_inc(s.x_chain, 1)
                    dve.wait_ge(s.x_chain, 2 * t + 1)
                    nc.vector.scalar_tensor_tensor(xt, bo, wt, xt, ALU.mult, ALU.add).then_inc(s.x_chain, 1)
                    dve.wait_ge(s.x_chain, 2 * t + 2)
                    nc.vector.bn_stats(row(m.bn6, t), xt)
                u, q = t + 3, 1 - p
                if inside(u):
                    upto(dve, s.xT_done, u - 2)
                    nc.vector.tensor_scalar(m.xn[q][:], row(m.x, u), m.rstd[:, tile_of(u)], m.nmr[:, tile_of(u)],
                                            ALU.mult, ALU.add).then_inc(s.xn_ready, 1)
            pipeline(dve, step, first, last, steady)

        @block.scalar
        def _(act):
            def step(t, p):
                u, q = t + 1, 1 - p
                if inside(u):
                    upto(act, s.ub_ready, u)
                    upto(act, s.ua_ready, u - 2)
                    nc.scalar.activation(m.us[q][:], m.ub[:], ACT.Silu).then_inc(s.silu_done, 1)
                if inside(t + 2):
                    upto(act, s.xT_done, t + 2)
                    upto(act, s.q_done, t)
                    nc.scalar.copy(m.xnT[p][:], m.bankA[:, 0:P]).then_inc(s.xnT_ready, 1)
                if inside(t):
                    upto(act, s.uaT_done, t)
                    upto(act, s.out_done, t - 1)
                    nc.scalar.copy(m.oT[:], C[:, 0:P]).then_inc(s.uaT_ready, 1)
            pipeline(act, step, first, last, steady)

        @block.tensor
        def _(pe):
            def step(t, p):
                u, q = t + 1, 1 - p
                if inside(u):
                    arrived(pe, s.ctx_in, u, q)
                    upto(pe, s.xnT_ready, u)
                    upto(pe, s.ub_ready, u - 1)
                    upto(pe, s.kv_ready, u - 1)
                    nc.tensor.matmul(U[:, 0:D], m.xnT[q][:], wg, start=True, stop=True)
                    nc.tensor.matmul(U[:, 2 * D:3 * D], m.ctx_t[q][:], wv, start=True, stop=True)
                    nc.tensor.matmul(U[:, D:D + D // 2], m.ctx_t[q][:], wk, start=True, stop=True).then_inc(s.u_done, 1)
                    upto(pe, s.q_ready, u - 1, 2)
                    for b in range(2):
                        out = nc.tensor.matmul(Q[64 * b:64 * b + 64, 0:S], wq, m.xnT[q][:, S * b:S * b + S], start=True, stop=True)
                    out.then_inc(s.q_done, 1)
                if inside(t):
                    settle(pe, (s.q_ready, 2 * t + 2), (s.kvs_ready, t + 1), (s.ua_ready, t))
                    for b in range(2):
                        out = nc.tensor.matmul(R[64 * b:64 * b + 64, 0:W], m.qq[p][64 * b:64 * b + 64, :],
                                               m.kvs[p][64 * b:64 * b + 64, :], start=True, stop=True)
                    out.then_inc(s.r_done, 1)
                if inside(t + 2):
                    upto(pe, s.xn_ready, t + 2)
                    upto(pe, s.xnT_ready, t + 1)
                    nc.tensor.transpose(m.bankA[:, 0:P], m.xn[p][:], m.ident).then_inc(s.xT_done, 1)
                if inside(u):
                    settle(pe, (s.kv_ready, u + 1), (s.kvs_ready, u))
                    for b in range(2):
                        out = nc.tensor.matmul(KV[64 * b:64 * b + 64, 0:W], m.kk[q][64 * b:64 * b + 64, :],
                                               m.va[q][64 * b:64 * b + 64, :], start=True, stop=True)
                    out.then_inc(s.kv_done, 1)
                if inside(t):
                    upto(pe, s.ua_ready, t)
                    upto(pe, s.uaT_ready, t - 1)
                    nc.tensor.transpose(C[:, 0:P], m.ua[p][:], m.ident).then_inc(s.uaT_done, 1)
                    upto(pe, s.uaT_ready, t)
                    if not isinstance(t, int) or t >= 1:
                        pe.wait_ge(s.x_chain, 2 * t - 1)
                    nc.tensor.matmul(O[:, 0:D], m.oT[:], wo, start=True, stop=True).then_inc(s.out_done, 1)
            pipeline(pe, step, first, last, steady)


def router(nc, m, layer, wr):
    G = F // P
    names = ["xn_ready", "xT_done", "xT_ready", "lg_done", "lg_read", "soft", "exp_done", "top_done", "idx_done", "out*"]
    with sems(nc, f"r{layer}_", *names) as s, nc.Block() as block:
        xn, xT = [pr[:, 0:F] for pr in m.probs], [pr[:, F:2 * F] for pr in m.probs]
        tiles = lambda ap: ap.rearrange("p (t d) -> p t d", d=D)

        @block.sync
        def _(sp):
            for g in range(T // G):
                upto(sp, s.xn_ready, g)
                sp.dma_start(m.XN[g * G * P:(g + 1) * G * P, :].rearrange("(t p) d -> p t d", p=P),
                             tiles(xn[g % 2])).then_inc(s.out[g % 2], 16)
            for q in range(2):
                sp.wait_ge(s.out[q], T // G // 2 * 16)

        @block.vector
        def _(dve):
            for g in range(T // G):
                upto(dve, s.xT_done, g - 2)
                if g >= 2:
                    dve.wait_ge(s.out[g % 2], g // 2 * 16)
                for t in range(G):
                    u = g * G + t
                    out = nc.vector.tensor_scalar(xn[g % 2][:, t * D:(t + 1) * D], m.x[:, u, :], m.rstd[:, u:u + 1],
                                                  m.nmr[:, u:u + 1], ALU.mult, ALU.add)
                out.then_inc(s.xn_ready, 1)
            upto(dve, s.lg_done, T // G - 1)
            nc.vector.tensor_copy(m.lg[:], m.bankB[:, 0:T * E].rearrange("p (t e) -> p t e", e=E)).then_inc(s.lg_read, 1)
            dve.wait_ge(s.lg_read, 1)
            scores = m.lg
            if layer == 2:
                e_t = lambda ap: ap.unsqueeze(2).to_broadcast([P, T, E])
                nc.vector.tensor_reduce(m.st_a[:], m.lg[:], AX_X, ALU.max).then_inc(s.soft, 1)
                dve.wait_ge(s.soft, 1)
                nc.vector.tensor_tensor(m.lp[:], m.lg[:], e_t(m.st_a[:]), ALU.subtract).then_inc(s.soft, 1)
                dve.wait_ge(s.exp_done, 1)
                nc.vector.tensor_reduce(m.st_b[:], m.lp[:], AX_X, ALU.add).then_inc(s.soft, 1)
                dve.wait_ge(s.soft, 3)
                nc.vector.reciprocal(m.st_c[:], m.st_b[:]).then_inc(s.soft, 1)
                dve.wait_ge(s.soft, 4)
                nc.vector.tensor_tensor(m.lp[:], m.lp[:], e_t(m.st_c[:]), ALU.mult).then_inc(s.soft, 1)
                dve.wait_ge(s.soft, 5)
                scores = m.lp
            for t in range(T):
                out = nc.vector.max(m.tops[:, t, :], scores[:, t, :])
            out.then_inc(s.top_done, 1)
            dve.wait_ge(s.top_done, 1)
            for t in range(T):
                out = nc.vector.max_index(m.idxs[:, t, :], m.tops[:, t, :], scores[:, t, :])
            out.then_inc(s.idx_done, 1)
            nc.vector.tensor_copy(m.tv[:].rearrange("p k t -> p t k"), m.tops[:, :, 0:2])
            dve.wait_ge(s.idx_done, 1)
            nc.vector.tensor_copy(m.ti[:].rearrange("p k t -> p t k"), m.idxs[:, :, 0:2])

        @block.scalar
        def _(act):
            for g in range(T // G):
                upto(act, s.xT_done, g)
                upto(act, s.lg_done, g - 2)
                nc.scalar.copy(xT[g % 2], (m.bankA, m.PT0)[g % 2][:]).then_inc(s.xT_ready, 1)
            if layer == 2:
                act.wait_ge(s.soft, 2)
                nc.scalar.activation(m.lp[:], m.lp[:], ACT.Exp).then_inc(s.exp_done, 1)

        @block.tensor
        def _(pe):
            pe.wait_ge(m.router_in, 32)

            def turn(g):
                upto(pe, s.xn_ready, g)
                upto(pe, s.xT_ready, g - 2)
                for t in range(G):
                    out = nc.tensor.transpose((m.bankA, m.PT0)[g % 2][:, t * P:(t + 1) * P],
                                              xn[g % 2][:, t * P:(t + 1) * P], m.ident)
                out.then_inc(s.xT_done, 1)
            turn(0)
            for g in range(T // G):
                if g + 1 < T // G:
                    turn(g + 1)
                upto(pe, s.xT_ready, g)
                for t in range(G):
                    u = g * G + t
                    out = nc.tensor.matmul(m.bankB[:, u * E:(u + 1) * E], xT[g % 2][:, t * P:(t + 1) * P], wr,
                                           start=True, stop=True)
                out.then_inc(s.lg_done, 1)


def two_best(nc, m, dve, s, scores, t, ready):
    settle(dve, ready, (s.idx_done, t))
    nc.vector.max(m.top[:], scores).then_inc(s.top_done, 1)
    settle(dve, (s.top_done, t + 1))
    nc.vector.max_index(m.idx[:], m.top[:], scores).then_inc(s.idx_done, 1)
    nc.vector.tensor_copy(m.tv[:, :, tile_of(t)].rearrange("p a b -> p (a b)"), m.top[:, 0:2])
    upto(dve, s.idx_done, t)
    nc.vector.tensor_copy(m.ti[:, :, tile_of(t)].rearrange("p a b -> p (a b)"), m.idx[:, 0:2])


def dispatch(nc, m, layer, tg):
    J, G = 2 * T, T // 2
    with sems(nc, f"d{layer}_", "chain", "marks_ready", "sums_done", "gap_ready", "exp_done", "hot_ready", "list_step") as s, nc.Block() as block:
        @block.vector
        def _(dve):
            n = [0]

            def then(ins):
                n[0] += 1
                ins.then_inc(s.chain, 1)
                dve.wait_ge(s.chain, n[0])

            e_t = lambda ap: ap.unsqueeze(1).to_broadcast([P, E, T])
            t_e = lambda ap: ap.unsqueeze(2).to_broadcast([P, E, T])
            v0, v1, w0, w1 = m.tv[:, 0, :], m.tv[:, 1, :], m.wt[:, 0, :], m.wt[:, 1, :]
            if layer == 1:
                nc.vector.tensor_tensor(m.st_a[:], v1, v0, ALU.subtract).then_inc(s.gap_ready, 1)
            for k in range(2):
                then(nc.vector.tensor_tensor(m.hot[k][:], e_t(m.ti[:, k, :]), t_e(m.con["expert"]), ALU.is_equal))
            nc.vector.tensor_tensor(m.marks[:], m.hot[0][:], m.hot[1][:], ALU.add).then_inc(s.marks_ready, 1)
            if layer == 1:
                dve.wait_ge(s.exp_done, 1)
                then(nc.vector.tensor_scalar(m.st_c[:], m.st_b[:], 1.0, None, ALU.add))
                then(nc.vector.reciprocal(m.st_c[:], m.st_c[:]))
                then(nc.vector.tensor_scalar(w0, m.st_c[:], tg, None, ALU.mult))
                nc.vector.tensor_tensor(w1, w0, m.st_b[:], ALU.mult)
            elif layer == 2:
                nc.vector.tensor_scalar(m.wt[:], m.tv[:], tg, None, ALU.mult)
            else:
                then(nc.vector.tensor_tensor(m.st_c[:], v0, v1, ALU.add))
                then(nc.vector.reciprocal(m.st_c[:], m.st_c[:]))
                then(nc.vector.tensor_scalar(m.st_c[:], m.st_c[:], tg, None, ALU.mult))
                nc.vector.tensor_tensor(w0, v0, m.st_c[:], ALU.mult)
                nc.vector.tensor_tensor(w1, v1, m.st_c[:], ALU.mult)
            dve.wait_ge(s.sums_done, 2)
            flat = lambda tensor: tensor[:].rearrange("p e t -> p (e t)")
            then(nc.vector.tensor_copy(flat(m.tot), m.bankB[:, 0:P]))
            then(nc.vector.tensor_tensor_scan(flat(m.incl), m.con["keep"], flat(m.tot), 0.0, ALU.mult, ALU.add))
            then(nc.vector.tensor_tensor(m.pos[:], m.incl[:], m.tot[:], ALU.subtract))
            then(nc.vector.tensor_tensor(flat(m.pos), flat(m.pos), m.bankA[:, 0:P], ALU.add))
            count = m.incl[:, :, T - 1]
            then(nc.vector.tensor_tensor(m.tot[:], t_e(count), e_t(m.con["tile128"]), ALU.is_gt))
            then(nc.vector.tensor_reduce(m.nb[:], m.tot[:], AX_X, ALU.add))
            then(nc.vector.tensor_tensor_scan(m.cum[:], m.ones[:, 0:E], m.nb[:], 0.0, ALU.mult, ALU.add))
            then(nc.vector.tensor_tensor(m.base[:], m.cum[:], m.nb[:], ALU.subtract))
            then(nc.vector.tensor_scalar(m.base[:], m.base[:], float(P), None, ALU.mult))
            then(nc.vector.tensor_tensor(m.pos[:], m.pos[:], t_e(m.base[:]), ALU.add))
            for k in range(2):
                then(nc.vector.tensor_tensor(m.tot[:], m.hot[k][:], m.pos[:], ALU.mult))
                then(nc.vector.tensor_reduce(m.dest[:, k, :], m.tot[:].rearrange("p e t -> p t e"), AX_X, ALU.add))
                then(nc.vector.tensor_reduce(m.valid[:, k, :], m.hot[k][:].rearrange("p e t -> p t e"), AX_X, ALU.add))
            then(nc.vector.tensor_tensor(m.wt[:], m.wt[:], m.valid[:], ALU.mult))
            then(nc.vector.tensor_tensor(m.valid[:], m.valid[:], m.con["token"].unsqueeze(1).to_broadcast([P, 2, T]), ALU.mult))
            then(nc.vector.tensor_copy(m.desti[:], m.dest[:]))
            then(nc.vector.tensor_scalar(m.blki[:], m.desti[:], 7, None, ALU.logical_shift_right))
            then(nc.vector.tensor_copy(m.blk[:], m.blki[:]))
            then(nc.vector.scalar_tensor_tensor(m.slot[:], m.blk[:], -float(P), m.dest[:], ALU.mult, ALU.add))
            then(nc.vector.tensor_scalar(m.nbf[:], m.cum[:, E - 1:E], 3.0, 1.0, ALU.max, ALU.add))
            then(nc.vector.tensor_copy(m.nbi[:], m.nbf[:]))
            then(nc.vector.tensor_scalar(m.nbi[:], m.nbi[:], 1, 1, ALU.logical_shift_right, ALU.logical_shift_left))
            big = m.ebc[:]
            then(nc.vector.tensor_tensor(big, m.con["block"].unsqueeze(1).to_broadcast([P, E, NBX]),
                                         m.cum[:].unsqueeze(2).to_broadcast([P, E, NBX]), ALU.is_ge))
            then(nc.vector.tensor_reduce(m.ebf[:], big.rearrange("p e b -> p b e"), AX_X, ALU.add))
            then(nc.vector.tensor_scalar(m.ebf[:], m.ebf[:], float(E - 1), None, ALU.min))
            nc.vector.tensor_scalar(m.eb[:, 0:2], m.ebf[:, 0:2], float(E), None, ALU.mult)
            nc.vector.scalar_tensor_tensor(m.eb[:, 2:NBX], m.ebf[:, 2:NBX], float(E), m.ebf[:, 0:NBX - 2], ALU.mult, ALU.add)

            for g in range(J // G):
                q, k, ts = g % 2, g * G // T, slice(g * G % T, g * G % T + G)
                over = lambda ap, n: ap[:, k, ts].unsqueeze(2).to_broadcast([P, G, n])
                upto(dve, s.list_step, g - 2)
                nc.vector.tensor_tensor(m.hot_slot[q][:], m.con["slot"].unsqueeze(1).to_broadcast([P, G, P]),
                                        over(m.slot, P), ALU.is_equal)
                if g:
                    dve.wait_ge(s.hot_ready, g)
                then(nc.vector.tensor_tensor(m.hot_f[:], m.con["block"].unsqueeze(1).to_broadcast([P, G, NBX]),
                                             over(m.blk, NBX), ALU.is_equal))
                nc.vector.tensor_tensor(m.hot_blk[q][:], m.hot_f[:], over(m.valid, NBX), ALU.mult).then_inc(s.hot_ready, 1)
            first, both, where = m.ebc[:, 0, :], m.ebc[:, 1, :], m.ebc[:, 2, :]
            dve.wait_ge(s.list_step, J // G)
            then(nc.vector.tensor_copy(first, m.PT0[:, 0:NBX]))
            then(nc.vector.tensor_tensor(both, first, m.PT1[:, 0:NBX], ALU.add))
            then(nc.vector.tensor_scalar(first, both, 1.0, 1.0, ALU.max, ALU.subtract))
            then(nc.vector.tensor_copy(m.tok[:], first))
            then(nc.vector.scalar_tensor_tensor(where, both, 0.5, m.con["spare"], ALU.is_lt, ALU.mult))
            then(nc.vector.tensor_tensor(where, where, first, ALU.add))
            then(nc.vector.tensor_scalar(both, m.PT1[:, 0:NBX], 0.5, float(N), ALU.is_gt, ALU.mult))
            nc.vector.tensor_tensor(m.goal[:], where, both, ALU.add)

        @block.scalar
        def _(act):
            if layer == 1:
                act.wait_ge(s.gap_ready, 1)
                nc.scalar.activation(m.st_b[:], m.st_a[:], ACT.Exp).then_inc(s.exp_done, 1)

        @block.tensor
        def _(pe):
            pe.wait_ge(s.marks_ready, 1)
            marks = m.marks[:].rearrange("p e t -> p (e t)")
            nc.tensor.matmul(m.bankA[:, 0:P], m.con["upper"], marks, start=True, stop=True).then_inc(s.sums_done, 1)
            nc.tensor.matmul(m.bankB[:, 0:P], m.ones[:], marks, start=True, stop=True).then_inc(s.sums_done, 1)

            for g in range(J // G):
                bank = (m.PT0, m.PT1)[g * G // T]
                pe.wait_ge(s.hot_ready, g + 1)
                for j in range(G):
                    out = nc.tensor.matmul(bank[:, 0:NBX], m.hot_slot[g % 2][:, j, :], m.hot_blk[g % 2][:, j, :],
                                           start=g * G % T + j == 0, stop=g * G % T + j == T - 1)
                out.then_inc(s.list_step, 1)


def mlp(nc, m, layer, W, gate=False, b1=None, b2=None):
    selu = layer == 3
    biased = b1 is not None
    func = {1: ACT.Gelu, 2: ACT.Gelu_apprx_tanh, 3: ACT.Exp}[layer]
    names = ["idx_ready", "xn_ready", "xT_done", "xgT_ready", "h_done", "z_ready", "z2_ready", "h_ready", "selu_ready",
             "hT_done", "hT_ready", "y_done", "y_ready", "top_done", "idx_done", "rows_out*"]
    H_, HT, Y = [m.S[i][:, 0:F] for i in range(2)], [m.S[i][:, F:2 * F] for i in range(2)], (m.PT0, m.PT1)
    live = inside if gate else (lambda u: not isinstance(u, int) or u >= 0)
    xg_in, y_out = m.gather_sems[layer, "xg_in"], m.gather_sems[layer, "y_out"]
    with sems(nc, f"{'g' if gate else 'm'}{layer}_", *names) as s, nc.Block() as block:
        def run(eng, step):
            if gate:
                return pipeline(eng, step, -4, T - 1, (2, 10))
            blocks = eng.value_load(m.nbi[0:1, 0:1], min_val=4, max_val=NB)
            for b in range(-4, 2):
                step(b, b % 2)
            with eng.Fori(2, blocks, 2) as i:
                step(i, 0)
                step(i + 1, 1)
            return blocks

        def experts(eng, b):
            both = eng.value_load(m.eb[0:1, tile_of(b + 2)], min_val=0, max_val=E * E - 1)
            return both % E, both // E

        @block.sync
        def _(sp):
            def step(b, p):
                u, q = b + 4, p
                if inside(u):
                    upto(sp, s.xn_ready, u)
                    sp.dma_start(m.XN[bass.ds(u * P, P), :], m.xn[q][:]).then_inc(s.rows_out[q], 16)
            if gate:
                run(sp, step)
                for q in range(2):
                    sp.wait_ge(s.rows_out[q], T // 2 * 16)
            else:
                blocks = sp.value_load(m.nbi[0:1, 0:1], min_val=4, max_val=NB)
                settle(sp, (y_out[0], blocks * 8), (y_out[1], blocks * 8))

        if not gate:
            @block.gpsimd
            def _(pool):
                def step(b, p):
                    u, q = b + 4, p
                    settle(pool, (s.idx_ready, u + 1), (s.xT_done, u - 1))
                    nc.gpsimd.indirect_dma_start(m.xg[q][:], None, m.XN, bass.IndirectOffsetOnAxis(ap=m.idx_t[q][:], axis=0))\
                        .then_inc(xg_in[q], 16)
                    if live(b):
                        settle(pool, (s.y_ready, b + 1))
                        nc.gpsimd.indirect_dma_start(m.YS, bass.IndirectOffsetOnAxis(ap=m.goal_t[p][:], axis=0), m.ys[p][:], None)\
                            .then_inc(y_out[p], 16)
                run(pool, step)

        @block.vector
        def _(dve):
            def step(b, p):
                u, q = b + 4, p
                if not gate:
                    if isinstance(u, int):
                        if u >= 2:
                            arrived(dve, xg_in, u - 2, q)
                    else:
                        arrived(dve, xg_in, u - 2, q)
                    nc.vector.tensor_copy(m.idx_t[q][:], m.tok[:, tile_of(u)]).then_inc(s.idx_ready, 1)
                elif inside(u):
                    upto(dve, s.xT_done, u - 2)
                    if isinstance(u, int):
                        if u >= 2:
                            dve.wait_ge(s.rows_out[q], (u // 2) * 16)
                    else:
                        dve.wait_ge(s.rows_out[q], (u - q) * 8)
                    nc.vector.tensor_scalar(m.xn[q][:], row(m.x, u), m.rstd[:, tile_of(u)], m.nmr[:, tile_of(u)],
                                            ALU.mult, ALU.add).then_inc(s.xn_ready, 1)
                u, q = b + 2, p
                if live(u) and biased:
                    if not gate:
                        e2, e1 = experts(dve, b)
                    bias = b1[:, 0:F] if gate else b1[:, bass.ds(e1 * F, F)]
                    upto(dve, s.h_done, u)
                    upto(dve, s.hT_done if selu else s.h_ready, u - 2)
                    if selu:
                        nc.vector.tensor_tensor(m.z[q][:], H_[q], bias, ALU.add).then_inc(s.z_ready, 1)
                        upto(dve, s.h_ready, u)
                        nc.vector.tensor_scalar(m.h[q][:], m.h[q][:], SELU_ALPHA, -SELU_ALPHA,
                                                ALU.min, ALU.add).then_inc(s.z2_ready, 1)
                        upto(dve, s.z2_ready, u)
                        nc.vector.scalar_tensor_tensor(m.h[q][:], m.z[q][:], 0.0, m.h[q][:], ALU.max, ALU.add).then_inc(s.selu_ready, 1)
                    else:
                        nc.vector.tensor_tensor(m.z[q][:], H_[q], bias, ALU.add).then_inc(s.z_ready, 1)
                if live(b):
                    upto(dve, s.y_done, b)
                    if gate:
                        nc.vector.scalar_tensor_tensor(m.lg128[:], Y[p][:, 0:D], SELU_SCALE, b2, ALU.mult, ALU.add).then_inc(s.y_ready, 1)
                        two_best(nc, m, dve, s, m.lg128[:], b, (s.y_ready, b + 1))
                    else:
                        if not isinstance(b, int) or b >= 2:
                            arrived(dve, y_out, b - 2, p)
                        nc.vector.tensor_copy(m.goal_t[p][:], m.goal[:, tile_of(b)])
                        if b2 is None:
                            nc.vector.tensor_copy(m.ys[p][:], Y[p][:, 0:D]).then_inc(s.y_ready, 1)
                        else:
                            nc.vector.scalar_tensor_tensor(m.ys[p][:], Y[p][:, 0:D], SELU_SCALE if selu else 1.0,
                                                           b2[:, bass.ds(e2 * D, D)], ALU.mult,
                                                           ALU.add).then_inc(s.y_ready, 1)
            if biased and not gate:
                dve.wait_ge(m.bias_in[layer], 32)
            run(dve, step)

        @block.scalar
        def _(act):
            def step(b, p):
                if live(b):
                    upto(act, s.hT_done, b)
                    upto(act, s.y_done, b - 1)
                    nc.scalar.copy(m.hT[:], HT[p]).then_inc(s.hT_ready, 1)
                u, q = b + 2, p
                if live(u):
                    upto(act, s.z_ready if biased else s.h_done, u)
                    upto(act, s.hT_done, u - 2)
                    if selu:
                        nc.scalar.activation(m.h[q][:], m.z[q][:], func, bias=m.ln_alpha[:, 0:1]).then_inc(s.h_ready, 1)
                    else:
                        nc.scalar.activation(m.h[q][:], m.z[q][:] if biased else H_[q], func).then_inc(s.h_ready, 1)
                u, q = b + 3, 1 - p
                if live(u):
                    upto(act, s.xT_done, u)
                    upto(act, s.h_done, u - 2)
                    nc.scalar.copy(m.xgT[q][:], m.bankA[:, 0:P]).then_inc(s.xgT_ready, 1)
            run(act, step)

        @block.tensor
        def _(pe):
            def step(b, p):
                if live(b):
                    upto(pe, s.selu_ready if selu else s.h_ready, b)
                    upto(pe, s.hT_ready, b - 2)
                    for k in range(FC):
                        out = nc.tensor.transpose(HT[p][:, k * P:(k + 1) * P], m.h[p][:, k * P:(k + 1) * P], m.ident)
                    out.then_inc(s.hT_done, 1)
                if not gate and live(b + 2):
                    e2, e1 = experts(pe, b)
                u, q = b + 2, p
                if live(u):
                    w1 = W[0] if gate else W[:, 0, bass.ds(e1 * F, F)]
                    upto(pe, s.xgT_ready, u)
                    upto(pe, s.z_ready if biased else s.h_ready, u - 2)
                    nc.tensor.matmul(H_[q], m.xgT[q][:], w1, start=True, stop=True).then_inc(s.h_done, 1)
                if live(b):
                    upto(pe, s.hT_ready, b)
                    upto(pe, s.y_ready, b - 2)
                    for k in range(FC):
                        w2 = W[1][:, k * D:(k + 1) * D] if gate else W[:, 1, bass.ds(e2 * F + k * D, D)]
                        out = nc.tensor.matmul(Y[p][:, 0:D], m.hT[:, k * P:(k + 1) * P], w2, start=(k == 0), stop=(k == FC - 1))
                    out.then_inc(s.y_done, 1)
                u, q = b + 3, 1 - p
                if live(u):
                    if gate:
                        upto(pe, s.xn_ready, u)
                    else:
                        arrived(pe, xg_in, u, q)
                    upto(pe, s.xgT_ready, u - 1)
                    nc.tensor.transpose(m.bankA[:, 0:P], (m.xn if gate else m.xg)[q][:], m.ident).then_inc(s.xT_done, 1)
            if not gate:
                pe.wait_ge(m.moe_in[layer], 16)
            run(pe, step)


def combine(nc, m, layer):
    halves = [m.probs, m.kexp]
    with sems(nc, f"k{layer}_", "y_in*", "x_chain") as s, nc.Block() as block:
        @block.sync
        def _(sp):
            for g in range(2):
                for k in range(2):
                    rows = slice(k * N + g * N // 2, k * N + (g + 1) * N // 2)
                    dst = halves[k][g][:] if k == 0 else halves[k][g][:].rearrange("p h k -> p (h k)")
                    sp.dma_start(dst.rearrange("p (t d) -> p t d", d=D),
                                 m.YS[rows, :].rearrange("(t p) d -> p t d", p=P)).then_inc(s.y_in[g], 16)

        @block.vector
        def _(dve):
            for g in range(2):
                ts = range(g * T // 2, (g + 1) * T // 2)
                dve.wait_ge(s.y_in[g], 32)
                for k in range(2):
                    for t in ts:
                        y = halves[k][g][:, (t % HALF) * D:(t % HALF + 1) * D] if k == 0 else halves[k][g][:, t % HALF, :]
                        out = nc.vector.scalar_tensor_tensor(m.x[:, t, :], y, m.wt[:, k, t:t + 1], m.x[:, t, :], ALU.mult, ALU.add)
                    out.then_inc(s.x_chain, 1)
                    dve.wait_ge(s.x_chain, 2 * g + k + 1)
                for t in ts:
                    nc.vector.bn_stats(m.bn6[:, t, :], m.x[:, t, :])


W_NAMES = ["q0", "k0", "v0", "o0", "q1", "k1", "v1", "o1", "g2", "v2", "o2", "qk2", "q3", "k3", "v3", "o3"]
COL_NAMES = ["g_pre", "b_pre", "bq2", "bq3", "bk3", "bv3"]
ROW_SIZES = {"g_ln": D, "b_ln": D, "bo1": D, "bg2": D, "bv2": D, "bk2": D // 2, "bo2": D, "bo3": D,
             "gate_bi": F, "gate_bo": D}
ROW_AT = {}
_at = 0
for _n, _k in ROW_SIZES.items():
    ROW_AT[_n] = (_at, _at + _k)
    _at += _k
ROWS = _at
C_SIZES = {"ident": P, "head_mask": HALF, "upper": P, "expert": E, "tile128": T, "block": NBX, "slot": P,
           "token": T, "keep": P, "spare": NBX}
C_AT = {}
_at = 0
for _n, _k in C_SIZES.items():
    C_AT[_n] = (_at, _at + _k)
    _at += _k
CONSTS = _at


def program(nc, a, out, stop=99):
    with ExitStack() as c:
        def sb(name, shape, dt=F32):
            return c.enter_context(nc.sbuf_tensor(name, shape, dt))

        m = Memory()
        numbers = iter(GATHER_NUMBERS)
        gather_sems = {(layer, n): [c.enter_context(nc.semaphore(f"{n}{layer}_{i}", num=next(numbers))) for i in range(2)]
                       for layer in (1, 2, 3) for n in ("xg_in", "y_out")}
        m.gather_sems = gather_sems
        numbers = iter(PREFETCH_NUMBERS)
        m.moe_in = {layer: c.enter_context(nc.semaphore(f"moe{layer}_in", num=next(numbers))) for layer in (1, 2, 3)}
        m.bias_in = {layer: c.enter_context(nc.semaphore(f"bias{layer}_in", num=next(numbers))) for layer in (2, 3)}
        m.router_in = c.enter_context(nc.semaphore("router_in", num=next(numbers)))
        m.x, m.ctx = sb("x", [P, T, D]), sb("ctx", [P, T, D])
        m.wts = sb("wts", [P, len(W_NAMES), P])
        m.cols = sb("cols", [P, len(COL_NAMES)])
        m.rows = sb("rows", [P, ROWS])
        m.consts = sb("consts", [P, CONSTS])
        m.gates = sb("gates", [P, 8])
        m.tg = sb("tg", [P, 8])
        m.bn6, m.cbn6 = sb("bn6", [P, T, 6]), sb("cbn6", [P, T, 6])
        m.rstd, m.nmr, m.crstd, m.cnmr, m.st_a, m.st_b, m.st_c, m.st_d, m.st_e, m.minus_half = (
            sb(n, [P, T]) for n in ("rstd", "nmr", "crstd", "cnmr", "st_a", "st_b", "st_c", "st_d", "st_e", "minus_half"))
        two = lambda n, shape, dt=F32: [sb(f"{n}{i}", shape, dt) for i in range(2)]
        m.ctx_t, m.xn, m.cn, m.xnT, m.cnT = (two(n, [P, P]) for n in ("ctx_t", "xn", "cn", "xnT", "cnT"))
        m.qT, m.kT, m.os, m.raw = (two(n, [P, P]) for n in ("qT", "kT", "os", "raw"))
        m.kexp = two("kexp", [P, HALF, P])
        m.vexp = two("vexp", [P, 2, CH * VW])
        m.probs = two("probs", [P, 2 * F])
        m.PTs, m.oT = sb("PTs", [P, 2 * F]), sb("oT", [P, P])
        m.rowmax = two("rowmax", [P, H])
        m.rden = sb("rden", [P, H])
        m.obn, m.omv, m.ovar, m.orstd = sb("obn", [P, 6]), two("omv", [P, 2]), two("ovar", [P, 1]), two("orstd", [P, 1])
        m.mask_t, m.pred = two("mask_t", [P, S], I32), two("pred", [P, S], I32)
        m.negs = sb("negs", [P, S])
        m.xb, m.xqT = sb("xb", [P, F], BF16), sb("xqT", [P, F], BF16)
        m.yb, m.yb2 = sb("yb", [P, FC, D], BF16), sb("yb2", [P, FC, D], BF16)
        m.small8, m.big8, m.over = sb("small8", [P, F], FP8), sb("big8", [P, F], FP8), sb("over", [P, F], I32)
        m.tgn, m.settled = sb("tgn", [P, T]), sb("settled", [P, 1])
        m.kraw, m.kq, m.bias0 = sb("kraw", [P, D], BF16), sb("kq", [P, D], BF16), sb("bias0", [P, D], BF16)
        m.scales, m.rks = sb("scales", [P, 4]), sb("rks", [P, 1])
        m.kmask8, m.kmask, m.qgate = sb("kmask8", [P, T], U8), sb("kmask", [P, T]), sb("qgate", [P, T])
        m.kb, m.vb, m.ub, m.zr, m.qr = sb("kb", [P, D // 2]), sb("vb", [P, D]), sb("ub", [P, D]), sb("zr", [P, 1]), sb("qr", [P, S])
        m.kk, m.va, m.us, m.ua, m.qq, m.kvs = (two(n, [P, k]) for n, k in (("kk", D // 2), ("va", D + 1), ("us", D), ("ua", D), ("qq", S), ("kvs", D + 1)))
        m.lg, m.lp = sb("lg", [P, T, E]), sb("lp", [P, T, E])
        m.tops, m.idxs = sb("tops", [P, T, 8]), sb("idxs", [P, T, 8], U32)
        m.lg128 = sb("lg128", [P, D])
        m.top, m.idx = sb("top", [P, E]), sb("idx", [P, E], U32)
        m.tv, m.ti, m.wt = sb("tv", [P, 2, T]), sb("ti", [P, 2, T]), sb("wt", [P, 2, T])
        m.hot = two("hot", [P, E, T])
        m.marks, m.tot, m.incl, m.pos = (sb(n, [P, E, T]) for n in ("marks", "tot", "incl", "pos"))
        m.nb, m.cum, m.base = sb("nb", [P, E]), sb("cum", [P, E]), sb("base", [P, E])
        m.dest, m.valid, m.blk, m.slot = (sb(n, [P, 2, T]) for n in ("dest", "valid", "blk", "slot_of"))
        m.desti, m.blki = sb("desti", [P, 2, T], I32), sb("blki", [P, 2, T], I32)
        m.nbf, m.nbi = sb("nbf", [P, 1]), sb("nbi", [P, 1], I32)
        m.ebc, m.ebf, m.eb, m.tok = sb("ebc", [P, E, NBX]), sb("ebf", [P, NBX]), sb("eb", [P, NBX], I32), sb("tok", [P, NBX], I32)
        m.hot_slot, m.hot_blk = two("hot_slot", [P, T // 2, P], F16), two("hot_blk", [P, T // 2, NBX], F16)
        m.hot_f, m.goal = sb("hot_f", [P, T // 2, NBX]), sb("goal", [P, NBX], I32)
        m.ones, m.ln_alpha = sb("ones", [P, P]), sb("ln_alpha", [P, 1])
        m.xg, m.xgT, m.ys, m.idx_t = two("xg", [P, D]), two("xgT", [P, P]), two("ys", [P, D]), two("idx_t", [P, 1], I32)
        m.goal_t = two("goal_t", [P, 1], I32)
        m.z, m.h = [pr[:, 0:F] for pr in m.probs], [pr[:, F:2 * F] for pr in m.probs]
        m.hT = m.PTs[:, 0:F]
        m.yg = [two("yg0", [P, D]), two("yg1", [P, D])]
        m.cidx = two("cidx", [P, 2], I32)
        m.router_w = sb("router_w", [P, 2, E])
        m.gate_w = sb("gate_w", [P, 2, F])
        m.b1, m.b2 = sb("b1", [P, E * F]), sb("b2", [P, E * D])
        m.XN = nc.dram_tensor("XN", [N, D], F32, kind="Internal").ap()
        m.YS = nc.dram_tensor("YS", [2 * N + NBX * P, D], F32, kind="Internal").ap()
        m.WA, m.WB = sb("WA", [P, 2, E * F]), sb("WB", [P, 2, E * F])
        m.za = m.WB[:, 0, 0:T * D].rearrange("p (t d) -> p t d", d=D)
        m.ola = m.WB[:, 1, 0:T * D].rearrange("p (t d) -> p t d", d=D)
        m.S = [c.enter_context(nc.psum_tensor(f"S{i}", [P, 2 * F], F32)) for i in range(2)]
        m.PT0, m.PT1, m.bankA, m.bankB = (c.enter_context(nc.psum_tensor(n, [P, F], F32)) for n in ("PT0", "PT1", "bankA", "bankB"))
        m.ctxT_dram, m.mask_dram = a["ctxT"], a["mask"]
        w = {n: m.wts[:, i, :] for i, n in enumerate(W_NAMES)}
        col = {n: m.cols[:, i:i + 1] for i, n in enumerate(COL_NAMES)}
        rowv = {n: m.rows[:, i:j] for n, (i, j) in ROW_AT.items()}
        con = {n: m.consts[:, i:j] for n, (i, j) in C_AT.items()}
        m.con = con
        m.ident, m.head_mask = con["ident"], con["head_mask"]
        m.g_pre, m.b_pre, m.g_ln, m.b_ln = col["g_pre"], col["b_pre"], rowv["g_ln"], rowv["b_ln"]
        tg = lambda i: m.tg[:, i:i + 1]

        with sems(nc, "s_", "x_in", "ctx_in", "w_in", "small_in", "zeroed", "zero_ready", "ys_out", "ready", "chain", "quant") as s, nc.Block() as block:
            @block.sync
            def _(sp):
                sp.dma_start(m.x[:], a["x"].rearrange("(t p) d -> p t d", p=P)).then_inc(s.x_in, 16)
                sp.dma_start(m.ctx[:], a["ctx"].rearrange("(t p) d -> p t d", p=P)).then_inc(s.ctx_in, 16)
                sp.dma_start(m.wts[:].rearrange("p a b -> p (a b)"), a["wts"]).then_inc(s.w_in, 16)
                sp.wait_ge(s.zero_ready, 1)
                sp.dma_start(m.YS[0:2 * N, :].rearrange("(b p) d -> p b d", p=P),
                             m.xg[0][:].unsqueeze(1).to_broadcast([P, 2 * T, D])).then_inc(s.ys_out, 16)
                sp.wait_ge(s.w_in, 16)
                sp.wait_ge(s.ys_out, 16)

            @block.scalar
            def _(act):
                act.dma_start(m.gates[:], a["gates"].partition_broadcast(P)).then_inc(s.small_in, 16)
                act.dma_start(m.cols[:], a["cols"]).then_inc(s.small_in, 16)
                act.dma_start(m.rows[:], a["rows"].partition_broadcast(P)).then_inc(s.small_in, 16)
                act.dma_start(m.consts[:], a["consts"]).then_inc(s.small_in, 16)
                act.dma_start(m.kraw[:], a["kernel0"]).then_inc(s.small_in, 16)
                act.dma_start(m.bias0[:], a["bias0"].partition_broadcast(P)).then_inc(s.small_in, 16)
                act.dma_start(m.scales[:, 0:2], a["scales"].partition_broadcast(P)).then_inc(s.small_in, 16)
                act.dma_start(m.kmask8[:], a["kmask"]).then_inc(s.small_in, 16)
                act.wait_ge(s.small_in, 128)
                nc.scalar.activation(m.tg[:], m.gates[:], ACT.Tanh).then_inc(s.ready, 1)

            @block.gpsimd
            def _(pool):
                nc.gpsimd.memset(m.xg[0][:], 0.0).then_inc(s.zero_ready, 1)
                nc.gpsimd.memset(m.minus_half[:], -0.5)
                nc.gpsimd.memset(m.ones[:], 1.0)
                nc.gpsimd.memset(m.ln_alpha[:], math.log(SELU_ALPHA))
                nc.gpsimd.memset(m.negs[:], NEG * DH ** 0.5)
                for i in range(2):
                    nc.gpsimd.memset(m.vexp[i][:], 0.0).then_inc(s.zeroed, 1)
                pool.wait_ge(s.zeroed, 2)
                for i in range(2):
                    v = m.vexp[i][:].rearrange("p b (c e d) -> p b c e d", c=CH, e=2)
                    for hh in range(2):
                        nc.gpsimd.memset(v[64 * hh:64 * hh + 64, :, :, hh, DH:DH + 1], 1.0)

            @block.vector
            def _(dve):
                dve.wait_ge(s.x_in, 16)
                for t in range(T):
                    nc.vector.bn_stats(m.bn6[:, t, :], m.x[:, t, :])
                dve.wait_ge(s.ctx_in, 16)
                for t in range(T):
                    nc.vector.bn_stats(m.cbn6[:, t, :], m.ctx[:, t, :])
                dve.wait_ge(s.ready, 1)
                for i, n in ((1, "bo1"), (3, "bo3")):
                    nc.vector.tensor_scalar(rowv[n], rowv[n], tg(i), None, ALU.mult)
                count = [0]

                def done(ins):
                    count[0] += 1
                    ins.then_inc(s.chain, 1)

                def wait():
                    dve.wait_ge(s.chain, count[0])
                done(nc.vector.tensor_copy(m.kmask[:], m.kmask8[:]))
                wait()
                nc.vector.tensor_scalar(m.qgate[:], m.kmask[:], tg(2), None, ALU.mult)
                done(nc.vector.reciprocal(m.scales[:, 2:3], m.scales[:, 0:1]))
                done(nc.vector.reciprocal(m.rks[:], m.scales[:, 1:2]))
                done(nc.vector.scalar_tensor_tensor(m.scales[:, 3:4], m.scales[:, 0:1], 4.0, m.scales[:, 1:2], ALU.mult, ALU.mult))
                wait()
                v, half, square = m.xn[0][:], m.xn[1][:], m.cn[0][:]
                done(nc.vector.tensor_scalar(v, m.kraw[:], m.rks[:], None, ALU.mult))
                wait()
                nc.vector.tensor_scalar(half, v, 0.5, None, ALU.mult)
                done(nc.vector.tensor_tensor(square, v, v, ALU.mult))
                wait()
                quantize(nc, dve, s.quant, 0, m, v, half, square, m.cn[1][:], m.xnT[0][:])
                nan = m.xnT[1][:]
                done(nc.vector.tensor_scalar(nan, square, 464.0 ** 2, 3e38, ALU.is_gt, ALU.mult))
                wait()
                done(nc.vector.tensor_scalar(nan, nan, 1e5, 0.0, ALU.mult, ALU.mult))
                wait()
                dve.wait_ge(s.quant, 4)
                nc.vector.tensor_tensor(m.kq[:], m.xnT[0][:], nan, ALU.add)

        batch_stats(nc, m, "c0_", m.cbn6, m.crstd, m.cnmr)
        batch_stats(nc, m, "x0_", m.bn6, m.rstd, m.nmr, double=True)
        attention(nc, m, 0, w["q0"], w["k0"], w["v0"], w["o0"])
        xattn0_tail(nc, m, tg(0))

        def finish():
            with sems(nc, "e_", "out") as s, nc.Block() as block:
                @block.sync
                def _(sp):
                    sp.dma_start(out.rearrange("(t p) d -> p t d", p=P), m.x[:]).then_inc(s.out, 16)
                    sp.wait_ge(s.out, 16)

        flat = lambda tensor: tensor[:].rearrange("p a b -> p (a b)")

        def fetch_moe12(sp):
            sp.dma_start(flat(m.router_w), a["router_w"]).then_inc(m.router_in, 16)
            sp.dma_start(flat(m.gate_w), a["gate_w"]).then_inc(m.router_in, 16)
            sp.dma_start(flat(m.WA), a["moe1"]).then_inc(m.moe_in[1], 16)
            sp.dma_start(flat(m.WB), a["moe2"]).then_inc(m.moe_in[2], 16)
            sp.dma_start(m.b1[:], a["b1_2"].partition_broadcast(P)).then_inc(m.bias_in[2], 16)
            sp.dma_start(m.b2[:], a["b2_2"].partition_broadcast(P)).then_inc(m.bias_in[2], 16)

        def fetch_moe3(sp):
            sp.dma_start(flat(m.WA), a["moe3"]).then_inc(m.moe_in[3], 16)

        def fetch_bias3(sp):
            sp.dma_start(m.b1[:], a["b1_3"].partition_broadcast(P)).then_inc(m.bias_in[3], 16)
            sp.dma_start(m.b2[:], a["b2_3"].partition_broadcast(P)).then_inc(m.bias_in[3], 16)

        if stop == 0:
            return finish()
        batch_stats(nc, m, "x1_", m.bn6, m.rstd, m.nmr)
        ffn0(nc, m, tg(4), fetch_moe12)
        if stop == 1:
            return finish()
        batch_stats(nc, m, "x2_", m.bn6, m.rstd, m.nmr)
        attention(nc, m, 1, w["q1"], w["k1"], w["v1"], w["o1"], tg=tg(1), out_bias=rowv["bo1"])
        if stop == 2:
            return finish()
        batch_stats(nc, m, "x3_", m.bn6, m.rstd, m.nmr)
        router(nc, m, 1, m.router_w[:, 0, :])
        dispatch(nc, m, 1, tg(5))
        mlp(nc, m, 1, m.WA)
        combine(nc, m, 1)
        if stop == 3:
            return finish()
        batch_stats(nc, m, "x4_", m.bn6, m.rstd, m.nmr)
        linear_attention(nc, m, w["g2"], w["v2"], w["o2"], w["qk2"][:, 0:64], w["qk2"][:, 64:128],
                         rowv["bg2"], rowv["bv2"], rowv["bk2"], col["bq2"], rowv["bo2"], fetch_moe3)
        if stop == 4:
            return finish()
        batch_stats(nc, m, "x5_", m.bn6, m.rstd, m.nmr)
        router(nc, m, 2, m.router_w[:, 1, :])
        dispatch(nc, m, 2, tg(6))
        mlp(nc, m, 2, m.WB, b1=m.b1, b2=m.b2)
        combine(nc, m, 2)
        if stop == 5:
            return finish()
        batch_stats(nc, m, "x6_", m.bn6, m.rstd, m.nmr)
        attention(nc, m, 3, w["q3"], w["k3"], w["v3"], w["o3"], bq=col["bq3"], bk=col["bk3"], bv=col["bv3"],
                  tg=tg(3), out_bias=rowv["bo3"], fetch=fetch_bias3)
        if stop == 6:
            return finish()
        batch_stats(nc, m, "x7_", m.bn6, m.rstd, m.nmr)
        mlp(nc, m, 3, [m.gate_w[:, 0, :], m.gate_w[:, 1, :]], gate=True, b1=rowv["gate_bi"], b2=rowv["gate_bo"])
        dispatch(nc, m, 3, tg(7))
        mlp(nc, m, 3, m.WA, b1=m.b1, b2=m.b2)
        combine(nc, m, 3)
        finish()


def layouts(i):
    import numpy as np
    i = {k: np.asarray(v) for k, v in i.items()}
    f = np.float32
    x, ctx = i["x"].reshape(N, D), i["ctx_1024"].reshape(N, D)
    wq2k2 = np.concatenate([i["L2_xattn_Wq"].T, i["L2_xattn_Wk"].T], axis=1)
    w = {"q0": i["L0_xattn_Wq"].T, "k0": i["L0_xattn_Wk"].T, "v0": i["L0_xattn_Wv"].T, "o0": i["L0_xattn_Wo"].T,
         "q1": i["L1_xattn_W_q"].T, "k1": i["L1_xattn_W_k"].T, "v1": i["L1_xattn_W_v"].T, "o1": i["L1_xattn_W_o"].T,
         "g2": i["L2_xattn_Wg"].T, "v2": i["L2_xattn_Wv"].T, "o2": i["L2_xattn_Wo"].T, "qk2": wq2k2,
         "q3": i["L3_xattn_wq_w"].T, "k3": i["L3_xattn_wk_w"].T, "v3": i["L3_xattn_wv_w"].T, "o3": i["L3_xattn_wo_w"].T}
    cols = {"g_pre": i["L0_xattn_g_pre"], "b_pre": i["L0_xattn_b_pre"], "bq2": np.tile(i["L2_xattn_bq"], 2),
            "bq3": i["L3_xattn_wq_b"], "bk3": i["L3_xattn_wk_b"], "bv3": i["L3_xattn_wv_b"]}
    rows = {"g_ln": i["L0_xattn_g_ln"], "b_ln": i["L0_xattn_b_ln"], "bo1": i["L1_xattn_b_o"], "bg2": i["L2_xattn_bg"],
            "bv2": i["L2_xattn_bv"], "bk2": i["L2_xattn_bk"], "bo2": i["L2_xattn_bo"], "bo3": i["L3_xattn_wo_b"],
            "gate_bi": i["L3_ffn_gate_bi"], "gate_bo": i["L3_ffn_gate_bo"]}
    one = lambda n: np.arange(n, dtype=f)[None, :].repeat(P, 0)
    consts = {"ident": np.eye(P, dtype=f), "head_mask": ((np.arange(P)[:, None] % 64) // DH == np.arange(HALF)).astype(f),
              "upper": np.triu(np.ones((P, P), f), 1), "expert": one(E), "tile128": one(T) * P, "block": one(NBX),
              "slot": one(P), "token": one(T) * P + np.arange(P, dtype=f)[:, None] + 1,
              "spare": 2 * N + one(NBX) * P + np.arange(P, dtype=f)[:, None],
              "keep": (np.arange(P) % T != 0).astype(f)[None, :].repeat(P, 0)}

    def moe(w1, w2):
        return np.concatenate([w1.transpose(1, 0, 2).reshape(P, E * F),
                               w2.reshape(E, FC, P, D).transpose(2, 0, 1, 3).reshape(P, E * F)], axis=1)

    return {"x": x, "ctx": ctx, "ctxT": ctx.T, "wts": np.stack([w[n] for n in W_NAMES], 1).reshape(P, -1),
            "cols": np.stack([cols[n] for n in COL_NAMES], 1), "rows": np.concatenate([rows[n] for n in ROW_SIZES]),
            "consts": np.concatenate([consts[n] for n in C_SIZES], axis=1),
            "gates": np.concatenate([i["g_xattn"], i["g_ffn"]]),
            "mask": i["mask_BxSxS2_ik1"].reshape(N, S),
            "kernel0": i["L0_ffn_kernel"], "bias0": i["L0_ffn_bias"],
            "scales": np.concatenate([i["L0_ffn_input_scale"], i["L0_ffn_kernel_scale"]]),
            "kmask": i["mask_BxS2_bf1"].view(np.uint8).reshape(T, P).T,
            "router_w": np.concatenate([i["L1_ffn_router_w"].T, i["L2_ffn_w_router"]], axis=1),
            "gate_w": np.concatenate([i["L3_ffn_gate_wi"], i["L3_ffn_gate_wo"].reshape(FC, P, D).transpose(1, 0, 2).reshape(P, F)], axis=1),
            "moe2": moe(i["L2_ffn_w1"], i["L2_ffn_w2"]), "moe3": moe(i["L3_ffn_exp_wi"], i["L3_ffn_exp_wo"]),
            "b1_2": i["L2_ffn_b1"].reshape(-1), "b2_2": i["L2_ffn_b2"].reshape(-1),
            "b1_3": i["L3_ffn_exp_bi"].reshape(-1), "b2_3": i["L3_ffn_exp_bo"].reshape(-1),
            "moe1": moe(i["L1_ffn_expert_w1"].transpose(0, 2, 1), i["L1_ffn_expert_w2"].transpose(0, 2, 1)),
            }


def kernel(**inputs):
    import numpy as np
    import concourse.bacc as bacc
    from concourse.bass_utils import run_bass_kernel_spmd

    nc = bacc.Bacc("TRN2", target_bir_lowering=False, num_devices=1)
    arrays, aps = {}, {}
    for name, array in layouts(inputs).items():
        array = np.ascontiguousarray(array)
        arrays[f"in_{name}"] = array
        aps[name] = nc.dram_tensor(f"in_{name}", array.shape, mybir.dt.from_np(array.dtype), kind="ExternalInput").ap()
    out = nc.dram_tensor("out_x", (N, D), F32, kind="ExternalOutput").ap()
    program(nc, aps, out)
    result = run_bass_kernel_spmd(nc, [arrays], core_ids=[0])
    return result.results[0]["out_x"].reshape(B, S, D)
```

```python
import itertools
import math

import concourse.bass as bass
from concourse import mybir
from collections import namedtuple
from contextlib import ExitStack, contextmanager

F32, BF16, F16, I32, U32, U8, FP8 = (mybir.dt.float32, mybir.dt.bfloat16, mybir.dt.float16,
                                 mybir.dt.int32, mybir.dt.uint32, mybir.dt.uint8, mybir.dt.float8e4)
ACT, ALU = mybir.ActivationFunctionType, mybir.AluOpType
AX_X = mybir.AxisListType.X

B, S, D, H, DH = 32, 64, 128, 16, 8
P = 128
N = B * S
T = N // P
E, F = 8, 512
FC = F // P
HALF = H // 2
VW = 2 * (DH + 1)
CH = H // 2
PAIRS = 2 * N
NB = PAIRS // P + E
NBX = NB + 8
LN_EPS = 1e-5
NEG = -1000000000.0
SELU_SCALE = 1.0507009873554804934193349852946
SELU_ALPHA = 1.6732632423543772848170429916717
KV_EPS = 1e-6
SEM_NUMBERS = itertools.cycle((range(110, 150), range(160, 200)))
GATHER_NUMBERS = range(210, 228)
PREFETCH_NUMBERS = range(230, 240)


def upto(engine, sem, tile, per=1):
    if isinstance(tile, int) and tile < 0:
        return
    engine.wait_ge(sem, (tile + 1) * per)


def settle(engine, *waits):
    waits = [(sem, value) for sem, value in waits if not isinstance(value, int) or value > 0]
    if any(not isinstance(value, int) for _, value in waits):
        waits = [(sem, value if isinstance(value, int) else engine.snap(value)) for sem, value in waits]
        for _, value in waits:
            if not isinstance(value, int):
                engine.compute_val(value)
        engine.wait_ge(waits[0][0], 1)
    for sem, value in waits:
        engine.wait_ge(sem, value)


def arrived(engine, sems_, u, q):
    engine.wait_ge(sems_[q], (u - q) * 8 + 16)


def inside(u):
    return not isinstance(u, int) or 0 <= u < T


class Memory:
    pass


@contextmanager
def sems(nc, prefix, *names):
    numbers = next(SEM_NUMBERS)
    free = iter(numbers)
    with ExitStack() as c:
        one = lambda n: c.enter_context(nc.semaphore(prefix + n, num=next(free)))
        Semaphores = namedtuple("Semaphores", [n.rstrip("*") for n in names])
        yield Semaphores(*([one(f"{n[:-1]}{i}") for i in range(2)] if n.endswith("*") else one(n) for n in names))
        nc.sync.sem_clear(numbers)


def row(tensor, t):
    return tensor[:, tile_of(t), :].rearrange("p a d -> p (a d)")


def tile_of(t):
    return bass.ds(t, 1) if not isinstance(t, int) else slice(t, t + 1)


def pipeline(eng, step, first, last, steady):
    lo, hi = steady
    for t in range(first, lo):
        step(t, t % 2)
    with eng.Fori(lo, hi, 2) as i:
        step(i, lo % 2)
        step(i + 1, (lo + 1) % 2)
    for t in range(hi, last + 1):
        step(t, t % 2)


def load_table(nc, m, func):
    nc.scalar.activation(m.primed[:], m.ln_alpha[:], func)


def warm_up(nc, m, count):
    for _ in range(count):
        nc.tensor.matmul(m.S[0][:, 0:F], m.ident, m.wts[:, 0:4, :].rearrange("p a b -> p (a b)"), start=True, stop=True)


STATS = ["bn_done", "stats", "var_ready", "pow_done"]


def row_stats(nc, dve, s, w, bn6, ts, g, double=False):
    sm, df, sq, var = w.sum[:, ts], w.diff[:, ts], w.square[:, ts], w.var[:, ts]
    even, odd = bn6[:, ts, 0:3], bn6[:, ts, 3:6]
    dve.wait_ge(s.bn_done, g + 1)
    nc.vector.tensor_tensor(sm, even[:, :, 1], odd[:, :, 1], ALU.add)
    nc.vector.tensor_tensor(var, even[:, :, 2], odd[:, :, 2], ALU.add)
    nc.vector.tensor_tensor(df, even[:, :, 1], odd[:, :, 1], ALU.subtract).then_inc(s.stats, 1)
    dve.wait_ge(s.stats, 3 * g + 1)
    nc.vector.scalar_tensor_tensor(sq, df, 0.25, df, ALU.mult, ALU.mult).then_inc(s.stats, 1)
    dve.wait_ge(s.stats, 3 * g + 2)
    nc.vector.scalar_tensor_tensor(var, var, 1.0 / D, sq, ALU.mult, ALU.add).then_inc(s.stats, 1)
    dve.wait_ge(s.stats, 3 * g + 3)
    nc.vector.tensor_scalar(w.base[:, ts], var, 1.0 + LN_EPS if double else 1.0, LN_EPS ** 2 if double else LN_EPS,
                            ALU.mult, ALU.add).then_inc(s.var_ready, 1)


def row_powers(nc, pool, s, m, groups):
    for g in range(groups):
        ts = slice(g * T // groups, (g + 1) * T // groups)
        pool.wait_ge(s.var_ready, g + 1)
        nc.gpsimd.tensor_tensor(m.rstd[:, ts], m.work.base[:, ts], m.minus_half[:, ts], ALU.pow).then_inc(s.pow_done, 1)


def row_offsets(nc, dve, s, m, groups):
    dve.wait_ge(s.pow_done, groups)
    nc.vector.scalar_tensor_tensor(m.nmr[:], m.work.sum[:], -0.5, m.rstd[:], ALU.mult, ALU.mult)


def batch_stats(nc, m, name):
    with sems(nc, name, *STATS) as s, nc.Block() as block:
        @block.vector
        def _(dve):
            nc.vector.tensor_copy(m.settled[:], m.minus_half[:, 0:1]).then_inc(s.bn_done, 1)
            row_stats(nc, dve, s, m.work, m.bn6, slice(0, T), 0)
            row_offsets(nc, dve, s, m, 1)

        @block.gpsimd
        def _(pool):
            row_powers(nc, pool, s, m, 1)

        @block.tensor
        def _(pe):
            warm_up(nc, m, 4)


def attention(nc, m, layer, wq, wk, wv, wo, bq=0.0, bk=0.0, bv=None, tg=None, out_bias=None, fetch=None):
    L0, L1 = layer == 0, layer == 1
    lag = 2 if L0 else 1
    scale = 1.0 / D ** 0.5 if L0 else 1.0 / DH ** 0.5
    clip = 10000.0 / scale
    PT, A, QKV = (m.PT0, m.PT1), m.bankA, m.bankB
    names = ["ctx_in*", "mask_in*", "xn_ready", "xT_done", "xnT_ready", "qk_done", "v_done", "k_out", "v_out",
             "kexp_ready", "scores_done", "pred", "masked", "max_done", "clipped", "sub_done", "exp_done",
             "pt_done", "pt_out", "pv_done", "rec_done", "raw_ready", "stats_done", "var_ready", "pow_done", "hat_done", "scaled_done", "ola_ready",
             "o_ready", "oT_done", "oT_ready", "out_done", "x_done"]
    first, last = -4, T - 1 + lag
    steady = (3, 11)
    with ExitStack() as c:
        s = c.enter_context(sems(nc, f"a{layer}_", *names))
        block = c.enter_context(nc.Block())

        @block.sync
        def _(sp):
            def step(t, p):
                u, q = t + 3, 1 - p
                if inside(u):
                    upto(sp, s.v_done, u - 2)
                    sp.dma_start(m.ctx_t[q][:], m.ctxT2_dram[:, bass.ds(u * 2 * P, 2 * P)]).then_inc(s.ctx_in[q], 16)
                    if L1:
                        upto(sp, s.pred, u - 2)
                        sp.dma_start(m.mask_t[q][:], m.mask_dram[bass.ds(u * P, P), :]).then_inc(s.mask_in[q], 16)
                    if fetch is not None:
                        fetch(sp, u)
            pipeline(sp, step, first, last, steady)

        @block.vector
        def _(dve):
            def soften(u, q):
                if not inside(u):
                    return
                if L1:
                    arrived(dve, s.mask_in, u, q)
                    nc.vector.tensor_scalar(m.pred[q][:], m.mask_t[q][:], 0, None, ALU.is_equal).then_inc(s.pred, 1)
                for b in range(2):
                    sc = m.S[q][:, b * F:(b + 1) * F].rearrange("p (h k) -> p h k", k=S)
                    pr = m.probs[q][:, b * F:(b + 1) * F].rearrange("p (h k) -> p h k", k=S)
                    mx = m.rowmax[q][:, b * HALF:(b + 1) * HALF]
                    if not L1:
                        dve.wait_ge(s.scores_done, u * 2 + b + 1)
                    else:
                        settle(dve, (s.scores_done, u * 2 + b + 1), (s.pred, u + 1))
                        nc.vector.copy_predicated(sc, m.pred[q][:, b * S:(b + 1) * S].unsqueeze(1).to_broadcast([P, HALF, S]),
                                                  m.negs[:].unsqueeze(1).to_broadcast([P, HALF, S])).then_inc(s.masked, 1)
                        dve.wait_ge(s.masked, u * 2 + b + 1)
                    nc.vector.tensor_reduce(mx, sc, AX_X, ALU.max).then_inc(s.max_done, 1)
                    dve.wait_ge(s.max_done, u * 2 + b + 1)
                    if b == 0:
                        upto(dve, s.pt_done, u - 2, 2)
                    rows = mx.unsqueeze(2).to_broadcast([P, HALF, S])
                    if L0:
                        nc.vector.tensor_scalar(mx, mx, -clip, clip, ALU.max, ALU.min).then_inc(s.clipped, 1)
                        dve.wait_ge(s.clipped, u * 2 + b + 1)
                        nc.vector.scalar_tensor_tensor(pr, sc, -clip, rows, ALU.max, ALU.subtract).then_inc(s.sub_done, 1)
                    else:
                        nc.vector.tensor_tensor(pr, sc, rows, ALU.subtract).then_inc(s.sub_done, 1)

            def clip_top(t, p):
                if not (L0 and inside(t)):
                    return
                for r in range(2):
                    dve.wait_ge(s.pt_done, t * 2 + r + 1)
                    if r == 0:
                        upto(dve, s.pv_done, t - 1)
                    nc.vector.tensor_scalar(m.PTs[:, r * F:(r + 1) * F], PT[r][:], 1.0, None,
                                            ALU.min).then_inc(s.pt_out, 1)

            def normal_output(u, q):
                if not (L0 and inside(u)):
                    return
                upto(dve, s.pow_done, u)
                upto(dve, s.stats_done, u, 2)
                upto(dve, s.o_ready, u - 1)
                nc.vector.tensor_scalar(m.hat[:], m.raw[q][:], m.omv[q][:, 0:1], m.orstd[q][:],
                                        ALU.subtract, ALU.mult).then_inc(s.hat_done, 1)

            def average(t, p):
                if not inside(t):
                    return
                o = m.PT0[:, 0:H * (DH + 1)].rearrange("p (h e) -> p h e", e=DH + 1)
                upto(dve, s.pv_done, t)
                nc.vector.reciprocal(m.rden[:], o[:, :, DH]).then_inc(s.rec_done, 1)
                upto(dve, s.rec_done, t)
                if L0:
                    upto(dve, s.hat_done, t - 2)
                else:
                    upto(dve, s.oT_done, t - 2)
                dst = (m.raw if L0 else m.os)[p][:]
                nc.vector.tensor_tensor(dst.rearrange("p (h d) -> p h d", d=DH), o[:, :, 0:DH],
                                        m.rden[:].unsqueeze(2).to_broadcast([P, H, DH]),
                                        ALU.mult).then_inc(s.raw_ready if L0 else s.o_ready, 1)
                if L0:
                    upto(dve, s.raw_ready, t)
                    nc.vector.bn_stats(m.obn[:], m.raw[p][:]).then_inc(s.stats_done, 1)
                    settle(dve, (s.stats_done, 2 * t + 1))
                    nc.vector.bn_aggr(m.omv[p][:], m.obn[:]).then_inc(s.stats_done, 1)
                    dve.wait_ge(s.stats_done, 2 * t + 2)
                    nc.vector.tensor_scalar(m.ovar[p][:], m.omv[p][:, 1:2], LN_EPS, None, ALU.add).then_inc(s.var_ready, 1)

            def residual(u):
                if L0 or not inside(u):
                    return
                upto(dve, s.out_done, u)
                xt = row(m.x, u)
                nc.vector.scalar_tensor_tensor(xt, m.PT1[:, 0:D], tg, xt, ALU.mult, ALU.add).then_inc(s.x_done, 1)
                upto(dve, s.x_done, u)
                nc.vector.bn_stats(row(m.bn6, u), xt)

            def step(t, p):
                clip_top(t, p)
                normal_output(t - 1, 1 - p)
                soften(t + 1, 1 - p)
                average(t, p)
                residual(t - lag)
            pipeline(dve, step, first, last, steady)

        @block.gpsimd
        def _(pool):
            def step(t, p):
                u, q = t + 2, p
                if inside(u):
                    upto(pool, s.k_out, u)
                    upto(pool, s.scores_done, u - 2, 2)
                    nc.gpsimd.tensor_tensor(m.kexp[q][:], m.kT[q][:].unsqueeze(1).to_broadcast([P, HALF, P]),
                                            m.head_mask.unsqueeze(2).to_broadcast([P, HALF, P]),
                                            ALU.mult).then_inc(s.kexp_ready, 1)
                if L0 and inside(t - 1):
                    u, q = t - 1, 1 - p
                    upto(pool, s.hat_done, u)
                    nc.gpsimd.tensor_tensor(m.scaled[:], m.hat[:], m.g_ln, ALU.mult).then_inc(s.scaled_done, 1)
                    upto(pool, s.scaled_done, u)
                    upto(pool, s.oT_done, u - 2)
                    nc.gpsimd.tensor_tensor(m.os[q][:], m.scaled[:], m.b_ln, ALU.add).then_inc(s.o_ready, 1)
                    upto(pool, s.o_ready, u)
                    nc.gpsimd.tensor_copy(row(m.ola, u), m.os[q][:]).then_inc(s.ola_ready, 1)
                if L0 and inside(t):
                    upto(pool, s.var_ready, t)
                    nc.gpsimd.tensor_tensor(m.orstd[p][:], m.ovar[p][:], m.minus_half[:, 0:1], ALU.pow).then_inc(s.pow_done, 1)
            pipeline(pool, step, first, last, steady)

        @block.scalar
        def _(act):
            def take_qkv(t, p):
                u, q = t + 2, p
                v, r = t + 1, 1 - p
                if inside(u):
                    upto(act, s.qk_done, u)
                if inside(v):
                    upto(act, s.v_done, v)
                if inside(u):
                    upto(act, s.scores_done, u - 2, 2)
                    upto(act, s.kexp_ready, u - 2)
                    for h in range(2):
                        half = slice(64 * h, 64 * h + 64)
                        nc.scalar.activation(m.qT[q][half, :, h, :], QKV[half, 0:P].rearrange("p (b s) -> p b s", b=2),
                                             ACT.Identity, bias=bq if isinstance(bq, float) else bq[half, :])
                    nc.scalar.activation(m.kT[q][:], QKV[:, P:2 * P], ACT.Identity, bias=bk).then_inc(s.k_out, 1)
                if inside(v):
                    upto(act, s.pv_done, v - 2)
                    for hh in range(2):
                        src = QKV[64 * hh:64 * hh + 64, 2 * P:4 * P].rearrange("p (b c e d) -> p b c e d", b=2, c=CH, e=2)
                        dst = m.vexp[r][64 * hh:64 * hh + 64, :, :].rearrange("p b (c e d) -> p b c e d", c=CH, e=2)
                        out = nc.scalar.copy(dst[:, :, :, hh, 0:DH], src[:, :, :, hh, :])
                    out.then_inc(s.v_out, 1)

            def take_turned_probs(t):
                if L0 or not inside(t):
                    return
                for r2 in range(2):
                    act.wait_ge(s.pt_done, t * 2 + r2 + 1)
                    if r2 == 0:
                        upto(act, s.pv_done, t - 1)
                    nc.scalar.copy(m.PTs[:, r2 * F:(r2 + 1) * F], PT[r2][:]).then_inc(s.pt_out, 1)

            def take_turned_rows(t, p):
                u, w = t + 3, t - lag
                if inside(w):
                    upto(act, s.oT_done, w)
                if inside(u):
                    upto(act, s.xT_done, u)
                if inside(w):
                    upto(act, s.out_done, w - 1)
                    nc.scalar.activation(m.oT[:], A[:, 0:P], ACT.Identity, bias=0.0 if bv is None else bv).then_inc(s.oT_ready, 1)
                if inside(u):
                    q = 1 - p
                    upto(act, s.qk_done, u - 2)
                    if L0:
                        nc.scalar.activation(m.xnT[q][:], A[:, P:2 * P], ACT.Identity, scale=m.g_pre, bias=m.b_pre)
                        nc.scalar.activation(m.cnT[q][:], A[:, 2 * P:3 * P], ACT.Identity, scale=m.g_pre,
                                             bias=m.b_pre).then_inc(s.xnT_ready, 1)
                    else:
                        nc.scalar.copy(m.xnT[q][:], A[:, P:2 * P]).then_inc(s.xnT_ready, 1)

            def keep_output(u):
                if not (L0 and inside(u)):
                    return
                upto(act, s.out_done, u)
                nc.scalar.copy(row(m.za, u), m.PT1[:, 0:D]).then_inc(s.x_done, 1)

            def exponential(u, q):
                if not inside(u):
                    return
                for r in range(2):
                    act.wait_ge(s.sub_done, u * 2 + r + 1)
                    pr = m.probs[q][:, r * F:(r + 1) * F]
                    nc.scalar.activation(pr, pr, ACT.Exp, scale=scale).then_inc(s.exp_done, 1)

            def normal_input(u, q):
                if not inside(u):
                    return
                upto(act, s.xT_done, u - 2)
                ln = nc.scalar.activation(m.xn[q][:], row(m.x, u), ACT.Identity, scale=m.rstd[:, tile_of(u)],
                                          bias=m.nmr[:, tile_of(u)])
                if L0:
                    ln = nc.scalar.activation(m.cn[q][:], row(m.ctx, u), ACT.Identity, scale=m.crstd[:, tile_of(u)],
                                              bias=m.cnmr[:, tile_of(u)])
                ln.then_inc(s.xn_ready, 1)

            def step(t, p):
                take_qkv(t, p)
                take_turned_probs(t)
                take_turned_rows(t, p)
                exponential(t + 1, 1 - p)
                normal_input(t + 4, p)
                keep_output(t - lag)
            pipeline(act, step, first, last, steady)
            if L0:
                load_table(nc, m, ACT.Gelu)

        @block.tensor
        def _(pe):
            once = lambda twice: twice[:].rearrange("p (b r s) -> p b r s", b=2, r=2)[:, :, 0, :]

            def project(t, p):
                u, q = t + 2, p
                v, r = t + 1, 1 - p
                if inside(u):
                    upto(pe, s.xnT_ready, u)
                    arrived(pe, s.ctx_in, u, q)
                    upto(pe, s.k_out, u - 1)
                if inside(v):
                    upto(pe, s.v_out, v - 1)
                if inside(u):
                    nc.tensor.matmul(QKV[:, 0:P], wq, m.xnT[q][:], start=True, stop=True)
                    nc.tensor.matmul(QKV[:, P:2 * P], wk, m.cnT[q][:] if L0 else once(m.ctx_t[q]), start=True,
                                     stop=True).then_inc(s.qk_done, 1)
                if inside(v):
                    for b in range(2):
                        out = nc.tensor.matmul(QKV[:, (2 + b) * P:(3 + b) * P], m.ctx_t[r][:, b * P:(b + 1) * P], wv, start=True, stop=True)
                    out.then_inc(s.v_done, 1)

            def score(u, q):
                if not inside(u):
                    return
                settle(pe, (s.kexp_ready, u + 1), (s.sub_done, 2 * (u - 1)))
                for b in range(2):
                    out = nc.tensor.matmul(m.S[q][:, b * F:(b + 1) * F], m.qT[q][:, b, :, :],
                                           m.kexp[q][:, :, S * b:S * b + S], start=True, stop=True)
                    out.then_inc(s.scores_done, 1)

            def turn_probs(t, p):
                if not inside(t):
                    return
                for r in range(2):
                    pe.wait_ge(s.exp_done, t * 2 + r + 1)
                    if r == 0:
                        upto(pe, s.raw_ready if L0 else s.o_ready, t - 1)
                    else:
                        upto(pe, s.x_done, t - 1 - lag)
                    for c4 in range(4):
                        cc = 4 * r + c4
                        out = nc.tensor.transpose(PT[r][:, c4 * P:(c4 + 1) * P], m.probs[p][:, cc * P:(cc + 1) * P], m.ident)
                    out.then_inc(s.pt_done, 1)

            def turn_rows(t, p):
                w, u = t - lag, t + 3
                if inside(w):
                    upto(pe, s.o_ready, w)
                    upto(pe, s.oT_ready, w - 1)
                if inside(u):
                    upto(pe, s.xn_ready, u)
                    upto(pe, s.xnT_ready, u - 1)
                if inside(w):
                    nc.tensor.transpose(A[:, 0:P], m.os[(p + lag) % 2][:], m.ident).then_inc(s.oT_done, 1)
                if inside(u):
                    out = nc.tensor.transpose(A[:, P:2 * P], m.xn[1 - p][:], m.ident)
                    if L0:
                        out = nc.tensor.transpose(A[:, 2 * P:3 * P], m.cn[1 - p][:], m.ident)
                    out.then_inc(s.xT_done, 1)

            def weigh(t, p):
                if not inside(t):
                    return
                pe.wait_ge(s.pt_out, 2 * t + 1)
                upto(pe, s.v_out, t)
                for b in range(2):
                    if b:
                        upto(pe, s.pt_out, t, 2)
                    for cc in range(CH):
                        r, c4 = cc // 4, cc % 4
                        turned = m.PTs[:, b * F + c4 * P + 64 * r:b * F + c4 * P + 64 * r + 64]
                        out = nc.tensor.matmul(m.PT0[64 * b:64 * b + 64, cc * VW:(cc + 1) * VW], turned,
                                               m.vexp[p][:, b, cc * VW:(cc + 1) * VW], start=True, stop=True)
                out.then_inc(s.pv_done, 1)

            def project_output(t):
                w = t - lag
                if not inside(w):
                    return
                upto(pe, s.oT_ready, w)
                if not inside(t):
                    upto(pe, s.pt_out, T - 1, 2)
                upto(pe, s.x_done, w - 1)
                if L0:
                    nc.tensor.matmul(m.PT1[:, 0:D], m.oT[:], wo, start=True, stop=True).then_inc(s.out_done, 1)
                else:
                    nc.tensor.matmul(m.PT1[:, 0:D], m.ones[0:1, :], out_bias[0:1, :], start=True, stop=False)
                    nc.tensor.matmul(m.PT1[:, 0:D], m.oT[:], wo, start=False, stop=True).then_inc(s.out_done, 1)

            def step(t, p):
                project(t, p)
                if not L1:
                    turn_probs(t, p)
                score(t + 1, 1 - p)
                if L1:
                    turn_probs(t, p)
                turn_rows(t, p)
                weigh(t, p)
                project_output(t)
            if not L0:
                pe.wait_ge(m.wts_in, 16)
            pipeline(pe, step, first, last, steady)


def xattn0_tail(nc, m, tg):
    G = 4
    with sems(nc, "t0_", "gelu_done", "sum_done", "x_done", *STATS) as s, nc.Block() as block:
        @block.scalar
        def _(act):
            for g in range(G):
                z = m.za[:, g * (T // G):(g + 1) * (T // G), :]
                nc.scalar.activation(z, z, ACT.Gelu).then_inc(s.gelu_done, 1)

        @block.vector
        def _(dve):
            for g in range(G):
                sl = slice(g * (T // G), (g + 1) * (T // G))
                dve.wait_ge(s.gelu_done, g + 1)
                nc.vector.tensor_tensor(m.za[:, sl, :], m.za[:, sl, :], m.ola[:, sl, :], ALU.add).then_inc(s.sum_done, 1)
                dve.wait_ge(s.sum_done, g + 1)
                nc.vector.scalar_tensor_tensor(m.x[:, sl, :], m.za[:, sl, :], tg, m.x[:, sl, :], ALU.mult, ALU.add).then_inc(s.x_done, 1)
                dve.wait_ge(s.x_done, g + 1)
                for t in range(sl.start, sl.stop):
                    out = nc.vector.bn_stats(m.bn6[:, t, :], m.x[:, t, :])
                if g % 2:
                    out.then_inc(s.bn_done, 1)
                    row_stats(nc, dve, s, m.work, m.bn6, slice(g // 2 * T // 2, (g // 2 + 1) * T // 2), g // 2)
            row_offsets(nc, dve, s, m, 2)

        @block.gpsimd
        def _(pool):
            row_powers(nc, pool, s, m, 2)


def quantize(nc, dve, sem, start, m, v, half, square, big, q):
    n = v.shape[-1]
    small8, big8, over = m.small8[:, 0:n], m.big8[:, 0:n], m.over[:, 0:n]
    nc.vector.tensor_scalar(small8, v, 16.0, -16.0, ALU.min, ALU.max, saturate=False)
    nc.vector.tensor_scalar(over, square, 256.0, None, ALU.is_gt)
    nc.vector.tensor_scalar(big8, half, 224.0, -224.0, ALU.min, ALU.max, saturate=False).then_inc(sem, 1)
    dve.wait_ge(sem, start + 1)
    nc.vector.tensor_scalar(q, small8, 0.5, None, ALU.mult).then_inc(sem, 1)
    nc.vector.tensor_copy(big, big8).then_inc(sem, 1)
    dve.wait_ge(sem, start + 3)
    nc.vector.copy_predicated(q, over, big).then_inc(sem, 1)


def quantize_kernel(nc, dve, m, s):
    count = [0]

    def then(ins):
        count[0] += 1
        ins.then_inc(s.kernel_chain, 1)
        dve.wait_ge(s.kernel_chain, count[0])
    v, half, square, nan = m.xn[0][:], m.xn[1][:], m.cn[0][:], m.xnT[1][:]
    then(nc.vector.tensor_scalar(v, m.kraw[:], m.rks[:], None, ALU.mult))
    nc.vector.tensor_scalar(half, v, 0.5, None, ALU.mult)
    then(nc.vector.tensor_tensor(square, v, v, ALU.mult))
    quantize(nc, dve, s.quant, 0, m, v, half, square, m.cn[1][:], m.xnT[0][:])
    then(nc.vector.tensor_scalar(nan, square, 464.0 ** 2, 3e38, ALU.is_gt, ALU.mult))
    then(nc.vector.tensor_scalar(nan, nan, 1e5, 0.0, ALU.mult, ALU.mult))
    dve.wait_ge(s.quant, 4)
    nc.vector.tensor_tensor(m.kq[:], m.xnT[0][:], nan, ALU.add).then_inc(s.kernel_ready, 1)


def ffn0(nc, m, tg, fetch):
    G = F // D
    flat = lambda tensor: tensor.rearrange("p t d -> p (t d)")
    with sems(nc, "f0_", "ln_done", "scaled", "squares", "quant", "q_read", "nan_chain", "qT_done", "qT_ready", "y_done", "y_chain", "x_done",
              "kernel_chain", "kernel_ready", *STATS) as s, nc.Block() as block:
        block.sync(fetch)
        v, half = [pr[:, 0:F] for pr in m.probs], [pr[:, F:2 * F] for pr in m.probs]
        square, quant = [flat(k[:, 0:G, :]) for k in m.kexp], [flat(k[:, G:2 * G, :]) for k in m.kexp]
        big, Y = m.PTs[:, 0:F], (m.PT0, m.PT1)

        @block.scalar
        def _(act):
            for g in range(T // G):
                q = g % 2
                upto(act, s.scaled, g - 1)
                for t in range(G):
                    u = g * G + t
                    out = nc.scalar.activation(m.xb[:, t * D:(t + 1) * D], m.x[:, u, :], ACT.Identity,
                                               scale=m.rstd[:, u:u + 1], bias=m.nmr[:, u:u + 1])
                out.then_inc(s.ln_done, 1)
                upto(act, s.ln_done, g)
                upto(act, s.q_read, g - 2)
                nc.scalar.activation(v[q], m.xb[:], ACT.Copy, scale=m.scales[:, 2:3]).then_inc(s.scaled, 1)
                upto(act, s.scaled, g)
                nc.scalar.activation(half[q], v[q], ACT.Copy, scale=0.5)
                nc.scalar.activation(square[q], v[q], ACT.Square).then_inc(s.squares, 1)
                if g:
                    upto(act, s.qT_done, g - 1)
                    upto(act, s.y_done, g - 2)
                    nc.scalar.copy(m.xqT[:], m.bankA[:]).then_inc(s.qT_ready, 1)
            upto(act, s.qT_done, T // G - 1)
            upto(act, s.y_done, T // G - 2)
            nc.scalar.copy(m.xqT[:], m.bankA[:]).then_inc(s.qT_ready, 1)
            load_table(nc, m, ACT.Exp)

        @block.vector
        def _(dve):
            def add(g):
                yb = flat(m.yb[:])
                upto(dve, s.y_done, g)
                nc.vector.tensor_scalar(yb, Y[g % 2][:], m.scales[:, 3:4], None, ALU.mult).then_inc(s.y_chain, 1)
                dve.wait_ge(s.y_chain, 2 * g + 1)
                nc.vector.tensor_tensor(m.yb2[:], m.yb[:], m.bias0[:].unsqueeze(1).to_broadcast([P, G, D]),
                                        ALU.add).then_inc(s.y_chain, 1)
                dve.wait_ge(s.y_chain, 2 * g + 2)
                for t in range(G):
                    u = g * G + t
                    out = nc.vector.scalar_tensor_tensor(m.x[:, u, :], m.yb2[:, t, :], m.tgn[:, u:u + 1], m.x[:, u, :],
                                                         ALU.mult, ALU.add)
                out.then_inc(s.x_done, 1)
                upto(dve, s.x_done, g)
                for t in range(G):
                    out = nc.vector.bn_stats(m.bn6[:, g * G + t, :], m.x[:, g * G + t, :])
                if g % 2:
                    out.then_inc(s.bn_done, 1)
                    row_stats(nc, dve, s, m.work, m.bn6, slice((g - 1) * G, (g + 1) * G), g // 2)

            quantize_kernel(nc, dve, m, s)
            for g in range(T // G):
                q = g % 2
                upto(dve, s.squares, g)
                upto(dve, s.qT_done, g - 2)
                quantize(nc, dve, s.quant, 4 * g + 4, m, v[q], half[q], square[q], big, quant[q])
                tgn = m.tgn[:, g * G:(g + 1) * G]
                nc.vector.tensor_reduce(tgn, v[q].rearrange("p (t d) -> p t d", d=D), AX_X, ALU.max,
                                        apply_absolute_value=True).then_inc(s.nan_chain, 1)
                dve.wait_ge(s.nan_chain, 4 * g + 1)
                nc.vector.tensor_scalar(tgn, tgn, 464.0, 3e38, ALU.is_gt, ALU.mult).then_inc(s.nan_chain, 1)
                dve.wait_ge(s.nan_chain, 4 * g + 2)
                nc.vector.tensor_scalar(tgn, tgn, 1e5, 0.0, ALU.mult, ALU.mult).then_inc(s.nan_chain, 1)
                dve.wait_ge(s.nan_chain, 4 * g + 3)
                nc.vector.tensor_scalar(tgn, tgn, tg, None, ALU.add).then_inc(s.nan_chain, 1)
                dve.wait_ge(s.quant, 4 * g + 8)
                dve.wait_ge(s.nan_chain, 4 * g + 4)
                nc.vector.tensor_copy(m.settled[:], tgn[:, 0:1]).then_inc(s.q_read, 1)
                if g:
                    add(g - 1)
            add(T // G - 1)
            row_offsets(nc, dve, s, m, 2)

        @block.gpsimd
        def _(pool):
            pool.wait_ge(s.ln_done, T // G)
            row_powers(nc, pool, s, m, 2)

        @block.tensor
        def _(pe):
            for g in range(T // G):
                upto(pe, s.q_read, g)
                upto(pe, s.qT_ready, g - 1)
                for t in range(G):
                    out = nc.tensor.transpose(m.bankA[:, t * P:(t + 1) * P], quant[g % 2][:, t * P:(t + 1) * P], m.ident)
                out.then_inc(s.qT_done, 1)
                upto(pe, s.qT_ready, g)
                if g == 0:
                    pe.wait_ge(s.kernel_ready, 1)
                upto(pe, s.x_done, g - 2)
                for t in range(G):
                    out = nc.tensor.matmul(Y[g % 2][:, t * D:(t + 1) * D], m.xqT[:, t * P:(t + 1) * P], m.kq[:],
                                           start=True, stop=True)
                out.then_inc(s.y_done, 1)
            upto(pe, s.x_done, T // G - 1)
            warm_up(nc, m, 2)


def linear_attention(nc, m, wg, wv, wo, wq, wk, bg, bv, bk, bq, bo, fetch):
    G, K2 = F // D, D // 2
    GROUPS = T // G
    X, U, V, Q, KV, A, O = (m.bankA, m.S[0][:, 0:F], m.S[0][:, F:2 * F], m.S[1][:, 0:F], m.S[1][:, F:2 * F], m.PT0, m.PT1)
    KB, Z = m.bankB[:, 0:G * K2], m.bankB[:, G * K2:G * K2 + 2 * G]
    ctx, xnT = [pr[:, 0:F] for pr in m.probs], [pr[:, F:2 * F] for pr in m.probs]
    flat = lambda tensor: tensor.rearrange("p t d -> p (t d)")
    xn, us = [flat(k[:, 0:G, :]) for k in m.kexp], [flat(k[:, G:2 * G, :]) for k in m.kexp]
    v, qq, kvs, ua = [m.PTs[:, i * F:(i + 1) * F] for i in range(2)], m.w1, m.w2[0], m.w2[1]
    names = ["ctx_in*", "xn_ready", "xT_done", "xnT_ready", "u_done", "v_done", "k_done", "q_done", "us_ready", "kb_ready",
             "kr_ready", "kk_ready", "v_ready", "qr_ready", "qq_ready", "kv_done", "kvs_ready", "ks_ready", "a_half_done", "a_done", "z_done",
             "ua_ready", "wz_chain", "out_done", "o_added", "bias_added", *STATS]
    with sems(nc, "l2_", *names) as s, nc.Block() as block:
        steps = range(-2, GROUPS)
        there = lambda g: 0 <= g < GROUPS

        @block.sync
        def _(sp):
            for g in range(GROUPS):
                upto(sp, s.v_done, g - 2)
                upto(sp, s.k_done, g - 2)
                sp.dma_start(ctx[g % 2], m.ctxT_dram[:, g * F:(g + 1) * F]).then_inc(s.ctx_in[g % 2], 16)
                fetch(sp, g)

        @block.vector
        def _(dve):
            for g in steps:
                n, q = g + 1, (g + 1) % 2
                if there(n):
                    upto(dve, s.k_done, n)
                    upto(dve, s.kk_ready, n - 1)
                    tiles = lambda ap: ap.rearrange("p (t d) -> p t d", t=G)
                    nc.vector.tensor_tensor(m.kb[:], tiles(KB), bk.unsqueeze(1).to_broadcast([P, G, K2]),
                                            ALU.add).then_inc(s.kb_ready, 1)
                    upto(dve, s.kb_ready, n)
                    nc.vector.scalar_tensor_tensor(m.kr[:], m.kb[:], 0.0, m.kmask[:, n * G:(n + 1) * G].unsqueeze(2)
                                                   .to_broadcast([P, G, K2]), ALU.max, ALU.mult).then_inc(s.kr_ready, 1)
                    upto(dve, s.kr_ready, n)
                    upto(dve, s.kv_done, n - 2)
                    nc.vector.tensor_tensor(m.kk[q][:], m.kr[:], m.kb[:], ALU.mult).then_inc(s.kk_ready, 1)
                    upto(dve, s.v_done, n)
                    nc.vector.tensor_tensor(tiles(v[q]), tiles(V), bv.unsqueeze(1).to_broadcast([P, G, D]),
                                            ALU.add).then_inc(s.v_ready, 1)
                    upto(dve, s.q_done, n)
                    upto(dve, s.qq_ready, n - 1)
                    nc.vector.tensor_scalar(m.qr[:], Q, bq, 0.0, ALU.add, ALU.max).then_inc(s.qr_ready, 1)
                if there(g):
                    upto(dve, s.a_done, g)
                    upto(dve, s.us_ready, g)
                    upto(dve, s.out_done, g - 1)
                    nc.vector.tensor_tensor(ua[:], A[:], us[g % 2], ALU.mult).then_inc(s.ua_ready, 1)
                    upto(dve, s.z_done, g)
                    upto(dve, s.o_added, g - 1)
                    nc.vector.tensor_scalar(m.wz[:], Z[:, G:2 * G], KV_EPS, None, ALU.add).then_inc(s.wz_chain, 1)
                    dve.wait_ge(s.wz_chain, 3 * g + 1)
                    nc.vector.reciprocal(m.wz[:], m.wz[:]).then_inc(s.wz_chain, 1)
                    dve.wait_ge(s.wz_chain, 3 * g + 2)
                    nc.vector.tensor_tensor(m.wz[:], m.wz[:], m.qgate[:, g * G:(g + 1) * G], ALU.mult).then_inc(s.wz_chain, 1)
                    for t in range(G):
                        u = g * G + t
                        out = nc.vector.scalar_tensor_tensor(m.x[:, u, :], bo, m.qgate[:, u:u + 1], m.x[:, u, :], ALU.mult, ALU.add)
                    out.then_inc(s.bias_added, 1)
                if there(n):
                    upto(dve, s.kv_done, n)
                    upto(dve, s.z_done, n - 1)
                    nc.vector.tensor_copy(m.ks[:], Z[:, 0:G]).then_inc(s.ks_ready, 1)
                if there(g):
                    upto(dve, s.out_done, g)
                    dve.wait_ge(s.wz_chain, 3 * g + 3)
                    upto(dve, s.bias_added, g)
                    for t in range(G):
                        xt = m.x[:, g * G + t, :]
                        out = nc.vector.scalar_tensor_tensor(xt, O[:, t * D:(t + 1) * D], m.wz[:, t:t + 1], xt, ALU.mult, ALU.add)
                    out.then_inc(s.o_added, 1)
                    upto(dve, s.o_added, g)
                    for t in range(G):
                        out = nc.vector.bn_stats(m.bn6[:, g * G + t, :], m.x[:, g * G + t, :])
                    out.then_inc(s.bn_done, 1)
                    row_stats(nc, dve, s, m.work, m.bn6, slice(g * G, (g + 1) * G), g)
            dve.wait_ge(s.xn_ready, GROUPS)
            row_offsets(nc, dve, s, m, GROUPS)

        @block.gpsimd
        def _(pool):
            pool.wait_ge(s.xn_ready, GROUPS)
            row_powers(nc, pool, s, m, GROUPS)

        @block.scalar
        def _(act):
            def normal(g):
                upto(act, s.xT_done, g - 2)
                for t in range(G):
                    u = g * G + t
                    out = nc.scalar.activation(xn[g % 2][:, t * D:(t + 1) * D], m.x[:, u, :], ACT.Identity,
                                               scale=m.rstd[:, u:u + 1], bias=m.nmr[:, u:u + 1])
                out.then_inc(s.xn_ready, 1)
            normal(0)
            for g in steps:
                n, q = g + 1, (g + 1) % 2
                if there(n):
                    upto(act, s.u_done, n)
                    upto(act, s.ua_ready, n - 2)
                    nc.scalar.activation(us[q], U, ACT.Silu, bias=bg).then_inc(s.us_ready, 1)
                    upto(act, s.qr_ready, n)
                    upto(act, s.a_done, n - 2)
                    upto(act, s.z_done, n - 2)
                    nc.scalar.activation(qq[q][:], m.qr[:], ACT.Square).then_inc(s.qq_ready, 1)
                if there(g + 2):
                    upto(act, s.xT_done, g + 2)
                    upto(act, s.u_done, g)
                    upto(act, s.q_done, g)
                    nc.scalar.copy(xnT[g % 2], X[:]).then_inc(s.xnT_ready, 1)
                if there(n):
                    upto(act, s.kv_done, n)
                    upto(act, s.a_done, n - 1)
                    nc.scalar.copy(kvs[:], KV).then_inc(s.kvs_ready, 1)
                if there(g + 3):
                    normal(g + 3)

        @block.tensor
        def _(pe):
            for g in steps:
                n, q = g + 1, (g + 1) % 2
                if there(n):
                    arrived(pe, s.ctx_in, n, q)
                    upto(pe, s.ks_ready, n - 1)
                    if g > 0:
                        pe.wait_ge(s.wz_chain, 3 * g - 2)
                    for t in range(G):
                        out = nc.tensor.matmul(KB[:, t * K2:(t + 1) * K2], ctx[q][:, t * P:(t + 1) * P], wk, start=True, stop=True)
                    out.then_inc(s.k_done, 1)
                    upto(pe, s.xnT_ready, n)
                    upto(pe, s.qr_ready, n - 1)
                    nc.tensor.matmul(Q, wq, xnT[q], start=True, stop=True).then_inc(s.q_done, 1)
                    upto(pe, s.v_ready, n - 1)
                    for t in range(G):
                        out = nc.tensor.matmul(V[:, t * D:(t + 1) * D], ctx[q][:, t * P:(t + 1) * P], wv, start=True, stop=True)
                    out.then_inc(s.v_done, 1)
                    upto(pe, s.us_ready, n - 1)
                    nc.tensor.matmul(U, wg, xnT[q], start=True, stop=True).then_inc(s.u_done, 1)
                if there(g):
                    p = g % 2
                    upto(pe, s.kvs_ready, g)
                    upto(pe, s.qq_ready, g)
                    upto(pe, s.ua_ready, g - 1)
                    for b in range(2):
                        if b:
                            pe.wait_ge(s.a_half_done, g + 1)
                        for t in range(G):
                            half, col = slice(64 * b, 64 * b + 64), t * P + S * b
                            out = nc.tensor.matmul(A[:, col:col + S], kvs[half, t * D:(t + 1) * D], qq[p][half, col:col + S],
                                                   start=True, stop=True)
                        out.then_inc(s.a_done if b else s.a_half_done, 1)
                    upto(pe, s.ks_ready, g)
                    upto(pe, s.kb_ready, n if there(n) else g)
                    for t in range(G):
                        for b in range(2):
                            half, col = slice(64 * b, 64 * b + 64), t * P + S * b
                            out = nc.tensor.matmul(Z[half, G + t:G + t + 1], qq[p][half, col:col + S], m.ks[half, t:t + 1],
                                                   start=True, stop=True)
                    out.then_inc(s.z_done, 1)
                if there(g + 2):
                    upto(pe, s.xn_ready, g + 2)
                    upto(pe, s.xnT_ready, g + 1)
                    for t in range(G):
                        out = nc.tensor.transpose(X[:, t * P:(t + 1) * P], xn[g % 2][:, t * P:(t + 1) * P], m.ident)
                    out.then_inc(s.xT_done, 1)
                if there(n):
                    upto(pe, s.kk_ready, n)
                    upto(pe, s.v_ready, n)
                    upto(pe, s.kvs_ready, n - 1)
                    if n:
                        pe.wait_ge(s.wz_chain, 3 * n - 2)
                    for t in range(G):
                        for b in range(2):
                            half = slice(64 * b, 64 * b + 64)
                            keys = m.kk[q][half, t, :]
                            nc.tensor.matmul(KV[half, t * D:(t + 1) * D], keys, v[q][half, t * D:(t + 1) * D], start=True, stop=True)
                            out = nc.tensor.matmul(Z[half, t:t + 1], keys, m.ones[half, 0:1], start=True, stop=True)
                    out.then_inc(s.kv_done, 1)
                if there(g):
                    upto(pe, s.ua_ready, g)
                    upto(pe, s.o_added, g - 1)
                    for t in range(G):
                        out = nc.tensor.matmul(O[:, t * D:(t + 1) * D], ua[:, t * P:(t + 1) * P], wo, start=True, stop=True)
                    out.then_inc(s.out_done, 1)


def router(nc, m, layer, wr):
    G = F // P
    names = ["xn_ready", "xT_done", "xT_ready", "lg_done", "lg_read", "soft", "exp_done", "top_done", "idx_done", "out"]
    with sems(nc, f"r{layer}_", *names) as s, nc.Block() as block:
        xT = [pr[:, F:2 * F] for pr in m.probs]
        xn = [pr[:, 0:F] for pr in m.probs] + [k[:, G:2 * G, :].rearrange("p t d -> p (t d)") for k in m.kexp]
        tiles = lambda ap: ap.rearrange("p (t d) -> p t d", d=D)

        @block.sync
        def _(sp):
            for g in range(T // G):
                upto(sp, s.xn_ready, g)
                sp.dma_start(m.XN[g * G * P:(g + 1) * G * P, :].rearrange("(t p) d -> p t d", p=P),
                             tiles(xn[g])).then_inc(s.out, 16)
            sp.wait_ge(s.out, T // G * 16)

        @block.vector
        def _(dve):
            for g in range(T // G):
                for t in range(G):
                    u = g * G + t
                    out = nc.vector.tensor_scalar(xn[g][:, t * D:(t + 1) * D], m.x[:, u, :], m.rstd[:, u:u + 1],
                                                  m.nmr[:, u:u + 1], ALU.mult, ALU.add)
                out.then_inc(s.xn_ready, 1)
            upto(dve, s.lg_done, T // G - 1)
            nc.vector.tensor_copy(m.lg[:], m.bankB[:, 0:T * E].rearrange("p (t e) -> p t e", e=E)).then_inc(s.lg_read, 1)
            dve.wait_ge(s.lg_read, 1)
            scores = m.lg
            if layer == 2:
                e_t = lambda ap: ap.unsqueeze(2).to_broadcast([P, T, E])
                nc.vector.tensor_reduce(m.st_a[:], m.lg[:], AX_X, ALU.max).then_inc(s.soft, 1)
                dve.wait_ge(s.soft, 1)
                nc.vector.tensor_tensor(m.lp[:], m.lg[:], e_t(m.st_a[:]), ALU.subtract).then_inc(s.soft, 1)
                dve.wait_ge(s.exp_done, 1)
                nc.vector.tensor_reduce(m.st_b[:], m.lp[:], AX_X, ALU.add).then_inc(s.soft, 1)
                dve.wait_ge(s.soft, 3)
                nc.vector.reciprocal(m.st_c[:], m.st_b[:]).then_inc(s.soft, 1)
                dve.wait_ge(s.soft, 4)
                nc.vector.tensor_tensor(m.lp[:], m.lp[:], e_t(m.st_c[:]), ALU.mult).then_inc(s.soft, 1)
                dve.wait_ge(s.soft, 5)
                scores = m.lp
            for t in range(T):
                out = nc.vector.max(m.tops[:, t, :], scores[:, t, :])
            out.then_inc(s.top_done, 1)
            dve.wait_ge(s.top_done, 1)
            for t in range(T):
                out = nc.vector.max_index(m.idxs[:, t, :], m.tops[:, t, :], scores[:, t, :])
            out.then_inc(s.idx_done, 1)
            take_two(nc, dve, m, s, 1)

        @block.scalar
        def _(act):
            for g in range(T // G):
                upto(act, s.xT_done, g)
                upto(act, s.lg_done, g - 2)
                nc.scalar.copy(xT[g % 2], (m.bankA, m.PT0)[g % 2][:]).then_inc(s.xT_ready, 1)
            if layer == 2:
                act.wait_ge(s.soft, 2)
                nc.scalar.activation(m.lp[:], m.lp[:], ACT.Exp).then_inc(s.exp_done, 1)

        @block.tensor
        def _(pe):
            pe.wait_ge(m.router_in, 32)

            def turn(g):
                upto(pe, s.xn_ready, g)
                upto(pe, s.xT_ready, g - 2)
                for t in range(G):
                    out = nc.tensor.transpose((m.bankA, m.PT0)[g % 2][:, t * P:(t + 1) * P],
                                              xn[g][:, t * P:(t + 1) * P], m.ident)
                out.then_inc(s.xT_done, 1)
            turn(0)
            for g in range(T // G):
                if g + 1 < T // G:
                    turn(g + 1)
                upto(pe, s.xT_ready, g)
                for t in range(G):
                    u = g * G + t
                    out = nc.tensor.matmul(m.bankB[:, u * E:(u + 1) * E], xT[g % 2][:, t * P:(t + 1) * P], wr,
                                           start=True, stop=True)
                out.then_inc(s.lg_done, 1)


def take_two(nc, dve, m, s, groups):
    nc.vector.tensor_copy(m.tv[:].rearrange("p k t -> p t k"), m.tops[:, :, 0:2])
    dve.wait_ge(s.idx_done, groups)
    nc.vector.tensor_copy(m.ti[:].rearrange("p k t -> p t k"), m.idxs[:, :, 0:2])


def selu_gate(nc, m, w1, w2, b1, b2):
    G = F // P
    GROUPS = T // G
    names = ["xn_ready", "xT_done", "xT_ready", "h_done", "z_ready", "exp_done", "min_done", "hT_ready", "y_done", "y_ready",
             "top_done", "idx_done", "out"]
    with sems(nc, "g3_", *names) as s, nc.Block() as block:
        xT = [pr[:, F:2 * F] for pr in m.probs]
        xn = [pr[:, 0:F] for pr in m.probs] + [k[:, G:2 * G, :].rearrange("p t d -> p (t d)") for k in m.kexp]
        flat = lambda ap: ap.rearrange("p t d -> p (t d)")
        tiles = lambda ap: ap.rearrange("p (t d) -> p t d", d=D)
        z, ez = [m.PTs[:, i * F:(i + 1) * F] for i in range(2)], [flat(k[:, 0:G, :]) for k in m.kexp]
        hT = m.w1 + m.w2
        H_ = [m.S[i][:, j * F:(j + 1) * F] for i in range(2) for j in range(2)]
        Y = (m.PT0, m.PT1)

        @block.sync
        def _(sp):
            for g in range(GROUPS):
                upto(sp, s.xn_ready, g)
                sp.dma_start(m.XN[g * G * P:(g + 1) * G * P, :].rearrange("(t p) d -> p t d", p=P),
                             tiles(xn[g])).then_inc(s.out, 16)
            sp.wait_ge(s.out, GROUPS * 16)

        @block.vector
        def _(dve):
            def normal(g):
                for t in range(G):
                    u = g * G + t
                    out = nc.vector.tensor_scalar(xn[g][:, t * D:(t + 1) * D], m.x[:, u, :], m.rstd[:, u:u + 1],
                                                  m.nmr[:, u:u + 1], ALU.mult, ALU.add)
                out.then_inc(s.xn_ready, 1)

            def best(g):
                upto(dve, s.y_done, g)
                upto(dve, s.idx_done, g - 1)
                nc.vector.scalar_tensor_tensor(tiles(m.qr[:]), tiles(Y[g % 2][:]), SELU_SCALE, b2.unsqueeze(1).to_broadcast([P, G, D]),
                                               ALU.mult, ALU.add).then_inc(s.y_ready, 1)
                upto(dve, s.y_ready, g)
                for t in range(G):
                    out = nc.vector.max(m.tops[:, g * G + t, :], m.qr[:, t * D:(t + 1) * D])
                out.then_inc(s.top_done, 1)
                upto(dve, s.top_done, g)
                for t in range(G):
                    out = nc.vector.max_index(m.idxs[:, g * G + t, :], m.tops[:, g * G + t, :], m.qr[:, t * D:(t + 1) * D])
                out.then_inc(s.idx_done, 1)

            normal(0)
            for g in range(GROUPS):
                if g + 1 < GROUPS:
                    normal(g + 1)
                for k in range(FC):
                    i = g * FC + k
                    upto(dve, s.exp_done, i)
                    nc.vector.tensor_scalar(ez[k % 2], ez[k % 2], SELU_ALPHA, -SELU_ALPHA, ALU.min, ALU.add).then_inc(s.min_done, 1)
                    upto(dve, s.min_done, i)
                    upto(dve, s.y_done, g - 1)
                    nc.vector.scalar_tensor_tensor(hT[k][:], z[k % 2], 0.0, ez[k % 2], ALU.max, ALU.add).then_inc(s.hT_ready, 1)
                if g:
                    best(g - 1)
            best(GROUPS - 1)
            take_two(nc, dve, m, s, GROUPS)

        @block.scalar
        def _(act):
            def take_rows(g):
                upto(act, s.xT_done, g)
                upto(act, s.h_done, g - 2, FC)
                nc.scalar.copy(xT[g % 2], m.bankA[:]).then_inc(s.xT_ready, 1)

            take_rows(0)
            for g in range(GROUPS):
                for k in range(FC):
                    i = g * FC + k
                    upto(act, s.h_done, i)
                    upto(act, s.hT_ready, i - 2)
                    nc.scalar.activation(z[k % 2], H_[k], ACT.Identity, bias=b1[:, k:k + 1]).then_inc(s.z_ready, 1)
                    upto(act, s.z_ready, i)
                    nc.scalar.activation(ez[k % 2], z[k % 2], ACT.Exp, bias=m.ln_alpha[:, 0:1]).then_inc(s.exp_done, 1)
                    if k == 1 and g + 1 < GROUPS:
                        take_rows(g + 1)

        @block.tensor
        def _(pe):
            def first_layer(g):
                upto(pe, s.xn_ready, g)
                upto(pe, s.xT_ready, g - 1)
                for t in range(G):
                    out = nc.tensor.transpose(m.bankA[:, t * P:(t + 1) * P], xn[g][:, t * P:(t + 1) * P], m.ident)
                out.then_inc(s.xT_done, 1)
                upto(pe, s.xT_ready, g)
                for k in range(FC):
                    upto(pe, s.z_ready, (g - 1) * FC + k)
                    nc.tensor.matmul(H_[k], w1[:, k * P:(k + 1) * P], xT[g % 2], start=True, stop=True).then_inc(s.h_done, 1)

            pe.wait_ge(m.router_in, 32)
            first_layer(0)
            for g in range(GROUPS):
                if g + 1 < GROUPS:
                    first_layer(g + 1)
                upto(pe, s.hT_ready, g, FC)
                upto(pe, s.y_ready, g - 2)
                for t in range(G):
                    for k in range(FC):
                        out = nc.tensor.matmul(Y[g % 2][:, t * D:(t + 1) * D], hT[k][:, t * P:(t + 1) * P],
                                               w2[:, k * D:(k + 1) * D], start=(k == 0), stop=(k == FC - 1))
                out.then_inc(s.y_done, 1)


def dispatch(nc, m, layer, tg):
    J, G = 2 * T, T // 2
    with sems(nc, f"d{layer}_", "chain", "marks_ready", "sums_done", "gap_ready", "exp_done", "hot_ready", "list_step") as s, nc.Block() as block:
        @block.vector
        def _(dve):
            n = [0]

            def mark(ins):
                n[0] += 1
                ins.then_inc(s.chain, 1)
                return n[0]

            def after(number):
                dve.wait_ge(s.chain, number)

            e_t = lambda ap: ap.unsqueeze(1).to_broadcast([P, E, T])
            t_e = lambda ap: ap.unsqueeze(2).to_broadcast([P, E, T])
            by_tile = lambda tensor: tensor[:].rearrange("p e t -> p t e")
            flat = lambda tensor: tensor[:].rearrange("p e t -> p (e t)")
            v0, v1, w0, w1 = m.tv[:, 0, :], m.tv[:, 1, :], m.wt[:, 0, :], m.wt[:, 1, :]
            if layer == 1:
                nc.vector.tensor_tensor(m.st_a[:], v1, v0, ALU.subtract).then_inc(s.gap_ready, 1)
            for k in range(2):
                hot_done = mark(nc.vector.tensor_tensor(m.hot[k][:], e_t(m.ti[:, k, :]), t_e(m.con["expert"]), ALU.is_equal))
            after(hot_done)
            nc.vector.tensor_tensor(m.marks[:], m.hot[0][:], m.hot[1][:], ALU.add).then_inc(s.marks_ready, 1)
            nc.vector.tensor_reduce(m.valid[:, 0, :], by_tile(m.hot[0]), AX_X, ALU.add)
            valid_done = mark(nc.vector.tensor_reduce(m.valid[:, 1, :], by_tile(m.hot[1]), AX_X, ALU.add))
            if layer == 2:
                weights_done = mark(nc.vector.tensor_scalar(m.wt[:], m.tv[:], tg, None, ALU.mult))
            else:
                if layer == 1:
                    dve.wait_ge(s.exp_done, 1)
                    after(mark(nc.vector.tensor_scalar(m.st_c[:], m.st_b[:], 1.0, None, ALU.add)))
                else:
                    after(mark(nc.vector.tensor_tensor(m.st_c[:], v0, v1, ALU.add)))
                share_done = mark(nc.vector.reciprocal(m.st_c[:], m.st_c[:]))
            dve.wait_ge(s.sums_done, 2)
            incl_done = mark(nc.vector.tensor_tensor_scan(flat(m.incl), m.con["keep"], m.bankB[:, 0:P], 0.0, ALU.mult, ALU.add))
            after(incl_done)
            count = m.incl[:, :, T - 1]
            over_done = mark(nc.vector.tensor_tensor(m.tot[:], t_e(count), e_t(m.con["tile128"]), ALU.is_gt))
            pos_done = mark(nc.vector.tensor_tensor(flat(m.pos), flat(m.incl), m.bankB[:, 0:P], ALU.subtract))
            after(over_done)
            nb_done = mark(nc.vector.tensor_reduce(m.nb[:], m.tot[:], AX_X, ALU.add))
            after(pos_done)
            place_done = mark(nc.vector.tensor_tensor(flat(m.pos), flat(m.pos), m.bankA[:, 0:P], ALU.add))
            after(nb_done)
            cum_done = mark(nc.vector.tensor_tensor_scan(m.cum[:], m.ones[:, 0:E], m.nb[:], 0.0, ALU.mult, ALU.add))
            if layer != 2:
                after(share_done)
                share_done = mark(nc.vector.tensor_scalar(m.st_c[:], m.st_c[:], tg, None, ALU.mult))
            after(cum_done)
            base_done = mark(nc.vector.tensor_tensor(m.base[:], m.cum[:], m.nb[:], ALU.subtract))
            if layer != 2:
                after(share_done)
                if layer == 1:
                    nc.vector.tensor_copy(w0, m.st_c[:])
                else:
                    nc.vector.tensor_tensor(w0, v0, m.st_c[:], ALU.mult)
                weights_done = mark(nc.vector.tensor_tensor(w1, m.st_b[:] if layer == 1 else v1, m.st_c[:], ALU.mult))
            after(base_done)
            after(place_done)
            at_done = mark(nc.vector.scalar_tensor_tensor(m.pos[:], t_e(m.base[:]), float(P), m.pos[:], ALU.mult, ALU.add))
            after(valid_done)
            after(weights_done)
            nc.vector.tensor_tensor(m.wt[:], m.wt[:], m.valid[:], ALU.mult)
            token_done = mark(nc.vector.tensor_tensor(m.named[:], m.valid[:], m.con["token"].unsqueeze(1).to_broadcast([P, 2, T]), ALU.mult))
            after(at_done)
            own = [m.tot, m.incl]
            for k in range(2):
                own_done = mark(nc.vector.tensor_tensor(own[k][:], m.hot[k][:], m.pos[:], ALU.mult))
            many_done = mark(nc.vector.tensor_scalar(m.nbf[:], m.cum[:, E - 1:E], 3.0, 1.0, ALU.max, ALU.add))
            after(own_done)
            for k in range(2):
                dest_done = mark(nc.vector.tensor_reduce(m.dest[:, k, :], by_tile(own[k]), AX_X, ALU.add))
            after(dest_done)
            desti_done = mark(nc.vector.tensor_copy(m.desti[:], m.dest[:]))
            nbi_done = mark(nc.vector.tensor_copy(m.nbi[:], m.nbf[:]))
            after(desti_done)
            blki_done = mark(nc.vector.tensor_scalar(m.blki[:], m.desti[:], 7, None, ALU.logical_shift_right))
            after(nbi_done)
            nc.vector.tensor_scalar(m.nbi[:], m.nbi[:], 1, 1, ALU.logical_shift_right, ALU.logical_shift_left)
            after(blki_done)
            blk_done = mark(nc.vector.tensor_copy(m.blk[:], m.blki[:]))
            after(blk_done)
            slot_done = mark(nc.vector.scalar_tensor_tensor(m.slot[:], m.blk[:], -float(P), m.dest[:], ALU.mult, ALU.add))

            after(token_done)
            after(slot_done)
            for g in range(J // G):
                q, k, ts = g % 2, g * G // T, slice(g * G % T, g * G % T + G)
                over = lambda ap, n: ap[:, k, ts].unsqueeze(2).to_broadcast([P, G, n])
                upto(dve, s.list_step, g - 2)
                hot_f_done = mark(nc.vector.tensor_tensor(m.hot_f[q][:], m.con["block"].unsqueeze(1).to_broadcast([P, G, NBX]),
                                                          over(m.blk, NBX), ALU.is_equal))
                nc.vector.tensor_tensor(m.hot_slot[q][:], m.con["slot"].unsqueeze(1).to_broadcast([P, G, P]),
                                        over(m.slot, P), ALU.is_equal)
                after(hot_f_done)
                nc.vector.tensor_tensor(m.hot_blk[q][:], m.hot_f[q][:], over(m.named, NBX), ALU.mult).then_inc(s.hot_ready, 1)
            ends_done = mark(nc.vector.tensor_tensor(m.ebc[:], m.con["block"].unsqueeze(1).to_broadcast([P, E, NBX]),
                                                     m.cum[:].unsqueeze(2).to_broadcast([P, E, NBX]), ALU.is_ge))
            after(ends_done)
            ebf_done = mark(nc.vector.tensor_reduce(m.ebf[:], m.ebc[:].rearrange("p e b -> p b e"), AX_X, ALU.add))
            first, both, where = m.ebc[:, 0, :], m.ebc[:, 1, :], m.ebc[:, 2, :]
            dve.wait_ge(s.list_step, J // G)
            after(ebf_done)
            first_done = mark(nc.vector.tensor_copy(first, m.PT0[:, 0:NBX]))
            ebf_done = mark(nc.vector.tensor_scalar(m.ebf[:], m.ebf[:], float(E - 1), None, ALU.min))
            after(first_done)
            both_done = mark(nc.vector.tensor_tensor(both, first, m.PT1[:, 0:NBX], ALU.add))
            after(ebf_done)
            nc.vector.tensor_scalar(m.eb[:, 0:2], m.ebf[:, 0:2], float(E), None, ALU.mult)
            nc.vector.scalar_tensor_tensor(m.eb[:, 2:NBX], m.ebf[:, 2:NBX], float(E), m.ebf[:, 0:NBX - 2], ALU.mult, ALU.add)
            after(both_done)
            where_done = mark(nc.vector.scalar_tensor_tensor(where, both, 0.5, m.con["spare"], ALU.is_lt, ALU.mult))
            first_done = mark(nc.vector.tensor_scalar(first, both, 1.0, 1.0, ALU.max, ALU.subtract))
            after(first_done)
            nc.vector.tensor_copy(m.tok[:], first)
            where_done = mark(nc.vector.tensor_tensor(where, where, first, ALU.add))
            both_done = mark(nc.vector.tensor_scalar(both, m.PT1[:, 0:NBX], 0.5, float(N), ALU.is_gt, ALU.mult))
            after(both_done)
            nc.vector.tensor_tensor(m.goal[:], where, both, ALU.add)

        @block.scalar
        def _(act):
            if layer == 1:
                act.wait_ge(s.gap_ready, 1)
                nc.scalar.activation(m.st_b[:], m.st_a[:], ACT.Exp).then_inc(s.exp_done, 1)

        @block.tensor
        def _(pe):
            pe.wait_ge(s.marks_ready, 1)
            marks = m.marks[:].rearrange("p e t -> p (e t)")
            nc.tensor.matmul(m.bankA[:, 0:P], m.con["upper"], marks, start=True, stop=True).then_inc(s.sums_done, 1)
            nc.tensor.matmul(m.bankB[:, 0:P], m.ones[:], marks, start=True, stop=True).then_inc(s.sums_done, 1)

            for g in range(J // G):
                bank = (m.PT0, m.PT1)[g * G // T]
                pe.wait_ge(s.hot_ready, g + 1)
                for j in range(G):
                    out = nc.tensor.matmul(bank[:, 0:NBX], m.hot_slot[g % 2][:, j, :], m.hot_blk[g % 2][:, j, :],
                                           start=g * G % T + j == 0, stop=g * G % T + j == T - 1)
                out.then_inc(s.list_step, 1)


MOE_PIECES = {1: 1, 2: T, 3: T * D // F}


def mlp(nc, m, layer, W, b1=None, b2=None):
    selu, biased = layer == 3, b1 is not None
    func = {1: ACT.Gelu, 2: ACT.Gelu_apprx_tanh}
    names = ["idx_ready", "xT_done", "xgT_ready", "w1_ready", "w2_ready", "b1_ready", "b2_ready", "h_done", "z_ready", "exp_done",
             "min_done", "hT_ready", "y_done", "y_ready"]
    H_, Y = [m.S[i][:, 0:F] for i in range(2)], (m.PT0, m.PT1)
    xg_in, y_out = m.gather_sems[layer, "xg_in"], m.gather_sems[layer, "y_out"]
    live = lambda u: not isinstance(u, int) or u >= 0
    hT, z, ez = [pr[:, 0:F] for pr in m.probs], [pr[:, F:2 * F] for pr in m.probs], [m.PTs[:, i * F:(i + 1) * F] for i in range(2)]
    with sems(nc, f"m{layer}_", *names) as s, nc.Block() as block:
        def run(eng, step):
            blocks = eng.value_load(m.nbi[0:1, 0:1], min_val=4, max_val=NB)
            for b in range(-4, 2):
                step(b, b % 2)
            with eng.Fori(2, blocks, 2) as i:
                step(i, 0)
                step(i + 1, 1)

        @block.sync
        def _(sp):
            blocks = sp.value_load(m.nbi[0:1, 0:1], min_val=4, max_val=NB)
            settle(sp, (y_out[0], blocks * 8), (y_out[1], blocks * 8))

        @block.gpsimd
        def _(pool):
            def step(b, p):
                u, q = b + 4, p
                settle(pool, (s.idx_ready, u + 1), (s.xT_done, u - 1))
                nc.gpsimd.indirect_dma_start(m.xg[q][:], None, m.XN, bass.IndirectOffsetOnAxis(ap=m.idx_t[q][:], axis=0))\
                    .then_inc(xg_in[q], 16)
                if live(b):
                    settle(pool, (s.y_ready, b + 1))
                    nc.gpsimd.indirect_dma_start(m.YS, bass.IndirectOffsetOnAxis(ap=m.goal_t[p][:], axis=0), m.ys[p][:], None)\
                        .then_inc(y_out[p], 16)
            pool.wait_ge(m.zeros_out, 16)
            run(pool, step)

        @block.vector
        def _(dve):
            def step(b, p):
                u, q = b + 4, p
                if not isinstance(u, int) or u >= 2:
                    arrived(dve, xg_in, u - 2, q)
                nc.vector.tensor_copy(m.idx_t[q][:], m.tok[:, tile_of(u)]).then_inc(s.idx_ready, 1)
                u, q = b + 3, 1 - p
                if live(u):
                    both = dve.value_load(m.eb[0:1, tile_of(u)], min_val=0, max_val=E * E - 1)
                    e1, e2 = both // E, both % E
                    upto(dve, s.h_done, b + 1)
                    nc.vector.tensor_copy(m.w1[q][:], W[:, 0, bass.ds(e1 * F, F)]).then_inc(s.w1_ready, 1)
                    if biased:
                        upto(dve, s.z_ready if selu else s.hT_ready, b + 1)
                        nc.vector.tensor_copy(m.b1[q][:], b1[:, bass.ds(e1 * FC, FC)]).then_inc(s.b1_ready, 1)
                u, q = b + 1, 1 - p
                if live(u):
                    upto(dve, s.y_done, b - 1)
                    nc.vector.tensor_copy(m.w2[q][:], W[:, 1, bass.ds(e2 * F, F)]).then_inc(s.w2_ready, 1)
                    if biased:
                        upto(dve, s.y_ready, b - 1)
                        nc.vector.tensor_copy(m.b2_row[q][:], b2[:, bass.ds(e2 * D, D)]).then_inc(s.b2_ready, 1)
                if live(b):
                    if not isinstance(b, int) or b >= 2:
                        arrived(dve, y_out, b - 2, p)
                    nc.vector.tensor_copy(m.goal_t[p][:], m.goal[:, tile_of(b)])
                    upto(dve, s.y_done, b)
                    if b2 is None:
                        nc.vector.tensor_copy(m.ys[p][:], Y[p][:, 0:D]).then_inc(s.y_ready, 1)
                    else:
                        upto(dve, s.b2_ready, b)
                        nc.vector.scalar_tensor_tensor(m.ys[p][:], Y[p][:, 0:D], SELU_SCALE if selu else 1.0,
                                                       m.b2_row[p][:], ALU.mult, ALU.add).then_inc(s.y_ready, 1)
                u, q = b + 2, p
                if selu and live(u):
                    upto(dve, s.exp_done, u)
                    nc.vector.tensor_scalar(ez[q], ez[q], SELU_ALPHA, -SELU_ALPHA, ALU.min, ALU.add).then_inc(s.min_done, 1)
                    upto(dve, s.min_done, u)
                    upto(dve, s.y_done, u - 2)
                    nc.vector.scalar_tensor_tensor(hT[q], z[q], 0.0, ez[q], ALU.max, ALU.add).then_inc(s.hT_ready, 1)
            if biased:
                dve.wait_ge(m.bias_in, 32)
            dve.wait_ge(m.moe_in[layer], 16 * MOE_PIECES[layer])
            run(dve, step)

        @block.scalar
        def _(act):
            def step(b, p):
                u, q = b + 3, 1 - p
                if live(u):
                    upto(act, s.xT_done, u)
                    upto(act, s.h_done, u - 2)
                    nc.scalar.copy(m.xgT[q][:], m.bankA[:, 0:P]).then_inc(s.xgT_ready, 1)
                u, q = b + 2, p
                if live(u):
                    upto(act, s.h_done, u)
                    if biased:
                        upto(act, s.b1_ready, u)
                        if selu:
                            upto(act, s.hT_ready, u - 2)
                        else:
                            upto(act, s.y_done, u - 2)
                        for k in range(FC):
                            out = nc.scalar.activation((z if selu else hT)[q][:, k * P:(k + 1) * P], H_[q][:, k * P:(k + 1) * P],
                                                       ACT.Identity if selu else func[layer], bias=m.b1[q][:, k:k + 1])
                        out.then_inc(s.z_ready if selu else s.hT_ready, 1)
                        if selu:
                            upto(act, s.z_ready, u)
                            nc.scalar.activation(ez[q], z[q], ACT.Exp, bias=m.ln_alpha[:, 0:1]).then_inc(s.exp_done, 1)
                    else:
                        upto(act, s.y_done, u - 2)
                        nc.scalar.activation(hT[q], H_[q], func[layer]).then_inc(s.hT_ready, 1)
            load_table(nc, m, ACT.Exp if selu else func[layer])
            run(act, step)

        @block.tensor
        def _(pe):
            def step(b, p):
                if live(b):
                    upto(pe, s.hT_ready, b)
                    upto(pe, s.w2_ready, b)
                    upto(pe, s.y_ready, b - 2)
                    for k in range(FC):
                        out = nc.tensor.matmul(Y[p][:, 0:D], hT[p][:, k * P:(k + 1) * P], m.w2[p][:, k * D:(k + 1) * D], start=(k == 0), stop=(k == FC - 1))
                    out.then_inc(s.y_done, 1)
                u, q = b + 2, p
                if live(u):
                    upto(pe, s.xgT_ready, u)
                    upto(pe, s.w1_ready, u)
                    upto(pe, s.z_ready if selu else s.hT_ready, u - 2)
                    for k in range(FC):
                        out = nc.tensor.matmul(H_[q][:, k * P:(k + 1) * P], m.w1[q][:, k * P:(k + 1) * P], m.xgT[q][:], start=True, stop=True)
                    out.then_inc(s.h_done, 1)
                u, q = b + 3, 1 - p
                if live(u):
                    arrived(pe, xg_in, u, q)
                    upto(pe, s.xgT_ready, u - 1)
                    nc.tensor.transpose(m.bankA[:, 0:P], m.xg[q][:], m.ident).then_inc(s.xT_done, 1)
            run(pe, step)


def combine(nc, m, layer, out=None):
    halves = [m.probs, m.kexp]
    with sems(nc, f"k{layer}_", "y_in*", "x_chain", "stored", *STATS) as s, nc.Block() as block:
        @block.sync
        def _(sp):
            for g in range(2):
                for k in range(2):
                    rows = slice(k * N + g * N // 2, k * N + (g + 1) * N // 2)
                    dst = halves[k][g][:] if k == 0 else halves[k][g][:].rearrange("p h k -> p (h k)")
                    sp.dma_start(dst.rearrange("p (t d) -> p t d", d=D),
                                 m.YS[rows, :].rearrange("(t p) d -> p t d", p=P)).then_inc(s.y_in[g], 16)
            if out is not None:
                for g in range(2):
                    sp.wait_ge(s.x_chain, 2 * g + 2)
                    sp.dma_start(out[g * N // 2:(g + 1) * N // 2, :].rearrange("(t p) d -> p t d", p=P),
                                 m.x[:, g * T // 2:(g + 1) * T // 2, :]).then_inc(s.stored, 16)
                sp.wait_ge(s.stored, 32)

        @block.vector
        def _(dve):
            for g in range(2):
                ts = range(g * T // 2, (g + 1) * T // 2)
                dve.wait_ge(s.y_in[g], 32)
                for k in range(2):
                    for t in ts:
                        y = halves[k][g][:, (t % HALF) * D:(t % HALF + 1) * D] if k == 0 else halves[k][g][:, t % HALF, :]
                        last = nc.vector.scalar_tensor_tensor(m.x[:, t, :], y, m.wt[:, k, t:t + 1], m.x[:, t, :], ALU.mult, ALU.add)
                    last.then_inc(s.x_chain, 1)
                    dve.wait_ge(s.x_chain, 2 * g + k + 1)
                if layer == 3:
                    continue
                for t in ts:
                    last = nc.vector.bn_stats(m.bn6[:, t, :], m.x[:, t, :])
                last.then_inc(s.bn_done, 1)
                row_stats(nc, dve, s, m.work, m.bn6, slice(ts.start, ts.stop), g)
            if layer != 3:
                row_offsets(nc, dve, s, m, 2)

        @block.scalar
        def _(act):
            if layer != 3:
                load_table(nc, m, ACT.Silu if layer == 1 else ACT.Exp)

        @block.gpsimd
        def _(pool):
            if layer != 3:
                row_powers(nc, pool, s, m, 2)

        @block.tensor
        def _(pe):
            if layer != 3:
                pe.wait_ge(s.x_chain, 4)
                warm_up(nc, m, 3 if layer == 1 else 2)


W_NAMES = ["q0", "k0", "v0", "o0", "q1", "k1", "v1", "o1", "g2", "v2", "o2", "q2", "k2", "q3", "k3", "v3", "o3"]
COL_NAMES = ["g_pre", "b_pre", "bq2", "bg2", "bq3", "bk3", "bv3"]
ROW_SIZES = {"g_ln": D, "b_ln": D, "bo1": D, "bv2": D, "bk2": D // 2, "bo2": D, "bo3": D,
             "gate_bo": D}
ROW_AT = {}
_at = 0
for _n, _k in ROW_SIZES.items():
    ROW_AT[_n] = (_at, _at + _k)
    _at += _k
ROWS = _at
C_SIZES = {"ident": P, "head_mask": HALF, "upper": P, "expert": E, "tile128": T, "block": NBX, "slot": P,
           "token": T, "keep": P, "spare": NBX}
C_AT = {}
_at = 0
for _n, _k in C_SIZES.items():
    C_AT[_n] = (_at, _at + _k)
    _at += _k
CONSTS = _at


def program(nc, a, out):
    with ExitStack() as c:
        def sb(name, shape, dt=F32):
            return c.enter_context(nc.sbuf_tensor(name, shape, dt))

        m = Memory()
        numbers = iter(GATHER_NUMBERS)
        m.gather_sems = {(layer, n): [c.enter_context(nc.semaphore(f"{n}{layer}_{i}", num=next(numbers))) for i in range(2)]
                       for layer in (1, 2, 3) for n in ("xg_in", "y_out")}
        numbers = iter(PREFETCH_NUMBERS)
        m.moe_in = {layer: c.enter_context(nc.semaphore(f"moe{layer}_in", num=next(numbers))) for layer in (1, 2, 3)}
        m.bias_in = c.enter_context(nc.semaphore("bias_in", num=next(numbers)))
        m.wts_in = c.enter_context(nc.semaphore("wts_in", num=next(numbers)))
        m.zeros_out = c.enter_context(nc.semaphore("zeros_out", num=next(numbers)))
        m.router_in = c.enter_context(nc.semaphore("router_in", num=next(numbers)))
        m.x, m.ctx = sb("x", [P, T, D]), sb("ctx", [P, T, D])
        m.wts = sb("wts", [P, len(W_NAMES), P])
        m.cols = sb("cols", [P, len(COL_NAMES)])
        m.rows = sb("rows", [P, ROWS])
        m.consts = sb("consts", [P, CONSTS])
        m.gates = sb("gates", [P, 8])
        m.tg = sb("tg", [P, 8])
        m.bn6, m.cbn6 = sb("bn6", [P, T, 6]), sb("cbn6", [P, T, 6])
        m.rstd, m.nmr, m.crstd, m.cnmr, m.st_a, m.st_b, m.st_c, m.minus_half = (
            sb(n, [P, T]) for n in ("rstd", "nmr", "crstd", "cnmr", "st_a", "st_b", "st_c", "minus_half"))
        m.work, m.ctx_work = Memory(), Memory()
        for w, n in ((m.work, "x"), (m.ctx_work, "ctx")):
            w.sum, w.diff, w.square, w.var, w.base = (sb(f"{n}_{k}", [P, T]) for k in ("sum", "diff", "square", "var", "base"))
        two = lambda n, shape, dt=F32: [sb(f"{n}{i}", shape, dt) for i in range(2)]
        m.ctx_t = two("ctx_t", [P, 2 * P])
        m.xn, m.cn, m.xnT, m.cnT = (two(n, [P, P]) for n in ("xn", "cn", "xnT", "cnT"))
        m.hat, m.scaled = sb("hat", [P, D]), sb("scaled", [P, D])
        m.kT, m.os, m.raw = (two(n, [P, P]) for n in ("kT", "os", "raw"))
        m.qT = two("qT", [P, 2, 2, S])
        m.kexp = two("kexp", [P, HALF, P])
        m.vexp = two("vexp", [P, 2, CH * VW])
        m.probs = two("probs", [P, 2 * F])
        m.PTs, m.oT = sb("PTs", [P, 2 * F]), sb("oT", [P, P])
        m.rowmax = two("rowmax", [P, H])
        m.rden = sb("rden", [P, H])
        m.obn, m.omv, m.ovar, m.orstd = sb("obn", [P, 6]), two("omv", [P, 2]), two("ovar", [P, 1]), two("orstd", [P, 1])
        m.mask_t, m.pred = two("mask_t", [P, 2 * S], I32), two("pred", [P, 2 * S], I32)
        m.negs = sb("negs", [P, S])
        m.xb, m.xqT = sb("xb", [P, F], BF16), sb("xqT", [P, F], BF16)
        m.yb, m.yb2 = sb("yb", [P, FC, D], BF16), sb("yb2", [P, FC, D], BF16)
        m.small8, m.big8, m.over = sb("small8", [P, F], FP8), sb("big8", [P, F], FP8), sb("over", [P, F], I32)
        m.primed = sb("primed", [P, 1])
        m.tgn, m.settled = sb("tgn", [P, T]), sb("settled", [P, 1])
        m.kraw, m.kq, m.bias0 = sb("kraw", [P, D], BF16), sb("kq", [P, D], BF16), sb("bias0", [P, D], BF16)
        m.scales, m.rks = sb("scales", [P, 4]), sb("rks", [P, 1])
        m.kmask8, m.kmask, m.qgate = sb("kmask8", [P, T], U8), sb("kmask", [P, T]), sb("qgate", [P, T])
        m.kb, m.kr, m.kk = sb("kb", [P, FC, D // 2]), sb("kr", [P, FC, D // 2]), two("kk", [P, FC, D // 2])
        m.qr, m.ks, m.wz = sb("qr", [P, F]), sb("ks", [P, FC]), sb("wz", [P, FC])
        m.lg, m.lp = sb("lg", [P, T, E]), sb("lp", [P, T, E])
        m.tops, m.idxs = sb("tops", [P, T, 8]), sb("idxs", [P, T, 8], U32)
        m.tv, m.ti, m.wt = sb("tv", [P, 2, T]), sb("ti", [P, 2, T]), sb("wt", [P, 2, T])
        m.hot = two("hot", [P, E, T])
        m.marks, m.tot, m.incl, m.pos = (sb(n, [P, E, T]) for n in ("marks", "tot", "incl", "pos"))
        m.nb, m.cum, m.base = sb("nb", [P, E]), sb("cum", [P, E]), sb("base", [P, E])
        m.dest, m.valid, m.blk, m.slot = (sb(n, [P, 2, T]) for n in ("dest", "valid", "blk", "slot_of"))
        m.desti, m.blki = sb("desti", [P, 2, T], I32), sb("blki", [P, 2, T], I32)
        m.nbf, m.nbi = sb("nbf", [P, 1]), sb("nbi", [P, 1], I32)
        m.ebc, m.ebf, m.eb, m.tok = sb("ebc", [P, E, NBX]), sb("ebf", [P, NBX]), sb("eb", [P, NBX], I32), sb("tok", [P, NBX], I32)
        m.hot_slot, m.hot_blk = two("hot_slot", [P, T // 2, P], F16), two("hot_blk", [P, T // 2, NBX], F16)
        m.hot_f, m.named, m.goal = two("hot_f", [P, T // 2, NBX]), sb("named", [P, 2, T]), sb("goal", [P, NBX], I32)
        m.ones, m.ln_alpha = sb("ones", [P, P]), sb("ln_alpha", [P, 1])
        m.xg, m.xgT, m.ys, m.idx_t = two("xg", [P, D]), two("xgT", [P, P]), two("ys", [P, D]), two("idx_t", [P, 1], I32)
        m.goal_t = two("goal_t", [P, 1], I32)
        m.w1, m.w2, m.b1, m.b2_row = two("w1", [P, F]), two("w2", [P, F]), two("b1", [P, FC]), two("b2_row", [P, D])
        m.b1_all, m.gate_b1 = sb("b1_all", [P, 2, E * FC]), sb("gate_b1", [P, FC])
        m.router_w = sb("router_w", [P, 2, E])
        m.gate_w = sb("gate_w", [P, 2, F])
        m.b2 = {layer: sb(f"b2_{layer}", [P, E * D]) for layer in (2, 3)}
        m.XN = nc.dram_tensor("XN", [N, D], F32, kind="Internal").ap()
        m.YS = nc.dram_tensor("YS", [2 * N + NBX * P, D], F32, kind="Internal").ap()
        m.WA, m.WB = sb("WA", [P, 2, E * F]), sb("WB", [P, 2, E * F])
        m.za = m.WB[:, 0, 0:T * D].rearrange("p (t d) -> p t d", d=D)
        m.ola = m.WB[:, 1, 0:T * D].rearrange("p (t d) -> p t d", d=D)
        m.S = [c.enter_context(nc.psum_tensor(f"S{i}", [P, 2 * F], F32)) for i in range(2)]
        m.PT0, m.PT1, m.bankA, m.bankB = (c.enter_context(nc.psum_tensor(n, [P, F], F32)) for n in ("PT0", "PT1", "bankA", "bankB"))
        m.ctxT_dram, m.ctxT2_dram, m.mask_dram = a["ctxT"], a["ctxT2"], a["mask"]
        w = {n: m.wts[:, i, :] for i, n in enumerate(W_NAMES)}
        col = {n: m.cols[:, i:i + 1] for i, n in enumerate(COL_NAMES)}
        rowv = {n: m.rows[:, i:j] for n, (i, j) in ROW_AT.items()}
        con = {n: m.consts[:, i:j] for n, (i, j) in C_AT.items()}
        m.con = con
        m.ident, m.head_mask = con["ident"], con["head_mask"]
        m.g_pre, m.b_pre, m.g_ln, m.b_ln = col["g_pre"], col["b_pre"], rowv["g_ln"], rowv["b_ln"]
        tg = lambda i: m.tg[:, i:i + 1]

        with sems(nc, "s_", "x_in", "ctx_in", "small_in", "zeroed", "ready", "chain", *STATS) as s, nc.Block() as block:
            @block.sync
            def _(sp):
                sp.dma_start(m.x[:], a["x"].rearrange("(t p) d -> p t d", p=P)).then_inc(s.x_in, 16)
                sp.dma_start(m.ctx[:], a["ctx"].rearrange("(t p) d -> p t d", p=P)).then_inc(s.ctx_in, 16)
                sp.dma_start(m.kraw[:], a["kernel0"]).then_inc(s.small_in, 16)
                sp.dma_start(m.bias0[:], a["bias0"].partition_broadcast(P)).then_inc(s.small_in, 16)
                sp.dma_start(m.kmask8[:], a["kmask"]).then_inc(s.small_in, 16)
                sp.dma_start(m.b1_all[:].rearrange("p a b -> p (a b)"), a["b1"]).then_inc(s.small_in, 16)
                sp.dma_start(m.gate_b1[:], a["gate_b1"]).then_inc(s.small_in, 16)

            @block.scalar
            def _(act):
                act.dma_start(m.gates[:], a["gates"].partition_broadcast(P)).then_inc(s.small_in, 16)
                act.dma_start(m.cols[:], a["cols"]).then_inc(s.small_in, 16)
                act.dma_start(m.scales[:, 0:2], a["scales"].partition_broadcast(P)).then_inc(s.small_in, 16)
                act.dma_start(m.consts[:], a["consts"]).then_inc(s.small_in, 16)
                act.dma_start(m.wts[:, 0:4, :].rearrange("p a b -> p (a b)"), a["wts"][:, 0:4 * P]).then_inc(s.small_in, 16)
                act.dma_start(m.rows[:], a["rows"].partition_broadcast(P)).then_inc(s.small_in, 16)
                act.wait_ge(s.small_in, 16 * 11)
                nc.scalar.activation(m.tg[:], m.gates[:], ACT.Tanh).then_inc(s.ready, 1)
                act.wait_ge(s.zeroed, 3)
                load_table(nc, m, ACT.Exp)

            @block.gpsimd
            def _(pool):
                nc.gpsimd.memset(m.minus_half[:], -0.5).then_inc(s.zeroed, 1)
                nc.gpsimd.memset(m.xg[0][:], 0.0)
                nc.gpsimd.memset(m.ones[:], 1.0)
                nc.gpsimd.memset(m.ln_alpha[:], math.log(SELU_ALPHA))
                nc.gpsimd.memset(m.negs[:], NEG * DH ** 0.5)
                for i in range(2):
                    nc.gpsimd.memset(m.qT[i][:], 0.0)
                    nc.gpsimd.memset(m.vexp[i][:], 0.0).then_inc(s.zeroed, 1)
                pool.wait_ge(s.zeroed, 3)
                for i in range(2):
                    v = m.vexp[i][:].rearrange("p b (c e d) -> p b c e d", c=CH, e=2)
                    for hh in range(2):
                        nc.gpsimd.memset(v[64 * hh:64 * hh + 64, :, :, hh, DH:DH + 1], 1.0).then_inc(s.zeroed, 1)
                pool.wait_ge(s.zeroed, 7)
                for g, (w_, rstd) in enumerate(((m.work, m.rstd), (m.ctx_work, m.crstd))):
                    pool.wait_ge(s.var_ready, g + 1)
                    nc.gpsimd.tensor_tensor(rstd[:], w_.base[:], m.minus_half[:], ALU.pow).then_inc(s.pow_done, 1)

            @block.tensor
            def _(pe):
                pe.wait_ge(s.small_in, 16 * 11)
                warm_up(nc, m, 4)

            @block.vector
            def _(dve):
                for g, (sem, data, bn6, w_) in enumerate(((s.x_in, m.x, m.bn6, m.work), (s.ctx_in, m.ctx, m.cbn6, m.ctx_work))):
                    dve.wait_ge(sem, 16)
                    for t in range(T):
                        bn = nc.vector.bn_stats(bn6[:, t, :], data[:, t, :])
                    bn.then_inc(s.bn_done, 1)
                    row_stats(nc, dve, s, w_, bn6, slice(0, T), g, double=g == 0)
                dve.wait_ge(s.ready, 1)
                nc.vector.tensor_copy(m.kmask[:], m.kmask8[:]).then_inc(s.chain, 1)
                nc.vector.reciprocal(m.scales[:, 2:3], m.scales[:, 0:1])
                nc.vector.reciprocal(m.rks[:], m.scales[:, 1:2])
                nc.vector.scalar_tensor_tensor(m.scales[:, 3:4], m.scales[:, 0:1], 4.0, m.scales[:, 1:2], ALU.mult, ALU.mult)
                dve.wait_ge(s.chain, 1)
                nc.vector.tensor_scalar(m.qgate[:], m.kmask[:], tg(2), None, ALU.mult)
                for g, (w_, rstd, nmr) in enumerate(((m.work, m.rstd, m.nmr), (m.ctx_work, m.crstd, m.cnmr))):
                    dve.wait_ge(s.pow_done, g + 1)
                    nc.vector.scalar_tensor_tensor(nmr[:], w_.sum[:], -0.5, rstd[:], ALU.mult, ALU.mult)

        attention(nc, m, 0, w["q0"], w["k0"], w["v0"], w["o0"])
        xattn0_tail(nc, m, tg(0))

        flat = lambda tensor: tensor[:].rearrange("p a b -> p (a b)")

        def fetch_rest(sp):
            sp.dma_start(m.wts[:, 4:, :].rearrange("p a b -> p (a b)"), a["wts"][:, 4 * P:]).then_inc(m.wts_in, 16)
            sp.dma_start(flat(m.router_w), a["router_w"]).then_inc(m.router_in, 16)
            sp.dma_start(flat(m.gate_w), a["gate_w"]).then_inc(m.router_in, 16)
            sp.dma_start(flat(m.WA), a["moe1"]).then_inc(m.moe_in[1], 16)
            for layer in (2, 3):
                sp.dma_start(m.b2[layer][:], a[f"b2_{layer}"].partition_broadcast(P)).then_inc(m.bias_in, 16)

            sp.dma_start(m.YS[0:2 * N, :].rearrange("(b p) d -> p b d", p=P),
                         m.xg[0][:].unsqueeze(1).to_broadcast([P, 2 * T, D])).then_inc(m.zeros_out, 16)

        def fetch_moe2(sp, t):
            cols = bass.ds(t * (2 * E * F // MOE_PIECES[2]), 2 * E * F // MOE_PIECES[2])
            sp.dma_start(flat(m.WB)[:, cols], a["moe2"][:, cols]).then_inc(m.moe_in[2], 16)

        def fetch_moe3(sp, g):
            cols = slice(g * 2 * E * F // MOE_PIECES[3], (g + 1) * 2 * E * F // MOE_PIECES[3])
            sp.dma_start(flat(m.WA)[:, cols], a["moe3"][:, cols]).then_inc(m.moe_in[3], 16)

        ffn0(nc, m, tg(4), fetch_rest)
        attention(nc, m, 1, w["q1"], w["k1"], w["v1"], w["o1"], tg=tg(1), out_bias=rowv["bo1"],
                  fetch=fetch_moe2)
        batch_stats(nc, m, "x3_")
        router(nc, m, 1, m.router_w[:, 0, :])
        dispatch(nc, m, 1, tg(5))
        mlp(nc, m, 1, m.WA)
        combine(nc, m, 1)
        linear_attention(nc, m, w["g2"], w["v2"], w["o2"], w["q2"], w["k2"][:, 0:D // 2],
                         col["bg2"], rowv["bv2"], rowv["bk2"], col["bq2"], rowv["bo2"], fetch_moe3)
        router(nc, m, 2, m.router_w[:, 1, :])
        dispatch(nc, m, 2, tg(6))
        mlp(nc, m, 2, m.WB, b1=m.b1_all[:, 0, :], b2=m.b2[2])
        combine(nc, m, 2)
        attention(nc, m, 3, w["q3"], w["k3"], w["v3"], w["o3"], bq=col["bq3"], bk=col["bk3"], bv=col["bv3"],
                  tg=tg(3), out_bias=rowv["bo3"])
        batch_stats(nc, m, "x7_")
        selu_gate(nc, m, m.gate_w[:, 0, :], m.gate_w[:, 1, :], m.gate_b1, rowv["gate_bo"])
        dispatch(nc, m, 3, tg(7))
        mlp(nc, m, 3, m.WA, b1=m.b1_all[:, 1, :], b2=m.b2[3])
        combine(nc, m, 3, out)


def layouts(i):
    import numpy as np
    i = {k: np.asarray(v) for k, v in i.items()}
    f = np.float32
    x, ctx = i["x"].reshape(N, D), i["ctx_1024"].reshape(N, D)
    twice = lambda a: np.concatenate([a, a], axis=1)
    w = {"q0": i["L0_xattn_Wq"].T, "k0": i["L0_xattn_Wk"].T, "v0": i["L0_xattn_Wv"].T, "o0": i["L0_xattn_Wo"].T,
         "q1": i["L1_xattn_W_q"].T, "k1": i["L1_xattn_W_k"].T, "v1": i["L1_xattn_W_v"].T, "o1": i["L1_xattn_W_o"].T,
         "g2": i["L2_xattn_Wg"].T, "v2": i["L2_xattn_Wv"].T, "o2": i["L2_xattn_Wo"].T, "q2": twice(i["L2_xattn_Wq"].T), "k2": twice(i["L2_xattn_Wk"].T),
         "q3": i["L3_xattn_wq_w"].T, "k3": i["L3_xattn_wk_w"].T, "v3": i["L3_xattn_wv_w"].T, "o3": i["L3_xattn_wo_w"].T}
    cols = {"g_pre": i["L0_xattn_g_pre"], "b_pre": i["L0_xattn_b_pre"], "bq2": np.tile(i["L2_xattn_bq"], 2), "bg2": i["L2_xattn_bg"],
            "bq3": i["L3_xattn_wq_b"], "bk3": i["L3_xattn_wk_b"], "bv3": i["L3_xattn_wv_b"]}
    rows = {"g_ln": i["L0_xattn_g_ln"], "b_ln": i["L0_xattn_b_ln"], "bo1": i["L1_xattn_b_o"],
            "bv2": i["L2_xattn_bv"], "bk2": i["L2_xattn_bk"], "bo2": i["L2_xattn_bo"], "bo3": i["L3_xattn_wo_b"],
            "gate_bo": i["L3_ffn_gate_bo"]}
    one = lambda n: np.arange(n, dtype=f)[None, :].repeat(P, 0)
    consts = {"ident": np.eye(P, dtype=f), "head_mask": ((np.arange(P)[:, None] % 64) // DH == np.arange(HALF)).astype(f),
              "upper": np.triu(np.ones((P, P), f), 1), "expert": one(E), "tile128": one(T) * P, "block": one(NBX),
              "slot": one(P), "token": one(T) * P + np.arange(P, dtype=f)[:, None] + 1,
              "spare": 2 * N + one(NBX) * P + np.arange(P, dtype=f)[:, None],
              "keep": (np.arange(P) % T != 0).astype(f)[None, :].repeat(P, 0)}

    def moe(w1, w2):
        return np.concatenate([w1.transpose(1, 0, 2).reshape(P, E * F),
                               w2.reshape(E, FC, P, D).transpose(2, 0, 1, 3).reshape(P, E * F)], axis=1)

    mask = i["mask_BxSxS2_ik1"].reshape(T, 2, S, S).transpose(0, 2, 1, 3).reshape(T, 1, S, 2 * S).repeat(2, 1).reshape(N, 2 * S)
    return {"x": x, "ctx": ctx, "ctxT": ctx.T, "ctxT2": ctx.T.reshape(P, B, 1, S).repeat(2, 2).reshape(P, 2 * N), "wts": np.stack([w[n] for n in W_NAMES], 1).reshape(P, -1),
            "cols": np.stack([cols[n] for n in COL_NAMES], 1), "rows": np.concatenate([rows[n] for n in ROW_SIZES]),
            "consts": np.concatenate([consts[n] for n in C_SIZES], axis=1),
            "gates": np.concatenate([i["g_xattn"], i["g_ffn"]]),
            "mask": mask,
            "kernel0": i["L0_ffn_kernel"], "bias0": i["L0_ffn_bias"],
            "scales": np.concatenate([i["L0_ffn_input_scale"], i["L0_ffn_kernel_scale"]]),
            "kmask": i["mask_BxS2_bf1"].view(np.uint8).reshape(T, P).T,
            "router_w": np.concatenate([i["L1_ffn_router_w"].T, i["L2_ffn_w_router"]], axis=1),
            "gate_w": np.concatenate([i["L3_ffn_gate_wi"], i["L3_ffn_gate_wo"].reshape(FC, P, D).transpose(1, 0, 2).reshape(P, F)], axis=1),
            "moe2": moe(i["L2_ffn_w1"], i["L2_ffn_w2"]), "moe3": moe(i["L3_ffn_exp_wi"], i["L3_ffn_exp_wo"]),
            "b1": np.concatenate([i["L2_ffn_b1"].reshape(-1, P).T, i["L3_ffn_exp_bi"].reshape(-1, P).T], axis=1),
            "gate_b1": i["L3_ffn_gate_bi"].reshape(-1, P).T,
            "b2_2": i["L2_ffn_b2"].reshape(-1), "b2_3": i["L3_ffn_exp_bo"].reshape(-1),
            "moe1": moe(i["L1_ffn_expert_w1"].transpose(0, 2, 1), i["L1_ffn_expert_w2"].transpose(0, 2, 1)),
            }


def kernel(**inputs):
    import numpy as np
    import concourse.bacc as bacc
    from concourse.bass_utils import run_bass_kernel_spmd

    nc = bacc.Bacc("TRN2", target_bir_lowering=False, num_devices=1)
    arrays, aps = {}, {}
    for name, array in layouts(inputs).items():
        array = np.ascontiguousarray(array)
        arrays[f"in_{name}"] = array
        aps[name] = nc.dram_tensor(f"in_{name}", array.shape, mybir.dt.from_np(array.dtype), kind="ExternalInput").ap()
    out = nc.dram_tensor("out_x", (N, D), F32, kind="ExternalOutput").ap()
    program(nc, aps, out)
    result = run_bass_kernel_spmd(nc, [arrays], core_ids=[0])
    return result.results[0]["out_x"].reshape(B, S, D)
```
